# Optimizing a Trainium2 kernel written in Bass

```python
import numpy as np
import jax
import jax.numpy as jnp

def _softmax(x, axis=-1):
    return jax.nn.softmax(x, axis=axis)

def _gelu(x):
    return jax.nn.gelu(x, approximate=True)

def _silu(x):
    return jax.nn.silu(x)

def _sigmoid(x):
    return jax.nn.sigmoid(x)

def _layernorm(x, axis=-1, eps=1e-05):
    m = jnp.mean(x, axis=axis, keepdims=True)
    v = jnp.var(x, axis=axis, keepdims=True)
    return (x - m) / jnp.sqrt(v + eps)

def _scatter_add(tgt, idx, src, axis=0):
    return tgt.at[idx].add(src)

def _segment_sum(src, seg, n):
    return jax.ops.segment_sum(src, seg, n)
kernel_name = 'mk_decoder_preln_d2_seqx_r8_a7f19c'

def setup_inputs(seed: int=0):
    np.random.seed(seed)
    _w = jnp.asarray

    def _rec_inputs():
        import jax
        import jax.numpy as jnp
        _rk = jax.random.key(seed)
        x = -0.0005207 + 1.001 * jax.random.normal(jax.random.fold_in(_rk, 1), (16, 128, 128), jnp.float32)
        _lenS = 128 - jax.random.randint(jax.random.fold_in(_rk, 7), (16,), 0, max(1, 128 // 4) + 1, jnp.int32)
        _lenS2 = 77 - jax.random.randint(jax.random.fold_in(_rk, 8), (16,), 0, max(1, 77 // 4) + 1, jnp.int32)
        _ctx_1024P = jax.random.normal(jax.random.fold_in(_rk, 11), (16, 16, 128), jnp.float32)
        _ctx_1024c = jax.random.dirichlet(jax.random.fold_in(_rk, 511), 0.3 * jnp.ones((16,), jnp.float32), (16, 77))
        _ctx_1024t = jnp.einsum('bsk,bkd->bsd', _ctx_1024c, _ctx_1024P)
        _ctx_1024t = _ctx_1024t * jax.lax.rsqrt(jnp.mean(jnp.square(_ctx_1024t)) + 1e-12) * 0.953939
        ctx_1024 = 2.81802e-05 + 1.00001 * (_ctx_1024t + 0.3 * jax.random.normal(jax.random.fold_in(_rk, 611), (16, 77, 128), jnp.float32))
        _validS = jnp.arange(128)[None, :] < _lenS[:, None]
        _validS2 = jnp.arange(77)[None, :] < _lenS2[:, None]
        _causal = jnp.tril(jnp.ones((128, 128), dtype=bool))
        mask_BxS2_bf1 = jnp.ones((16, 77), dtype=bool)
        mask_BxS2_ik0 = jnp.where(jnp.broadcast_to(_validS2[:, :], (16, 77)), 0, 1).astype(jnp.int32)
        return (x, ctx_1024, mask_BxS2_bf1, mask_BxS2_ik0)
    x, ctx_1024, mask_BxS2_bf1, mask_BxS2_ik0 = _rec_inputs()

    def _L0_attn_setup():
        import jax, jax.numpy as jnp
        import numpy as np
        T, N, D, H = (128, 32, 128, 128)
        LR = 0.001

        def _recon(params, z):
            W1, b1, W2, b2 = params
            h = jax.nn.gelu(z @ W1.T + b1, approximate=False)
            return z + h @ W2.T + b2
        key = jax.random.key(seed)
        ks = jax.random.split(key, 6)
        sd = 1.0 / np.sqrt(D)
        sh = 1.0 / np.sqrt(H)
        s4 = 1.0 / np.sqrt(H // 4)
        return {'in_seq': jax.random.normal(ks[0], (T, N, D), jnp.float32), 't_k': jax.random.normal(ks[1], (H, D), jnp.float32) * sd, 't_v': jax.random.normal(ks[2], (H, D), jnp.float32) * sd, 't_q': jax.random.normal(ks[3], (H, D), jnp.float32) * sd, 'W1': jax.random.normal(ks[4], (H // 4, H), jnp.float32) * sh, 'b1': jnp.zeros((H // 4,), jnp.float32), 'W2': jax.random.normal(ks[5], (H, H // 4), jnp.float32) * s4, 'b2': jnp.zeros((H,), jnp.float32)}
    _L0_attn_all = _L0_attn_setup()
    _L0_attn_in = {k: v for k, v in _L0_attn_all.items() if k in ('t_k', 't_v', 't_q', 'W1', 'b1', 'W2', 'b2')}
    del _L0_attn_all

    def _L0_xattn_setup():
        import jax, jax.numpy as jnp
        import numpy as np
        EMB = 128
        HEADS = 16
        HEAD_DIM = EMB // HEADS
        EPS = 1e-05

        def _layer_norm(x, gamma, beta):
            m = jnp.mean(x, axis=-1, keepdims=True)
            v = jnp.mean(jnp.square(x - m), axis=-1, keepdims=True)
            return (x - m) / jnp.sqrt(v + EPS) * gamma + beta
        key = jax.random.key(seed)
        ks = jax.random.split(key, 8)
        B, Tx, Tc = (2, 128, 1024)
        scale = 1.0 / np.sqrt(EMB)
        return {'x': jax.random.normal(ks[0], (B, Tx, EMB), dtype=jnp.float32), 'context': jax.random.normal(ks[1], (B, Tc, EMB), dtype=jnp.float32), 'context_mask': jnp.ones((B, Tc), dtype=bool), 'Wq': jax.random.normal(ks[2], (EMB, EMB), dtype=jnp.float32) * scale, 'Wk': jax.random.normal(ks[3], (EMB, EMB), dtype=jnp.float32) * scale, 'Wv': jax.random.normal(ks[4], (EMB, EMB), dtype=jnp.float32) * scale, 'Wo': jax.random.normal(ks[5], (EMB, EMB), dtype=jnp.float32) * scale, 'bo': jnp.zeros((EMB,), dtype=jnp.float32), 'g1': jnp.ones((EMB,), dtype=jnp.float32), 'b1': jnp.zeros((EMB,), dtype=jnp.float32), 'g2': jnp.ones((EMB,), dtype=jnp.float32), 'b2': jnp.zeros((EMB,), dtype=jnp.float32)}
    _L0_xattn_all = _L0_xattn_setup()
    _L0_xattn_in = {k: v for k, v in _L0_xattn_all.items() if k in ('Wq', 'Wk', 'Wv', 'Wo', 'bo', 'g1', 'b1', 'g2', 'b2')}
    del _L0_xattn_all

    def _L0_ffn_setup():
        import jax, jax.numpy as jnp
        import numpy as np
        N_EMBD = 128
        NUM_EXPERTS = 8
        TOP_K = 2
        D_FF = 4 * N_EMBD
        B, S = (4, 256)
        key = jax.random.key(seed)
        ks = jax.random.split(key, 7)
        scale = lambda fan_in: 1.0 / np.sqrt(fan_in)
        x = jax.random.normal(ks[0], (B, S, N_EMBD), dtype=jnp.float32)
        W_router = jax.random.normal(ks[1], (N_EMBD, NUM_EXPERTS), dtype=jnp.float32) * scale(N_EMBD)
        b_router = jnp.zeros((NUM_EXPERTS,), dtype=jnp.float32)
        W1 = jax.random.normal(ks[2], (NUM_EXPERTS, N_EMBD, D_FF), dtype=jnp.float32) * scale(N_EMBD)
        b1 = jnp.zeros((NUM_EXPERTS, D_FF), dtype=jnp.float32)
        W2 = jax.random.normal(ks[3], (NUM_EXPERTS, D_FF, N_EMBD), dtype=jnp.float32) * scale(D_FF)
        b2 = jnpp = jnp.zeros((NUM_EXPERTS, N_EMBD), dtype=jnp.float32)
        return {'x': x, 'W_router': W_router, 'b_router': b_router, 'W1': W1, 'b1': b1, 'W2': W2, 'b2': b2}
    _L0_ffn_all = _L0_ffn_setup()
    _L0_ffn_in = {k: v for k, v in _L0_ffn_all.items() if k in ('W_router', 'b_router', 'W1', 'b1', 'W2', 'b2')}
    del _L0_ffn_all

    def _L1_attn_setup():
        import jax, jax.numpy as jnp
        import numpy as np
        EMBED = 128
        HEADS = 16
        GQA_GROUPS = 2
        KV_HEADS = HEADS // GQA_GROUPS
        HEAD_DIM = EMBED // HEADS
        ALIBI_ALPHA = 1.0
        START_I = 0
        N, S = (2, 256)

        def _alibi_bias(q_len, k_len):
            i = jnp.arange(1, HEADS + 1, dtype=jnp.float32)
            slopes = jnp.exp2(-ALIBI_ALPHA * (i + START_I)).reshape(1, HEADS, 1, 1)
            t_q = jnp.arange(q_len, dtype=jnp.float32)
            t_k = jnp.arange(k_len, dtype=jnp.float32)
            dist = jnp.abs(t_q[:, None] - t_k[None, :])
            return -dist[None, None] * slopes
        key = jax.random.key(seed)
        ks = jax.random.split(key, 6)
        x = jax.random.normal(ks[0], (N, S, EMBED), dtype=jnp.float32)
        sc = 1.0 / np.sqrt(EMBED)
        Wq = jax.random.normal(ks[1], (HEADS * HEAD_DIM, EMBED), dtype=jnp.float32) * sc
        Wk = jax.random.normal(ks[2], (KV_HEADS * HEAD_DIM, EMBED), dtype=jnp.float32) * sc
        Wv = jax.random.normal(ks[3], (KV_HEADS * HEAD_DIM, EMBED), dtype=jnp.float32) * sc
        Wo = jax.random.normal(ks[4], (EMBED, HEADS * HEAD_DIM), dtype=jnp.float32) * sc
        bo = jax.random.normal(ks[5], (EMBED,), dtype=jnp.float32) * 0.01
        return {'x': x, 'Wq': Wq, 'Wk': Wk, 'Wv': Wv, 'Wo': Wo, 'bo': bo}
    _L1_attn_all = _L1_attn_setup()
    _L1_attn_in = {k: v for k, v in _L1_attn_all.items() if k in ('Wq', 'Wk', 'Wv', 'Wo', 'bo')}
    del _L1_attn_all

    def _L1_xattn_setup():
        import jax, jax.numpy as jnp
        import numpy as np
        B, SQ, SKV, D, H = (2, 256, 256, 128, 16)
        W = D // H

        def _heads(x):
            b, s, _ = x.shape
            return x.reshape(b, s, H, W).transpose(0, 2, 1, 3)
        key = jax.random.key(seed)
        ks = jax.random.split(key, 10)
        s = 1.0 / np.sqrt(D)
        return {'x_q': jax.random.normal(ks[0], (B, SQ, D), jnp.float32), 'x_k': jax.random.normal(ks[1], (B, SKV, D), jnp.float32), 'x_v': jax.random.normal(ks[2], (B, SKV, D), jnp.float32), 'mask': jax.random.randint(ks[3], (B, SKV), 0, 2, jnp.int32), 'Wq': jax.random.normal(ks[4], (D, D), jnp.float32) * s, 'bq': jnp.zeros((D,), jnp.float32), 'Wk': jax.random.normal(ks[5], (D, D), jnp.float32) * s, 'bk': jnp.zeros((D,), jnp.float32), 'Wv': jax.random.normal(ks[6], (D, D), jnp.float32) * s, 'bv': jnp.zeros((D,), jnp.float32)}
    _L1_xattn_all = _L1_xattn_setup()
    _L1_xattn_in = {k: v for k, v in _L1_xattn_all.items() if k in ('Wq', 'bq', 'Wk', 'bk', 'Wv', 'bv')}
    del _L1_xattn_all

    def _L1_ffn_setup():
        import jax, jax.numpy as jnp
        import numpy as np
        D_MODEL = 128
        NUM_EXPERTS = 8
        HIDDEN = 512
        TOP_K = 2
        key = jax.random.key(seed)
        ks = jax.random.split(key, 6)
        x = jax.random.normal(ks[0], (2, 128, D_MODEL), dtype=jnp.float32)
        gate_w = jax.random.normal(ks[1], (NUM_EXPERTS, D_MODEL), dtype=jnp.float32) * (1.0 / np.sqrt(D_MODEL))
        w1 = jax.random.normal(ks[2], (NUM_EXPERTS, HIDDEN, D_MODEL), dtype=jnp.float32) * (1.0 / np.sqrt(D_MODEL))
        b1 = jax.random.normal(ks[3], (NUM_EXPERTS, HIDDEN), dtype=jnp.float32) * 0.01
        w2 = jax.random.normal(ks[4], (NUM_EXPERTS, D_MODEL, HIDDEN), dtype=jnp.float32) * (1.0 / np.sqrt(HIDDEN))
        b2 = jax.random.normal(ks[5], (NUM_EXPERTS, D_MODEL), dtype=jnp.float32) * 0.01
        return {'x': x, 'gate_w': gate_w, 'w1': w1, 'b1': b1, 'w2': w2, 'b2': b2}
    _L1_ffn_all = _L1_ffn_setup()
    _L1_ffn_in = {k: v for k, v in _L1_ffn_all.items() if k in ('gate_w', 'w1', 'b1', 'w2', 'b2')}
    del _L1_ffn_all
    return {'x': x, 'ctx_1024': ctx_1024, 'mask_BxS2_bf1': mask_BxS2_bf1, 'mask_BxS2_ik0': mask_BxS2_ik0, 'L0_attn_t_k': _L0_attn_in['t_k'], 'L0_attn_t_v': _L0_attn_in['t_v'], 'L0_attn_t_q': _L0_attn_in['t_q'], 'L0_attn_W1': _L0_attn_in['W1'], 'L0_attn_b1': _L0_attn_in['b1'], 'L0_attn_W2': _L0_attn_in['W2'], 'L0_attn_b2': _L0_attn_in['b2'], 'L0_xattn_Wq': _L0_xattn_in['Wq'], 'L0_xattn_Wk': _L0_xattn_in['Wk'], 'L0_xattn_Wv': _L0_xattn_in['Wv'], 'L0_xattn_Wo': _L0_xattn_in['Wo'], 'L0_xattn_bo': _L0_xattn_in['bo'], 'L0_xattn_g1': _L0_xattn_in['g1'], 'L0_xattn_b1': _L0_xattn_in['b1'], 'L0_xattn_g2': _L0_xattn_in['g2'], 'L0_xattn_b2': _L0_xattn_in['b2'], 'L0_ffn_W_router': _L0_ffn_in['W_router'], 'L0_ffn_b_router': _L0_ffn_in['b_router'], 'L0_ffn_W1': _L0_ffn_in['W1'], 'L0_ffn_b1': _L0_ffn_in['b1'], 'L0_ffn_W2': _L0_ffn_in['W2'], 'L0_ffn_b2': _L0_ffn_in['b2'], 'L1_attn_Wq': _L1_attn_in['Wq'], 'L1_attn_Wk': _L1_attn_in['Wk'], 'L1_attn_Wv': _L1_attn_in['Wv'], 'L1_attn_Wo': _L1_attn_in['Wo'], 'L1_attn_bo': _L1_attn_in['bo'], 'L1_xattn_Wq': _L1_xattn_in['Wq'], 'L1_xattn_bq': _L1_xattn_in['bq'], 'L1_xattn_Wk': _L1_xattn_in['Wk'], 'L1_xattn_bk': _L1_xattn_in['bk'], 'L1_xattn_Wv': _L1_xattn_in['Wv'], 'L1_xattn_bv': _L1_xattn_in['bv'], 'L1_ffn_gate_w': _L1_ffn_in['gate_w'], 'L1_ffn_w1': _L1_ffn_in['w1'], 'L1_ffn_b1': _L1_ffn_in['b1'], 'L1_ffn_w2': _L1_ffn_in['w2'], 'L1_ffn_b2': _L1_ffn_in['b2']}

def reference(x, ctx_1024, mask_BxS2_bf1, mask_BxS2_ik0, L0_attn_t_k, L0_attn_t_v, L0_attn_t_q, L0_attn_W1, L0_attn_b1, L0_attn_W2, L0_attn_b2, L0_xattn_Wq, L0_xattn_Wk, L0_xattn_Wv, L0_xattn_Wo, L0_xattn_bo, L0_xattn_g1, L0_xattn_b1, L0_xattn_g2, L0_xattn_b2, L0_ffn_W_router, L0_ffn_b_router, L0_ffn_W1, L0_ffn_b1, L0_ffn_W2, L0_ffn_b2, L1_attn_Wq, L1_attn_Wk, L1_attn_Wv, L1_attn_Wo, L1_attn_bo, L1_xattn_Wq, L1_xattn_bq, L1_xattn_Wk, L1_xattn_bk, L1_xattn_Wv, L1_xattn_bv, L1_ffn_gate_w, L1_ffn_w1, L1_ffn_b1, L1_ffn_w2, L1_ffn_b2):
    import jax
    import jax.numpy as jnp

    def _L0_attn_ref(in_seq, t_k, t_v, t_q, W1, b1, W2, b2):
        import jax, jax.numpy as jnp
        import numpy as np
        T, N, D, H = (128, 32, 128, 128)
        LR = 0.001

        def _recon(params, z):
            W1, b1, W2, b2 = params
            h = jax.nn.gelu(z @ W1.T + b1, approximate=False)
            return z + h @ W2.T + b2

        def loss_fn(params, z, y):
            return jnp.mean((_recon(params, z) - y) ** 2)

        def step(params, x):
            z = x @ t_k.T
            y = x @ t_v.T
            grads = jax.grad(loss_fn)(params, z, y)
            new_params = jax.tree_util.tree_map(lambda p, g: jax.lax.stop_gradient(p - LR * g), params, grads)
            out = _recon(new_params, x @ t_q.T)
            return (new_params, out)
        _, outs = jax.lax.scan(step, (W1, b1, W2, b2), in_seq)
        return outs

    def _L0_xattn_ref(x, context, context_mask, Wq, Wk, Wv, Wo, bo, g1, b1, g2, b2):
        import jax, jax.numpy as jnp
        import numpy as np
        EMB = 128
        HEADS = 16
        HEAD_DIM = EMB // HEADS
        EPS = 1e-05

        def _layer_norm(x, gamma, beta):
            m = jnp.mean(x, axis=-1, keepdims=True)
            v = jnp.mean(jnp.square(x - m), axis=-1, keepdims=True)
            return (x - m) / jnp.sqrt(v + EPS) * gamma + beta
        B, Tx, C = x.shape
        Tc = context.shape[1]
        xn = _layer_norm(x, g1, b1)
        cn = _layer_norm(context, g2, b2)
        q = (xn @ Wq.T).reshape(B, Tx, HEADS, HEAD_DIM)
        k = (cn @ Wk.T).reshape(B, Tc, HEADS, HEAD_DIM)
        v = (cn @ Wv.T).reshape(B, Tc, HEADS, HEAD_DIM)
        scores = jnp.einsum('bqhs,bkhs->bhqk', q, k) / np.sqrt(HEAD_DIM)
        scores = jnp.where(context_mask[:, None, None, :], scores, -jnp.inf)
        attn = jax.nn.softmax(scores, axis=-1)
        out = jnp.einsum('bhqk,bkhs->bqhs', attn, v).reshape(B, Tx, C)
        return out @ Wo.T + bo

    def _L0_ffn_ref(x, W_router, b_router, W1, b1, W2, b2):
        import jax, jax.numpy as jnp
        import numpy as np
        N_EMBD = 128
        NUM_EXPERTS = 8
        TOP_K = 2
        D_FF = 4 * N_EMBD
        B, S = (4, 256)
        Bv, Sv, D = x.shape
        flat_x = x.reshape(-1, D)
        T = flat_x.shape[0]
        logits = flat_x @ W_router + b_router
        top_vals, top_idx = jax.lax.top_k(logits, TOP_K)
        neg_inf = jnp.full_like(logits, -jnp.inf)
        sparse_logits = neg_inf.at[jnp.arange(T)[:, None], top_idx].set(top_vals)
        router_weights = jax.nn.softmax(sparse_logits, axis=-1)
        final_output = jnp.zeros_like(flat_x)
        for e in range(NUM_EXPERTS):
            expert_mask = jnp.any(top_idx == e, axis=-1)
            h = jax.nn.relu(flat_x @ W1[e] + b1[e])
            y = h @ W2[e] + b2[e]
            w = router_weights[:, e] * expert_mask.astype(x.dtype)
            final_output = final_output + y * w[:, None]
        return final_output.reshape(Bv, Sv, D)

    def _L1_attn_ref(x, Wq, Wk, Wv, Wo, bo):
        import jax, jax.numpy as jnp
        import numpy as np
        EMBED = 128
        HEADS = 16
        GQA_GROUPS = 2
        KV_HEADS = HEADS // GQA_GROUPS
        HEAD_DIM = EMBED // HEADS
        ALIBI_ALPHA = 1.0
        START_I = 0
        N, S = (2, 256)

        def _alibi_bias(q_len, k_len):
            i = jnp.arange(1, HEADS + 1, dtype=jnp.float32)
            slopes = jnp.exp2(-ALIBI_ALPHA * (i + START_I)).reshape(1, HEADS, 1, 1)
            t_q = jnp.arange(q_len, dtype=jnp.float32)
            t_k = jnp.arange(k_len, dtype=jnp.float32)
            dist = jnp.abs(t_q[:, None] - t_k[None, :])
            return -dist[None, None] * slopes
        n, s, _ = x.shape
        q = (x @ Wq.T).reshape(n, s, HEADS, HEAD_DIM)
        k = (x @ Wk.T).reshape(n, s, KV_HEADS, HEAD_DIM)
        v = (x @ Wv.T).reshape(n, s, KV_HEADS, HEAD_DIM)
        k = jnp.repeat(k, GQA_GROUPS, axis=2)
        v = jnp.repeat(v, GQA_GROUPS, axis=2)
        energy = jnp.einsum('nqhd,nkhd->nhqk', q, k)
        energy = energy + _alibi_bias(s, s)
        attn = jax.nn.softmax(energy / jnp.sqrt(jnp.float32(HEAD_DIM)), axis=-1)
        out = jnp.einsum('nhqk,nkhd->nqhd', attn, v).reshape(n, s, HEADS * HEAD_DIM)
        return out @ Wo.T + bo

    def _L1_xattn_ref(x_q, x_k, x_v, mask, Wq, bq, Wk, bk, Wv, bv):
        import jax, jax.numpy as jnp
        import numpy as np
        B, SQ, SKV, D, H = (2, 256, 256, 128, 16)
        W = D // H

        def _heads(x):
            b, s, _ = x.shape
            return x.reshape(b, s, H, W).transpose(0, 2, 1, 3)
        q = _heads(x_q @ Wq.T + bq)
        k = _heads(x_k @ Wk.T + bk)
        v = _heads(x_v @ Wv.T + bv)
        scores = jnp.einsum('bhqw,bhkw->bhqk', q, k) / np.sqrt(W).astype(np.float32)
        m = mask[:, None, None, :].astype(scores.dtype)
        scores = scores - 10000.0 * (1.0 - m)
        p = jax.nn.softmax(scores, axis=-1)
        h = jnp.einsum('bhqk,bhkw->bhqw', p, v)
        return h.transpose(0, 2, 1, 3).reshape(x_q.shape[0], x_q.shape[1], D)

    def _L1_ffn_ref(x, gate_w, w1, b1, w2, b2):
        import jax, jax.numpy as jnp
        import numpy as np
        D_MODEL = 128
        NUM_EXPERTS = 8
        HIDDEN = 512
        TOP_K = 2
        B, S, D = x.shape
        xf = x.reshape(-1, D)
        T = xf.shape[0]
        gate_logits = xf @ gate_w.T
        gate_probs = jax.nn.softmax(gate_logits, axis=-1)
        topk_scores, topk_idx = jax.lax.top_k(gate_probs, TOP_K)
        topk_scores = topk_scores / jnp.sum(topk_scores, axis=-1, keepdims=True)
        combine = jnp.zeros((T, NUM_EXPERTS), dtype=x.dtype)
        combine = combine.at[jnp.arange(T)[:, None], topk_idx].set(topk_scores)
        h = jax.nn.relu(jnp.einsum('td,ehd->teh', xf, w1) + b1)
        expert_out = jnp.einsum('teh,edh->ted', h, w2) + b2
        out = jnp.einsum('ted,te->td', expert_out, combine)
        return out.reshape(B, S, D)
    x = x + _L0_attn_ref(_layernorm(x, axis=-1), L0_attn_t_k, L0_attn_t_v, L0_attn_t_q, L0_attn_W1, L0_attn_b1, L0_attn_W2, L0_attn_b2)
    x = x + _L0_xattn_ref(_layernorm(x, axis=-1), ctx_1024, mask_BxS2_bf1, L0_xattn_Wq, L0_xattn_Wk, L0_xattn_Wv, L0_xattn_Wo, L0_xattn_bo, L0_xattn_g1, L0_xattn_b1, L0_xattn_g2, L0_xattn_b2)
    x = x + _L0_ffn_ref(_layernorm(x, axis=-1), L0_ffn_W_router, L0_ffn_b_router, L0_ffn_W1, L0_ffn_b1, L0_ffn_W2, L0_ffn_b2)
    x = x + _L1_attn_ref(_layernorm(x, axis=-1), L1_attn_Wq, L1_attn_Wk, L1_attn_Wv, L1_attn_Wo, L1_attn_bo)
    x = x + _L1_xattn_ref(_layernorm(x, axis=-1), ctx_1024, ctx_1024, mask_BxS2_ik0, L1_xattn_Wq, L1_xattn_bq, L1_xattn_Wk, L1_xattn_bk, L1_xattn_Wv, L1_xattn_bv)
    x = x + _L1_ffn_ref(_layernorm(x, axis=-1), L1_ffn_gate_w, L1_ffn_w1, L1_ffn_b1, L1_ffn_w2, L1_ffn_b2)
    return x

_drawn_inputs = setup_inputs


def setup_inputs(seed=0):
    import zlib

    import numpy as np

    out = dict(_drawn_inputs(seed))
    spreads = {'L0_attn_b1': (0.0, 0.1),
     'L0_attn_b2': (0.0, 0.1),
     'L0_xattn_bo': (0.0, 0.1),
     'L0_xattn_g1': (1.0, 0.2),
     'L0_xattn_b1': (0.0, 0.1),
     'L0_xattn_g2': (1.0, 0.2),
     'L0_xattn_b2': (0.0, 0.1),
     'L0_ffn_b_router': (0.0, 0.1),
     'L0_ffn_b1': (0.0, 0.1),
     'L0_ffn_b2': (0.0, 0.1),
     'L1_xattn_bq': (0.0, 0.303),
     'L1_xattn_bk': (0.0, 2.0),
     'L1_xattn_bv': (0.0, 0.1)}
    factors = {'L0_attn_t_k': 8.0,
     'L0_attn_t_v': 24.917,
     'L1_attn_bo': 4.558,
     'L1_ffn_b1': 21.859,
     'L1_ffn_b2': 8.0}
    for name, (base, spread) in spreads.items():
        noise = np.random.default_rng([zlib.crc32(name.encode()), seed]).standard_normal(out[name].shape)
        drawn = base * np.exp(spread * noise) if base else spread * noise
        out[name] = jnp.asarray(drawn.astype(out[name].dtype))
    for name, factor in factors.items():
        out[name] = (out[name] * factor).astype(out[name].dtype)
    return out
```

```python
import concourse.bass as bass
from concourse import mybir
from contextlib import ExitStack

F32 = mybir.dt.float32
BF16 = mybir.dt.bfloat16
I32 = mybir.dt.int32
U8 = mybir.dt.uint8
ALU = mybir.AluOpType
ACT = mybir.ActivationFunctionType
AX = mybir.AxisListType

NB = 16
P = 128
TC = 77
NH = 16
DH = P // NH
NG = 4
HG = NH // NG
R = P // NG
HID = 32
NE = 8
FF = 512
FC = FF // P
EPS = 1e-5
LR = 0.001
GRAD = LR * 2.0 / (P * P)
SQRT_DH = float(DH) ** 0.5
DENSITY = 0.3989422804014327

SQUARES = ["ident", "tk", "tv", "tq",
           "x0_q", "x0_k", "x0_v", "x0_o", "s1_q", "s1_o", "x1_q", "x1_k", "x1_v"]
HALVES = ["s1_k", "s1_v"]
COLS = ["x0_g1", "x0_b1", "x0_g2", "x0_b2", "x1_bq", "x1_bk"]
ROWS = ["x0_o", "s1_o", "x1_v", "s_b2"]


def wait(eng, sem, value):
    if isinstance(value, int) and value <= 0:
        return
    eng.wait_ge(sem, value)


def pass_waits(eng, m):
    eng.sem_inc(m["passed"], 1)


class Steps:

    def __init__(self, eng, sem, b, per):
        self.eng, self.sem, self.base, self.per, self.n = eng, sem, b * per, per, 0

    def done(self, ins):
        self.n += 1
        assert self.n <= self.per
        ins.then_inc(self.sem, 1)
        self.eng.wait_ge(self.sem, self.base + self.n)

    def end(self):
        assert self.n == self.per, (self.n, self.per)


def staggered(eng, stages, first=4):
    def peeled(k):
        for lag, stage in stages:
            if 0 <= k - lag < NB:
                stage(k - lag, (k - lag) % 2)
    for k in range(first):
        peeled(k)
    with eng.Fori(0, (NB - first) // 2) as i:
        for u in range(2):
            for lag, stage in stages:
                stage(i * 2 + (first + u - lag), (first + u - lag) % 2)
    for k in range(NB, NB + max(lag for lag, _ in stages)):
        peeled(k)


def build(nc, t, out):
    ctx = ExitStack()
    with ctx:
        def sb(name, shape, dt=F32):
            return ctx.enter_context(nc.sbuf_tensor(name, shape, dt))

        def sem(name):
            return ctx.enter_context(nc.semaphore(name))

        x = sb("x", [P, NB, P])
        c = sb("c", [TC, NB, P])
        sq = sb("sq", [P, len(SQUARES), P])
        half = sb("half", [P, len(HALVES), NH, DH])
        cols = sb("cols", [P, len(COLS)])
        rows = sb("rows", [1, len(ROWS), P])
        ones = sb("ones", [P, P])
        ones_bf = sb("ones_bf", [P, P], BF16)
        ident_bf = sb("ident_bf", [P, P], BF16)
        half_power = sb("half_power", [P, 2])
        headsel = sb("headsel", [P, 2, HG])
        alibi = sb("alibi", [P, NH, P], BF16)
        m = dict(x=x, c=c, sq=sq, half=half, cols=cols, rows=rows, ones=ones, ones_bf=ones_bf,
                 ident_bf=ident_bf, half_power=half_power, headsel=headsel, alibi=alibi)
        m["eye"] = sq[:, SQUARES.index("ident"), :]
        m["w"] = lambda name: sq[:, SQUARES.index(name), :]
        m["row"] = lambda name: rows[0:1, ROWS.index(name), :]
        m["col"] = lambda name: cols[:, COLS.index(name):COLS.index(name) + 1]
        for q in (0, 1):
            m[f"w1_{q}"] = sb(f"w1_{q}", [P, NE, FF])
            m[f"w2_{q}"] = sb(f"w2_{q}", [P, NE, FC, P])
            m[f"b1_{q}"] = sb(f"b1_{q}", [P, NE, FC])
            m[f"b2_{q}"] = sb(f"b2_{q}", [NE, P])
            m[f"wr_{q}"] = sb(f"wr_{q}", [P, NE])
        m["br_0"] = sb("br_0", [1, NE])
        m["scan_w1T"] = sb("scan_w1T", [P, HID])
        m["scan_w2T"] = sb("scan_w2T", [HID + 1, P])
        m["scan_w2"] = sb("scan_w2", [P, HID])
        m["scan_b1c"] = sb("scan_b1c", [HID, 1])
        m["scan_b1r"] = sb("scan_b1r", [1, HID])
        m["mask_0"] = sb("mask_0", [P, NB, TC], BF16)
        m["mask_1"] = sb("mask_1", [P, NB, TC], BF16)
        m["mask_u8"] = sb("mask_u8", [P, NB, TC], U8)
        m["mask_i32"] = sb("mask_i32", [P, NB, TC], I32)
        m["mask_f"] = sb("mask_f", [P, NB, TC])
        m["mask_hi"] = sb("mask_hi", [P, NB, TC], BF16)
        m["mask_part"] = sb("mask_part", [P, NB, TC], BF16)
        m["mask_sel"] = sb("mask_sel", [P, 3])
        m["countdown"] = sb("countdown", [P, NE])

        loaded_scan = sem("loaded_scan")
        loaded_mask = sem("loaded_mask")
        loaded_rest = sem("loaded_rest")
        stored = sem("stored")
        m.update(loaded_scan=loaded_scan, loaded_mask=loaded_mask, loaded_rest=loaded_rest,
                 stored=stored)
        m["passed"] = sem("passed")
        load_and_scan(nc, t, m)
        attention(nc, m, "x0", TC, weights="x0", context=True, mask="mask_0", mask_rows=1,
                  norm_context=True, out_proj=True, exp_scale=1.0, sel=1)
        experts(nc, m, 0, None)
        attention(nc, m, "s1", P, weights="s1", context=False, mask=None, mask_rows=0,
                  norm_context=False, out_proj=True, exp_scale=1.0 / SQRT_DH, sel=0)
        attention(nc, m, "x1", TC, weights="x1", context=True, mask="mask_1", mask_rows=3,
                  norm_context=False, out_proj=False, exp_scale=1.0, sel=1)
        experts(nc, m, 1, out)


def load_and_scan(nc, t, m):
    x, c = m["x"], m["c"]
    eye, ones = m["eye"], m["ones"]
    ctx = ExitStack()
    with ctx:
        def sb(name, shape, dt=F32):
            return ctx.enter_context(nc.sbuf_tensor(name, shape, dt))

        def ps(name):
            return ctx.enter_context(nc.psum_tensor(name, [P, 512], F32))

        def sem(name):
            return ctx.enter_context(nc.semaphore(name))

        w1T, w2T, w2, b1c, b1r = (m[k] for k in ("scan_w1T", "scan_w2T", "scan_w2", "scan_b1c", "scan_b1r"))
        tkv = sb("tkv", [P, P])
        stats = sb("stats", [P, 2, 6])
        mv = sb("mv", [P, 2, 2])
        var = sb("var", [P, 2, 1])
        rstd = sb("rstd", [P, 2, 1])
        xn = sb("xn", [P, 2, P])
        xnT = sb("xnT", [P, 2, P])
        z = sb("z", [P, 2, P])
        zq = sb("zq", [P, 2, 2 * P])
        hT = sb("hT", [HID + 1, P])
        hqT = sb("hqT", [HID + 1, P])
        h = sb("h", [P, HID + 1])
        zero = sb("zero", [P, HID])
        a = sb("a", [P, HID])
        a2 = sb("a2", [P, HID])
        th = sb("th", [P, HID])
        dn = sb("dn", [P, 5, HID])
        slope = sb("slope", [P, HID])
        eT = sb("eT", [P, P])
        e = sb("e", [P, P])
        da = sb("da", [P, HID])

        p_pre, p_aT, p_a, p_eT, p_e, p_dh, p_grad, p_out = (
            ps(f"p_{n}") for n in ("pre", "aT", "a", "eT", "e", "dh", "grad", "out"))
        g_w1T, g_w2T, g_w2 = p_grad[:, 0:HID], p_grad[0:HID + 1, 128:256], p_grad[:, 256:256 + HID]
        g_b1c, g_b1r = p_grad[0:HID, 300:301], p_grad[0:1, 320:320 + HID]

        set_pool, set_dve = sem("scan_set_pool"), sem("scan_set_dve")
        masks = sem("scan_masks")
        pre_dve, pre_pool = sem("pre_dve"), sem("pre_pool")
        normed, turned, turned_sb = sem("s_normed"), sem("s_turned"), sem("s_turned_sb")
        projected, projected_sb = sem("s_projected"), sem("s_projected_sb")
        acts_ready, a_ready, hT_ready, h_ready = (sem(n) for n in ("s_acts", "s_a", "s_hT", "s_h"))
        a_safe, th_ready, slope_dve = sem("s_a_safe"), sem("s_th"), sem("s_slope")
        th_mid = sem("s_th_mid")
        eT_ready, eT_sb, e_ready, e_sb = (sem(n) for n in ("s_eT", "s_eT_sb", "s_e", "s_e_sb"))
        dh_ready, da_ready, g2_ready, g1_ready = (sem(n) for n in ("s_dh", "s_da", "s_g2", "s_g1"))
        w1_new, w2_new = sem("s_w1_new"), sem("s_w2_new")
        aq_ready, hqT_ready, out_ready, added = (sem(n) for n in ("s_aq", "s_hqT", "s_out", "s_added"))

        SCAN_LOADS = 10
        with nc.Block() as block:
            @block.sync
            def _(sp):
                def load(dst, src, s):
                    sp.dma_start(dst, src).then_inc(s, 16)
                ls = m["loaded_scan"]
                load(x[:, :, :], t["x"].rearrange("b p d -> p b d"), ls)
                load(m["sq"][:, :, :], t["squares"].rearrange("n p d -> p n d"), ls)
                load(w1T[:, :], t["scan_w1T"], ls)
                load(w2T[0:HID, :], t["scan_w2T"], ls)
                load(w2T[HID:HID + 1, :], t["rows"][ROWS.index("s_b2"):ROWS.index("s_b2") + 1, :], ls)
                load(w2[:, :], t["scan_w2"], ls)
                load(b1c[:, :], t["scan_b1"].rearrange("(p a) -> p a", a=1), ls)
                load(b1r[:, :], t["scan_b1"].rearrange("(a p) -> a p", a=1), ls)
                load(m["mask_sel"][:, :], t["mask_select"], ls)
                load(m["headsel"][:, :, :], t["head_select"], ls)
                lm = m["loaded_mask"]
                for q in range(2):
                    load(m[("mask_u8", "mask_i32")[q]][:, :, :], t[f"mask_{q}"].rearrange("(a b) s -> a b s", a=1).to_broadcast([P, NB, TC]), lm)
                lr = m["loaded_rest"]
                n = 0
                rest = [(c[:, :, :], t["ctx"].rearrange("b p d -> p b d")),
                        (m["cols"][:, :], t["cols"]),
                        (m["rows"][:, :, :], t["rows"].rearrange("(a n) d -> a n d", a=1)),
                        (m["alibi"][:, :, :], t["alibi"]),
                        (m["countdown"][:, :], t["countdown"])]
                for j in range(len(HALVES)):
                    for r in range(2):
                        rest.append((m["half"][:, j, :, :].rearrange("p (k r) d -> p k r d", r=2)[:, :, r, :],
                                     t["halves"][j].rearrange("p (k d) -> p k d", d=DH)))
                for q in range(2):
                    rest += [(m[f"w1_{q}"][:, :, :], t[f"w1_{q}"].rearrange("e p f -> p e f")),
                             (m[f"w2_{q}"][:, :, :, :], t[f"w2_{q}"].rearrange("e (k p) d -> p e k d", p=P)),
                             (m[f"b1_{q}"][:, :, :], t[f"b1_{q}"].rearrange("e (k p) -> p e k", p=P)),
                             (m[f"b2_{q}"][:, :], t[f"b2_{q}"]),
                             (m[f"wr_{q}"][:, :], t[f"wr_{q}"])]
                rest.append((m["br_0"][:, :], t["br_0"].rearrange("(a n) -> a n", a=1)))
                for dst, src in rest:
                    with nc.allow_non_contiguous_dma(reason="one-time weight load"):
                        load(dst, src, lr)
                m["n_rest"] = len(rest)

            @block.gpsimd
            def _(pool):
                n = 0
                for tile, value in ((m["half_power"][:, :], -0.5), (ones[:, :], 1.0), (m["ones_bf"][:, :], 1.0),
                                    (hT[HID:HID + 1, :], 1.0), (hqT[HID:HID + 1, :], 1.0), (h[:, HID:HID + 1], 1.0)):
                    nc.gpsimd.memset(tile, value).then_inc(set_pool, 1)
                    n += 1
                    pool.wait_ge(set_pool, n)

                def rstd_of(b, p):
                    pool.wait_ge(pre_dve, b * 3 + 2)
                    pass_waits(pool, m)
                    nc.gpsimd.tensor_scalar(var[:, p, :], mv[:, p, 1:2], EPS, None, ALU.add).then_inc(pre_pool, 1)
                    pool.wait_ge(pre_pool, b * 2 + 1)
                    nc.gpsimd.tensor_tensor(rstd[:, p, :], var[:, p, :], m["half_power"][:, 0:1], ALU.pow).then_inc(pre_pool, 1)

                rstd_of(0, 0)
                rstd_of(1, 1)
                pool.wait_ge(m["loaded_mask"], 32)
                nc.gpsimd.tensor_scalar(m["mask_f"][:, :, :], m["mask_u8"][:, :, :], -1.0, 3e38, ALU.add, ALU.mult).then_inc(masks, 1)
                pool.wait_ge(masks, 1)
                nc.gpsimd.tensor_scalar(m["mask_0"][:, :, :], m["mask_f"][:, :, :], 3e38, None, ALU.mult).then_inc(masks, 1)
                with pool.Fori(0, (NB - 2) // 2) as i:
                    for u in range(2):
                        rstd_of(i * 2 + (u + 2), u)

            def scan(eng, pre, main, out_, last=None):
                pre(0, 0)
                main(0, 0, False)
                pre(1, 1)
                with eng.Fori(0, (NB - 2) // 2) as i:
                    for u in (1, 0):
                        s = i * 2 + (2 - u)
                        main(s, u, True)
                        pre(s + 1, 1 - u)
                main(NB - 1, 1, True)
                out_(NB - 1, 1)

            @block.vector
            def _(dve):
                dve.wait_ge(m["loaded_scan"], 16 * SCAN_LOADS)
                nc.vector.tensor_tensor(tkv[:, :], m["w"]("tk"), m["w"]("tv"), ALU.subtract).then_inc(set_dve, 1)
                nc.vector.tensor_copy(m["ident_bf"][:, :], eye).then_inc(set_dve, 1)

                def pre(b, p):
                    s = Steps(dve, pre_dve, b, 3)
                    s.done(nc.vector.bn_stats(stats[:, p, :], x[:, bass.ds(b, 1), :].rearrange("p a d -> p (a d)")))
                    pass_waits(dve, m)
                    s.done(nc.vector.bn_aggr(mv[:, p, :], stats[:, p, :]))
                    dve.wait_ge(pre_pool, b * 2 + 2)
                    if not (isinstance(b, int) and b < 2):
                        dve.wait_ge(turned, b - 1)
                    s.done(nc.vector.tensor_scalar(xn[:, p, :], x[:, bass.ds(b, 1), :].rearrange("p a d -> p (a d)"),
                                                   mv[:, p, 0:1], rstd[:, p, 0:1], ALU.subtract, ALU.mult))
                    s.end()

                def main(b, p, has_out):
                    s = Steps(dve, slope_dve, b, 9)
                    dve.wait_ge(a_ready, b + 1)
                    s.done(nc.vector.tensor_scalar(dn[:, 0, :], p_a[:, 0:HID], 0.0, 1e-12, ALU.is_equal, ALU.mult))
                    nc.vector.tensor_tensor(a[:, :], p_a[:, 0:HID], dn[:, 0, :], ALU.add).then_inc(a_safe, 1)
                    dve.wait_ge(a_safe, b + 1)
                    s.done(nc.vector.reciprocal(dn[:, 1, :], a[:, :]))
                    dve.wait_ge(eT_ready, b + 1)
                    wait(dve, dh_ready, b)
                    nc.vector.tensor_copy(eT[:, :], p_eT[:, 0:P]).then_inc(eT_sb, 1)
                    dve.wait_ge(th_ready, b + 1)
                    s.done(nc.vector.tensor_scalar(dn[:, 2, :], th[:, :], 1.0, None, ALU.add))
                    s.done(nc.vector.reciprocal(dn[:, 3, :], dn[:, 2, :]))
                    s.done(nc.vector.tensor_scalar(dn[:, 4, :], th[:, :], -DENSITY, DENSITY, ALU.mult, ALU.add))
                    s.done(nc.vector.tensor_tensor(dn[:, 4, :], dn[:, 4, :], dn[:, 3, :], ALU.mult))
                    s.done(nc.vector.tensor_tensor(dn[:, 4, :], dn[:, 4, :], a[:, :], ALU.mult))
                    dve.wait_ge(h_ready, b + 1)
                    s.done(nc.vector.tensor_tensor(dn[:, 0, :], h[:, 0:HID], dn[:, 1, :], ALU.mult))
                    s.done(nc.vector.tensor_tensor(slope[:, :], dn[:, 0, :], dn[:, 4, :], ALU.add))
                    s.end()
                    dve.wait_ge(dh_ready, b + 1)
                    wait(dve, g1_ready, b)
                    nc.vector.tensor_tensor(da[:, :], p_dh[:, 0:HID], slope[:, :], ALU.mult).then_inc(da_ready, 1)
                    if has_out:
                        out_(b - 1, 1 - p)
                    dve.wait_ge(g1_ready, b + 1)
                    for w_, g_ in ((w1T[:, :], g_w1T), (b1c[:, :], g_b1c), (b1r[:, :], g_b1r)):
                        nc.vector.scalar_tensor_tensor(w_, g_, -GRAD, w_, ALU.mult, ALU.add).then_inc(w1_new, 1)
                    for w_, g_ in ((w2T[:, :], g_w2T), (w2[:, :], g_w2)):
                        nc.vector.scalar_tensor_tensor(w_, g_, -GRAD, w_, ALU.mult, ALU.add).then_inc(w2_new, 1)

                def out_(b, p):
                    dve.wait_ge(out_ready, b + 1)
                    xb = x[:, bass.ds(b, 1), :].rearrange("p a d -> p (a d)")
                    nc.vector.tensor_tensor(xb, p_out[:, 0:P], xb, ALU.add).then_inc(added, 1)

                scan(dve, pre, main, out_)

            @block.scalar
            def _(act):
                act.wait_ge(m["loaded_scan"], 16 * SCAN_LOADS)

                def pre(b, p):
                    act.wait_ge(turned, b + 1)
                    if not (isinstance(b, int) and b < 2):
                        act.wait_ge(out_ready, b - 1)
                    nc.scalar.activation(xnT[:, p, :], p_pre[:, 0:P], ACT.Copy).then_inc(turned_sb, 1)
                    act.wait_ge(projected, b + 1)
                    if not (isinstance(b, int) and b < 2):
                        act.wait_ge(g1_ready, b - 1)
                        act.wait_ge(aq_ready, b - 1)
                    nc.scalar.activation(z[:, p, :], p_pre[:, 128:256], ACT.Copy).then_inc(projected_sb, 1)
                    nc.scalar.activation(zq[:, p, :], p_pre[:, 256:512], ACT.Copy).then_inc(projected_sb, 1)

                def main(b, p, has_out):
                    act.wait_ge(acts_ready, b + 1)
                    wait(act, e_ready, b)
                    nc.scalar.activation(hT[0:HID, :], p_aT[0:HID, 0:P], ACT.Gelu, bias=b1c[:, 0:1]).then_inc(hT_ready, 1)
                    act.wait_ge(a_safe, b + 1)
                    nc.scalar.activation(a2[:, :], a[:, :], ACT.Square, scale=0.5).then_inc(th_mid, 1)
                    wait(act, g2_ready, b)
                    nc.scalar.activation(h[:, 0:HID], a[:, :], ACT.Gelu).then_inc(h_ready, 1)
                    act.wait_ge(th_mid, b + 1)
                    nc.scalar.activation(th[:, :], a2[:, :], ACT.Tanh).then_inc(th_ready, 1)
                    act.wait_ge(e_ready, b + 1)
                    nc.scalar.activation(e[:, :], p_e[:, 0:P], ACT.Copy).then_inc(e_sb, 1)
                    if has_out:
                        out_(b - 1, 1 - p)

                def out_(b, p):
                    act.wait_ge(aq_ready, b + 1)
                    wait(act, out_ready, b)
                    nc.scalar.activation(hqT[0:HID, :], p_aT[0:HID, 128:256], ACT.Gelu, bias=b1c[:, 0:1]).then_inc(hqT_ready, 1)

                scan(act, pre, main, out_)

            @block.tensor
            def _(pe):
                pe.wait_ge(m["loaded_scan"], 16 * SCAN_LOADS)
                pe.wait_ge(set_pool, 6)
                pe.wait_ge(set_dve, 2)
                mm = nc.tensor.matmul

                def pre(b, p):
                    pe.wait_ge(pre_dve, b * 3 + 3)
                    wait(pe, projected_sb, 2 * b)
                    nc.tensor.transpose(p_pre[:, 0:P], xn[:, p, :], eye).then_inc(turned, 1)
                    pe.wait_ge(turned_sb, b + 1)
                    mm(p_pre[:, 128:256], xnT[:, p, :], m["w"]("tk"), start=True, stop=True)
                    mm(p_pre[:, 256:384], m["w"]("tk"), xnT[:, p, :], start=True, stop=True)
                    mm(p_pre[:, 384:512], m["w"]("tq"), xnT[:, p, :], start=True, stop=True).then_inc(projected, 1)

                def main(b, p, has_out):
                    pe.wait_ge(projected_sb, 2 * b + 2)
                    wait(pe, w1_new, 3 * b)
                    mm(p_aT[0:HID, 0:P], w1T[:, :], zq[:, p, 0:P], start=True, stop=True).then_inc(acts_ready, 1)
                    wait(pe, a_safe, b)
                    mm(p_a[:, 0:HID], zq[:, p, 0:P], w1T[:, :], start=True, stop=False)
                    mm(p_a[:, 0:HID], ones[0:1, :], b1r[:, :], start=False, stop=True).then_inc(a_ready, 1)
                    wait(pe, eT_sb, b)
                    mm(p_eT[:, 0:P], tkv[:, :], xnT[:, p, :], start=True, stop=False)
                    pe.wait_ge(hT_ready, b + 1)
                    wait(pe, w2_new, 2 * b)
                    mm(p_eT[:, 0:P], w2T[:, :], hT[:, :], start=False, stop=True).then_inc(eT_ready, 1)
                    wait(pe, e_sb, b)
                    mm(p_e[:, 0:P], xnT[:, p, :], tkv[:, :], start=True, stop=False)
                    mm(p_e[:, 0:P], hT[:, :], w2T[:, :], start=False, stop=True).then_inc(e_ready, 1)
                    pe.wait_ge(eT_sb, b + 1)
                    wait(pe, da_ready, b)
                    mm(p_dh[:, 0:HID], eT[:, :], w2[:, :], start=True, stop=True).then_inc(dh_ready, 1)
                    if has_out:
                        out_(b - 1, 1 - p)
                    pe.wait_ge(e_sb, b + 1)
                    pe.wait_ge(h_ready, b + 1)
                    mm(g_w2T, h[:, :], e[:, :], start=True, stop=True)
                    mm(g_w2, e[:, :], h[:, 0:HID], start=True, stop=True).then_inc(g2_ready, 1)
                    pe.wait_ge(da_ready, b + 1)
                    mm(g_b1c, da[:, :], ones[:, 0:1], start=True, stop=True)
                    mm(g_b1r, ones[:, 0:1], da[:, :], start=True, stop=True)
                    mm(g_w1T, z[:, p, :], da[:, :], start=True, stop=True).then_inc(g1_ready, 1)

                def out_(b, p):
                    pe.wait_ge(w1_new, 3 * b + 3)
                    pe.wait_ge(hT_ready, b + 1)
                    mm(p_aT[0:HID, 128:256], w1T[:, :], zq[:, p, P:2 * P], start=True, stop=True).then_inc(aq_ready, 1)
                    wait(pe, added, b)
                    mm(p_out[:, 0:P], xnT[:, p, :], m["w"]("tq"), start=True, stop=False)
                    pe.wait_ge(hqT_ready, b + 1)
                    pe.wait_ge(w2_new, 2 * b + 2)
                    mm(p_out[:, 0:P], hqT[:, :], w2T[:, :], start=False, stop=True).then_inc(out_ready, 1)

                scan(pe, pre, main, out_)


def attention(nc, m, name, T, weights, context, mask, mask_rows, norm_context, out_proj, exp_scale, sel):
    x, c = m["x"], m["c"]
    eye, ones, ones_bf = m["eye"], m["ones"], m["ones_bf"]
    GW = HG * T
    n_src = 2 if context else 1
    V1 = DH + 1
    ctx = ExitStack()
    with ctx:
        def sb(n, shape, dt=F32):
            return ctx.enter_context(nc.sbuf_tensor(f"{name}_{n}", shape, dt))

        def sem(n):
            return ctx.enter_context(nc.semaphore(f"{name}_{n}"))

        stats = sb("stats", [P, 2, 2, 6])
        mv = sb("mv", [P, 2, 2, 2])
        var = sb("var", [P, 2, 2])
        rstd = sb("rstd", [P, 2, 2])
        xn = sb("xn", [P, 2, P])
        cn = sb("cn", [TC, 2, P])
        xT = sb("xT", [P, P])
        cT = sb("cT", [P, TC])
        qT = sb("qT", [P, 2, HG, P])
        kT = sb("kT", [P, 2, T])
        v = sb("v", [T, 2, NH, V1])
        top = sb("top", [P, NH])
        prob = sb("prob", [P, 2, NH, T])
        pT = sb("pT", [T, NG, HG, P])
        inv = sb("inv", [P, NH])
        o = sb("o", [P, NH, DH])
        oT = sb("oT", [P, P])

        p_s = ctx.enter_context(nc.psum_tensor(f"{name}_p_s", [P, NG, 512], F32))
        p_pT = ctx.enter_context(nc.psum_tensor(f"{name}_p_pT", [P, 2, 512], F32))
        p_in = ctx.enter_context(nc.psum_tensor(f"{name}_p_in", [P, 512], F32))
        p_o = ctx.enter_context(nc.psum_tensor(f"{name}_p_o", [P, 512], F32))
        scores = p_s[:, :, 0:GW].rearrange("p g (h k) -> p g h k", k=T)
        C_IN = P
        V_IN = P + max(T, P)

        set_up = sem("set_up")
        counted, in_pool, in_dve = sem("counted"), sem("in_pool"), sem("in_dve")
        turned, turned_sb, projected = sem("turned"), sem("turned_sb"), sem("projected")
        q_sb, kv_sb = sem("q_sb"), sem("kv_sb")
        scored, top_done, shifted, exped = sem("scored"), sem("top_done"), sem("shifted"), sem("exped")
        p_turned, pT_act, pT_dve = sem("p_turned"), sem("pT_act"), sem("pT_dve")
        mixed, inv_done, o_done, res_done = sem("mixed"), sem("inv_done"), sem("o_done"), sem("res_done")
        o_turned, oT_sb, projected_o = sem("o_turned"), sem("oT_sb"), sem("projected_o")

        norm_n = 2 if norm_context else 1
        copied = sem("copied")
        n_copies = (1 if mask else 0) + (1 if context and not norm_context else 0)
        c_fix = sb("c_fix", [TC, 2, P])
        m_fix = sb("m_fix", [P, 2, TC], BF16)

        def at(tile, b):
            return tile[:, bass.ds(b, 1), :].rearrange("p a d -> p (a d)")

        with nc.Block() as block:
            @block.gpsimd
            def _(pool):
                nc.gpsimd.memset(v[:, :, :, DH:V1], 1.0).then_inc(set_up, 1)
                nc.gpsimd.memset(mv[:, :, :, :], 1.0).then_inc(set_up, 1)

                def rstd_of(b, p):
                    pool.wait_ge(counted, (b + 1) * (2 * norm_n))
                    pass_waits(pool, m)
                    nc.gpsimd.tensor_scalar(var[:, p, 0:norm_n], mv[:, p, 0:norm_n, 1], EPS, None, ALU.add).then_inc(in_pool, 1)
                    pool.wait_ge(in_pool, b * 2 + 1)
                    nc.gpsimd.tensor_tensor(rstd[:, p, 0:norm_n], var[:, p, 0:norm_n], m["half_power"][:, 0:norm_n], ALU.pow).then_inc(in_pool, 1)

                def copy_in(b, p):
                    if mask:
                        wait(pool, scored, b - 1)
                        pass_waits(pool, m)
                        nc.gpsimd.tensor_copy(m_fix[:, p, :], at(m[mask], b)).then_inc(copied, 1)
                    if context and not norm_context:
                        wait(pool, turned, b - 1)
                        pass_waits(pool, m)
                        nc.gpsimd.tensor_copy(c_fix[:, p, :], at(c, b)).then_inc(copied, 1)

                staggered(pool, [(0, rstd_of), (0, copy_in)])

            @block.vector
            def _(dve):
                dve.wait_ge(set_up, 2)
                dve.wait_ge(m["loaded_rest"], 16 * m["n_rest"])

                def count(b, p):
                    s = Steps(dve, counted, b, 2 * norm_n)
                    s.done(nc.vector.bn_stats(stats[:, p, 0, :], at(x, b)))
                    pass_waits(dve, m)
                    s.done(nc.vector.bn_aggr(mv[:, p, 0, :], stats[:, p, 0, :]))
                    if norm_context:
                        s.done(nc.vector.bn_stats(stats[0:TC, p, 1, :], at(c, b)))
                        pass_waits(dve, m)
                        s.done(nc.vector.bn_aggr(mv[0:TC, p, 1, :], stats[0:TC, p, 1, :]))
                    s.end()

                def normalise(b, p):
                    dve.wait_ge(in_pool, b * 2 + 2)
                    wait(dve, turned, b - 1)
                    nc.vector.tensor_scalar(xn[:, p, :], at(x, b), mv[:, p, 0, 0:1], rstd[:, p, 0:1],
                                            ALU.subtract, ALU.mult).then_inc(in_dve, 1)
                    if norm_context:
                        nc.vector.tensor_scalar(cn[:, p, :], at(c, b), mv[0:TC, p, 1, 0:1], rstd[0:TC, p, 1:2],
                                                ALU.subtract, ALU.mult).then_inc(in_dve, 1)

                def masked_q(b, p):
                    dve.wait_ge(projected, b + 1)
                    wait(dve, scored, b - 1)
                    mask_ap = m["headsel"][:, sel, :].unsqueeze(2).to_broadcast([P, HG, P])
                    src = p_in[:, 0:P].unsqueeze(1).to_broadcast([P, HG, P])
                    if name == "x1":
                        ins = nc.vector.scalar_tensor_tensor(qT[:, p, :, :], src, m["col"]("x1_bq"), mask_ap, ALU.add, ALU.mult)
                    else:
                        ins = nc.vector.tensor_tensor(qT[:, p, :, :], src, mask_ap, ALU.mult)
                    ins.then_inc(q_sb, 1)

                def shift(b, p):
                    dve.wait_ge(scored, b + 1)
                    nc.vector.tensor_reduce(top[:, :].rearrange("p (g h) -> p g h", h=HG), scores, AX.X, ALU.max).then_inc(top_done, 1)
                    dve.wait_ge(top_done, b + 1)
                    wait(dve, p_turned, 4 * (b - 1))
                    nc.vector.tensor_tensor(prob[:, p, :, :].rearrange("p (g h) k -> p g h k", h=HG), scores,
                                            top[:, :].rearrange("p (g h) -> p g h", h=HG).unsqueeze(3).to_broadcast([P, NG, HG, T]),
                                            ALU.subtract).then_inc(shifted, 1)

                def pT_odd(b, p):
                    for g in (1, 3):
                        dve.wait_ge(p_turned, 4 * b + g + 1)
                        wait(dve, mixed, b)
                        nc.vector.tensor_copy(pT[:, g, :, :].rearrange("k h q -> k (h q)"), p_pT[0:T, 1, :]).then_inc(pT_dve, 1)

                def finish(b, p):
                    dve.wait_ge(mixed, b + 1)
                    mix = p_o[:, 0:NH * V1].rearrange("p (h v) -> p h v", v=V1)
                    wait(dve, o_turned if out_proj else res_done, b)
                    nc.vector.reciprocal(inv[:, :].unsqueeze(2), mix[:, :, DH:V1]).then_inc(inv_done, 1)
                    dve.wait_ge(inv_done, b + 1)
                    nc.vector.tensor_tensor(o[:, :, :], mix[:, :, 0:DH], inv[:, :].unsqueeze(2).to_broadcast([P, NH, DH]),
                                            ALU.mult).then_inc(o_done, 1)

                def residual(b, p):
                    xb = at(x, b)
                    if out_proj:
                        dve.wait_ge(projected_o, b + 1)
                        nc.vector.tensor_tensor(xb, p_o[:, 256:384], xb, ALU.add).then_inc(res_done, 1)
                    else:
                        dve.wait_ge(o_done, b + 1)
                        nc.vector.tensor_tensor(xb, o[:, :, :].rearrange("p h d -> p (h d)"), xb, ALU.add).then_inc(res_done, 1)

                staggered(dve, [(0, count), (1, shift), (3, residual), (0, normalise), (2, pT_odd),
                                (0, masked_q), (2, finish)])

            @block.scalar
            def _(act):
                act.wait_ge(set_up, 1)
                act.wait_ge(m["loaded_rest"], 16 * m["n_rest"])

                def turn_in(b, p):
                    act.wait_ge(turned, b + 1)
                    wait(act, projected, b)
                    if name == "x0":
                        nc.scalar.activation(xT[:, :], p_in[:, 0:P], ACT.Identity, bias=m["col"]("x0_b1"), scale=m["col"]("x0_g1")).then_inc(turned_sb, 1)
                        nc.scalar.activation(cT[:, :], p_in[:, C_IN:C_IN + TC], ACT.Identity, bias=m["col"]("x0_b2"), scale=m["col"]("x0_g2")).then_inc(turned_sb, 1)
                    else:
                        nc.scalar.activation(xT[:, :], p_in[:, 0:P], ACT.Copy).then_inc(turned_sb, 1)
                        if context:
                            nc.scalar.activation(cT[:, :], p_in[:, C_IN:C_IN + TC], ACT.Copy).then_inc(turned_sb, 1)

                def kv(b, p):
                    act.wait_ge(q_sb, b + 1)
                    wait(act, scored, b - 1)
                    if name == "x1":
                        nc.scalar.activation(kT[:, p, :], p_in[:, C_IN:C_IN + T], ACT.Identity, bias=m["col"]("x1_bk")).then_inc(kv_sb, 1)
                    else:
                        nc.scalar.activation(kT[:, p, :], p_in[:, C_IN:C_IN + T], ACT.Copy).then_inc(kv_sb, 1)
                    wait(act, mixed, b - 1)
                    nc.scalar.activation(v[:, p, :, 0:DH], p_in[0:T, V_IN:V_IN + P].rearrange("k (h d) -> k h d", d=DH),
                                         ACT.Copy).then_inc(kv_sb, 1)

                def exps(b, p):
                    act.wait_ge(shifted, b + 1)
                    pr = prob[:, p, :, :].rearrange("p h k -> p (h k)")
                    nc.scalar.activation(pr, pr, ACT.Exp, scale=exp_scale).then_inc(exped, 1)

                def pT_even(b, p):
                    for g in (0, 2):
                        act.wait_ge(p_turned, 4 * b + g + 1)
                        wait(act, mixed, b)
                        nc.scalar.activation(pT[:, g, :, :].rearrange("k h q -> k (h q)"), p_pT[0:T, 0, :], ACT.Copy).then_inc(pT_act, 1)

                def turn_o(b, p):
                    if out_proj:
                        act.wait_ge(o_turned, b + 1)
                        nc.scalar.activation(oT[:, :], p_o[:, 256:384], ACT.Copy).then_inc(oT_sb, 1)

                staggered(act, [(3, turn_o), (2, pT_even), (0, turn_in), (1, exps), (0, kv)])

            @block.tensor
            def _(pe):
                mm = nc.tensor.matmul
                pe.wait_ge(m["loaded_rest"], 16 * m["n_rest"])
                pe.wait_ge(set_up, 1)

                def turn_in(b, p):
                    pe.wait_ge(in_dve, (b + 1) * norm_n)
                    wait(pe, kv_sb, 2 * b)
                    last = nc.tensor.transpose(p_in[:, 0:P], xn[:, p, :], eye)
                    if context:
                        if norm_context:
                            src = cn[:, p, :]
                        else:
                            src = c_fix[:, p, :]
                            pe.wait_ge(copied, n_copies * (b + 1))
                        last = nc.tensor.transpose(p_in[:, C_IN:C_IN + TC], src, eye[0:TC, 0:TC])
                    last.then_inc(turned, 1)

                def project(b, p):
                    pe.wait_ge(turned_sb, n_src * (b + 1))
                    src = cT if context else xT
                    if weights == "s1":
                        wk, wv = (m["half"][:, j, :, :].rearrange("p h d -> p (h d)") for j in range(2))
                    else:
                        wk, wv = m["w"](weights + "_k"), m["w"](weights + "_v")
                    mm(p_in[:, 0:P], m["w"](weights + "_q"), xT[:, :], start=True, stop=True)
                    mm(p_in[:, C_IN:C_IN + T], wk, src[:, :], start=True, stop=True)
                    last = mm(p_in[0:T, V_IN:V_IN + P], src[:, :], wv, start=True, stop=name != "x1")
                    if name == "x1":
                        last = mm(p_in[0:T, V_IN:V_IN + P], ones[0:1, 0:T], m["row"]("x1_v"), start=False, stop=True)
                    last.then_inc(projected, 1)

                def score(b, p):
                    pe.wait_ge(q_sb, b + 1)
                    pe.wait_ge(kv_sb, 2 * (b + 1))
                    wait(pe, shifted, b)
                    if mask:
                        pe.wait_ge(copied, n_copies * (b + 1))
                    for g in range(NG):
                        r = slice(R * g, R * g + mask_rows)
                        if mask:
                            mm(p_s[:, g, 0:GW].rearrange("p (h k) -> p h k", k=T), ones_bf[r, :],
                               m_fix[r, p, :].unsqueeze(1).to_broadcast([mask_rows, HG, T]), start=True, stop=False)
                        else:
                            mm(p_s[:, g, 0:GW], m["ident_bf"][:, :], m["alibi"][:, HG * g:HG * (g + 1), :].rearrange("p h k -> p (h k)"),
                               start=True, stop=False)
                    for h in range(HG):
                        for g in range(NG):
                            r = slice(R * g, R * (g + 1))
                            last = mm(p_s[:, g, h * T:(h + 1) * T], qT[r, p, h, :], kT[r, p, :], start=False, stop=h == HG - 1)
                    last.then_inc(scored, 1)

                def turn_p(b, p):
                    pe.wait_ge(exped, b + 1)
                    for g in range(NG):
                        if g % 2 == 0:
                            wait(pe, pT_act, 2 * b + g // 2)
                        else:
                            wait(pe, pT_dve, 2 * b + g // 2)
                        for h in range(HG):
                            last = nc.tensor.transpose(p_pT[0:T, g % 2, h * P:(h + 1) * P], prob[:, p, HG * g + h, :], eye)
                        last.then_inc(p_turned, 1)

                def mix(b, p):
                    wait(pe, res_done, b)
                    for g in range(NG):
                        if g % 2 == 0:
                            pe.wait_ge(pT_act, 2 * b + g // 2 + 1)
                        else:
                            pe.wait_ge(pT_dve, 2 * b + g // 2 + 1)
                        for h in range(HG * g, HG * (g + 1)):
                            last = mm(p_o[:, h * V1:(h + 1) * V1], pT[:, g, h % HG, :], v[:, p, h, :], start=True, stop=True)
                    last.then_inc(mixed, 1)

                def project_o(b, p):
                    if not out_proj:
                        return
                    pe.wait_ge(o_done, b + 1)
                    nc.tensor.transpose(p_o[:, 256:384], o[:, :, :].rearrange("p h d -> p (h d)"), eye).then_inc(o_turned, 1)
                    pe.wait_ge(oT_sb, b + 1)
                    mm(p_o[:, 256:384], oT[:, :], m["w"](weights + "_o"), start=True, stop=False)
                    mm(p_o[:, 256:384], ones[0:1, :], m["row"](weights + "_o"), start=False, stop=True).then_inc(projected_o, 1)

                staggered(pe, [(1, score), (3, project_o), (2, turn_p), (0, turn_in), (2, mix), (0, project)])


def mask_parts(nc, pool, m, masks):
    g = nc.gpsimd
    s = Steps(pool, masks, 0, 11)
    f, hi, part, mask = (m[k][:, :, :] for k in ("mask_f", "mask_hi", "mask_part", "mask_1"))
    s.done(g.tensor_scalar(f, m["mask_i32"][:, :, :], -1.0, 10000.0, ALU.add, ALU.mult))
    s.done(g.tensor_copy(hi, f))
    s.done(g.tensor_scalar(mask, hi, m["mask_sel"][:, 0:1], None, ALU.mult))
    for r in (1, 2):
        s.done(g.tensor_tensor(f, f, hi, ALU.subtract))
        s.done(g.tensor_copy(hi, f))
        s.done(g.tensor_scalar(part, hi, m["mask_sel"][:, r:r + 1], None, ALU.mult))
        s.done(g.tensor_tensor(mask, mask, part, ALU.add))
    s.end()


def experts(nc, m, q, out):
    x, eye, ones = m["x"], m["eye"], m["ones"]
    GT = 4
    w1, w2, b1, b2, wr = (m[f"{k}_{q}"] for k in ("w1", "w2", "b1", "b2", "wr"))
    ctx = ExitStack()
    with ctx:
        def sb(n, shape, dt=F32):
            return ctx.enter_context(nc.sbuf_tensor(f"f{q}_{n}", shape, dt))

        def sem(n):
            return ctx.enter_context(nc.semaphore(f"f{q}_{n}"))

        def ps(n, shape, c):
            return c.enter_context(nc.psum_tensor(f"f{q}_{n}", shape, F32))

        def at(tile, b):
            return tile[:, bass.ds(b, 1), :].rearrange("p a d -> p (a d)")

        stats = sb("stats", [P, 2, 6])
        mv = sb("mv", [P, 2, 2])
        var = sb("var", [P, 2, 1])
        rstd = sb("rstd", [P, 2, 1])
        xn = sb("xn", [P, 2, P])
        xT = sb("xT", [P, 2, P])
        xTs = sb("xTs", [P, NB, P])
        lg = sb("lg", [P, NB, NE])
        best = sb("best", [P, 2, NB])
        where = sb("where", [P, 2, NB])
        gap = sb("gap", [P, NB])
        egap = sb("egap", [P, NB])
        den = sb("den", [P, NB])
        inv = sb("inv", [P, NB])
        one_hot = sb("one_hot", [P, 2, NB, NE])
        wts = sb("wts", [P, NB, NE])
        wT = sb("wT", [NE, NB, P])
        hT = sb("hT", [P, 2, FC, GT * P])

        counted, in_pool, in_dve = sem("counted"), sem("in_pool"), sem("in_dve")
        turned, turned_sb, routed, gap_ready = sem("turned"), sem("turned_sb"), sem("routed"), sem("gap_ready")
        router_dve, router_act = sem("router_dve"), sem("router_act")
        w_turned, w_sb, b2_ready, b2_added = sem("w_turned"), sem("w_sb"), sem("b2_ready"), sem("b2_added")
        masks = sem("masks")
        h_ready, h_sb, y_ready, combined = sem("h_ready"), sem("h_sb"), sem("y_ready"), sem("combined")

        with ExitStack() as pctx:
            p_t = ps("p_t", [P, 2, 512], pctx)
            p_l = ps("p_l", [P, 512], pctx)
            p_w = ps("p_w", [P, 4, 512], pctx)
            with nc.Block() as block:
                @block.gpsimd
                def _(pool):
                    def rstd_of(b, p):
                        pool.wait_ge(counted, (b + 1) * 2)
                        pass_waits(pool, m)
                        nc.gpsimd.tensor_scalar(var[:, p, :], mv[:, p, 1:2], EPS, None, ALU.add).then_inc(in_pool, 1)
                        pool.wait_ge(in_pool, b * 2 + 1)
                        nc.gpsimd.tensor_tensor(rstd[:, p, :], var[:, p, :], m["half_power"][:, 0:1], ALU.pow).then_inc(in_pool, 1)
                    staggered(pool, [(0, rstd_of)])

                @block.vector
                def _(dve):
                    def count(b, p):
                        s = Steps(dve, counted, b, 2)
                        s.done(nc.vector.bn_stats(stats[:, p, :], at(x, b)))
                        pass_waits(dve, m)
                        s.done(nc.vector.bn_aggr(mv[:, p, :], stats[:, p, :]))
                        s.end()

                    def normalise(b, p):
                        dve.wait_ge(in_pool, b * 2 + 2)
                        wait(dve, turned, b - 1)
                        nc.vector.tensor_scalar(xn[:, p, :], at(x, b), mv[:, p, 0:1], rstd[:, p, 0:1],
                                                ALU.subtract, ALU.mult).then_inc(in_dve, 1)

                    staggered(dve, [(0, count), (0, normalise)])
                    s = Steps(dve, router_dve, 0, 17)
                    dve.wait_ge(routed, NB)
                    logits = p_l[:, 0:NB * NE].rearrange("p (b e) -> p b e", e=NE)
                    s.done(nc.vector.tensor_copy(lg[:, :, :], logits))
                    for j in range(2):
                        hot = one_hot[:, j, :, :]
                        s.done(nc.vector.tensor_reduce(best[:, j, :], lg[:, :, :], AX.X, ALU.max))
                        s.done(nc.vector.tensor_tensor(hot, lg[:, :, :], best[:, j, :].unsqueeze(2).to_broadcast([P, NB, NE]), ALU.is_equal))
                        countdown = m["countdown"][:, :].unsqueeze(1).to_broadcast([P, NB, NE])
                        s.done(nc.vector.tensor_tensor(hot, hot, countdown, ALU.mult))
                        s.done(nc.vector.tensor_reduce(where[:, j, :], hot, AX.X, ALU.max))
                        s.done(nc.vector.tensor_tensor(hot, countdown, where[:, j, :].unsqueeze(2).to_broadcast([P, NB, NE]), ALU.is_equal))
                        if j == 0:
                            s.done(nc.vector.scalar_tensor_tensor(lg[:, :, :], hot, -3e38, lg[:, :, :], ALU.mult, ALU.add))
                    nc.vector.tensor_tensor(gap[:, :], best[:, 1, :], best[:, 0, :], ALU.subtract).then_inc(gap_ready, 1)
                    dve.wait_ge(router_act, 1)
                    s.done(nc.vector.tensor_scalar(den[:, :], egap[:, :], 1.0, None, ALU.add))
                    s.done(nc.vector.reciprocal(inv[:, :], den[:, :]))
                    s.done(nc.vector.tensor_tensor(one_hot[:, 1, :, :], one_hot[:, 1, :, :],
                                                   egap[:, :].unsqueeze(2).to_broadcast([P, NB, NE]), ALU.mult))
                    s.done(nc.vector.tensor_tensor(one_hot[:, 0, :, :], one_hot[:, 0, :, :], one_hot[:, 1, :, :], ALU.add))
                    s.done(nc.vector.tensor_tensor(wts[:, :, :], one_hot[:, 0, :, :],
                                                   inv[:, :].unsqueeze(2).to_broadcast([P, NB, NE]), ALU.mult))
                    s.end()
                    for g in range(4):
                        dve.wait_ge(w_turned, g + 1)
                        nc.vector.tensor_copy(wT[:, 4 * g:4 * g + 4, :].rearrange("e b t -> e (b t)"), p_w[0:NE, g, :]).then_inc(w_sb, 1)
                    for g in range(4):
                        dve.wait_ge(b2_ready, g + 1)
                        xg = x[:, 4 * g:4 * g + 4, :].rearrange("p b d -> p (b d)")
                        nc.vector.tensor_tensor(xg, p_w[:, g, :], xg, ALU.add).then_inc(b2_added, 1)

                @block.scalar
                def _(act):
                    def turn_in(b, p):
                        act.wait_ge(turned, b + 1)
                        wait(act, routed, b - 1)
                        nc.scalar.activation(xT[:, p, :], p_t[:, p, 0:P], ACT.Copy).then_inc(turned_sb, 1)
                        nc.scalar.activation(at(xTs, b), p_t[:, p, 0:P], ACT.Copy).then_inc(turned_sb, 1)
                    staggered(act, [(0, turn_in)])
                    act.wait_ge(gap_ready, 1)
                    nc.scalar.activation(egap[:, :], gap[:, :], ACT.Exp).then_inc(router_act, 1)

                @block.tensor
                def _(pe):
                    mm = nc.tensor.matmul

                    def turn_in(b, p):
                        pe.wait_ge(in_dve, b + 1)
                        wait(pe, turned_sb, 2 * (b - 1))
                        nc.tensor.transpose(p_t[:, p, 0:P], xn[:, p, :], eye).then_inc(turned, 1)

                    def route(b, p):
                        pe.wait_ge(turned_sb, 2 * (b + 1))
                        to = p_l[:, bass.ds(b * NE, NE)]
                        last = mm(to, xT[:, p, :], wr[:, :], start=True, stop=q == 1)
                        if q == 0:
                            last = mm(to, ones[0:1, :], m["br_0"][:, :], start=False, stop=True)
                        last.then_inc(routed, 1)

                    staggered(pe, [(0, turn_in), (1, route)])
                    pe.wait_ge(router_dve, 17)
                    for g in range(4):
                        for j in range(4):
                            last = nc.tensor.transpose(p_w[0:NE, g, P * j:P * j + P], wts[:, 4 * g + j, :], eye)
                        last.then_inc(w_turned, 1)
                    for g in range(4):
                        pe.wait_ge(w_sb, g + 1)
                        for j in range(4):
                            last = mm(p_w[:, g, P * j:P * j + P], wT[:, 4 * g + j, :], b2[:, :], start=True, stop=True)
                        last.then_inc(b2_ready, 1)

        with ExitStack() as pctx:
            p_h = ps("p_h", [P, FC, 512], pctx)
            p_y = ps("p_y", [P, 2, 512], pctx)
            with nc.Block() as block:
                def groups(eng, run):
                    run(0)
                    with eng.Fori(1, NB // GT) as g:
                        run(g)

                @block.tensor
                def _(pe):
                    mm = nc.tensor.matmul

                    def run(g):
                        def up(e):
                            n = g * NE + e
                            for k in range(FC):
                                wait(pe, h_sb, FC * (n - 1) + k + 1)
                                mm(p_h[:, k, :], w1[:, e, P * k:P * k + P],
                                   xTs[:, bass.ds(g * GT, GT), :].rearrange("p b t -> p (b t)"),
                                   start=True, stop=True).then_inc(h_ready, 1)

                        def down(e):
                            n = g * NE + e
                            wait(pe, combined, GT * (n - 1))
                            pe.wait_ge(h_sb, FC * n + FC)
                            for j in range(GT):
                                for k in range(FC):
                                    last = mm(p_y[:, e % 2, P * j:P * j + P], hT[:, e % 2, k, P * j:P * j + P],
                                              w2[:, e, k, :], start=k == 0, stop=k == FC - 1)
                            last.then_inc(y_ready, 1)
                        up(0)
                        for e in range(1, NE):
                            up(e)
                            down(e - 1)
                        down(NE - 1)
                    groups(pe, run)

                @block.scalar
                def _(act):
                    def run(g):
                        for e in range(NE):
                            n = g * NE + e
                            wait(act, y_ready, n - 1)
                            for k in range(FC):
                                act.wait_ge(h_ready, FC * n + k + 1)
                                nc.scalar.activation(hT[:, e % 2, k, :], p_h[:, k, :], ACT.Relu,
                                                     bias=b1[:, e, k:k + 1]).then_inc(h_sb, 1)
                    groups(act, run)

                @block.vector
                def _(dve):
                    def run(g):
                        for e in range(NE):
                            n = g * NE + e
                            dve.wait_ge(y_ready, n + 1)
                            wait(dve, combined, GT * n)
                            for j in range(GT):
                                xb = at(x, g * GT + j)
                                nc.vector.scalar_tensor_tensor(xb, p_y[:, e % 2, P * j:P * j + P],
                                                               wts[:, bass.ds(g * GT + j, 1), e:e + 1].rearrange("p a b -> p (a b)"),
                                                               xb, ALU.mult, ALU.add).then_inc(combined, 1)
                    groups(dve, run)

                @block.gpsimd
                def _(pool):
                    if q == 0:
                        mask_parts(nc, pool, m, masks)

                @block.sync
                def _(sp):
                    if out is not None:
                        for g in range(NB // GT):
                            sp.wait_ge(combined, GT * NE * (g + 1))
                            sp.dma_start(out[GT * g:GT * (g + 1)].rearrange("b p d -> p b d"),
                                         x[:, GT * g:GT * (g + 1), :]).then_inc(m["stored"], 16)
                        sp.wait_ge(m["stored"], 16 * (NB // GT))


def kernel(**inputs):
    import numpy as np
    import concourse.bacc as bacc
    from concourse import mybir as mb
    from concourse.bass_utils import run_bass_kernel_spmd
    import ml_dtypes

    a = {k: np.asarray(v) for k, v in inputs.items()}
    T = lambda w: np.ascontiguousarray(np.swapaxes(w, -1, -2))
    squares = {"ident": np.eye(P, dtype=np.float32),
               "tk": T(a["L0_attn_t_k"]), "tv": T(a["L0_attn_t_v"]), "tq": T(a["L0_attn_t_q"]),
               "x0_q": T(a["L0_xattn_Wq"]), "x0_k": T(a["L0_xattn_Wk"]), "x0_v": T(a["L0_xattn_Wv"]),
               "x0_o": T(a["L0_xattn_Wo"]), "s1_q": T(a["L1_attn_Wq"]), "s1_o": T(a["L1_attn_Wo"]),
               "x1_q": T(a["L1_xattn_Wq"]), "x1_k": T(a["L1_xattn_Wk"]), "x1_v": T(a["L1_xattn_Wv"])}
    head = np.arange(P) // DH
    select = (head[:, None] % HG == np.arange(HG)[None, :]).astype(np.float32)
    slopes = 2.0 ** -(np.arange(NH) + 1.0)
    dist = np.abs(np.arange(P)[:, None] - np.arange(P)[None, :])
    t = {
        "x": a["x"], "ctx": a["ctx_1024"],
        "squares": np.stack([squares[k] for k in SQUARES]),
        "halves": np.stack([T(a["L1_attn_Wk"]), T(a["L1_attn_Wv"])]),
        "cols": np.stack([a[k] for k in ("L0_xattn_g1", "L0_xattn_b1", "L0_xattn_g2", "L0_xattn_b2",
                                         "L1_xattn_bq", "L1_xattn_bk")], axis=1),
        "rows": np.stack([a[k] for k in ("L0_xattn_bo", "L1_attn_bo", "L1_xattn_bv", "L0_attn_b2")]),
        "scan_w1T": T(a["L0_attn_W1"]), "scan_w2T": T(a["L0_attn_W2"]), "scan_w2": a["L0_attn_W2"],
        "scan_b1": a["L0_attn_b1"],
        "mask_0": a["mask_BxS2_bf1"].view(np.uint8), "mask_1": a["mask_BxS2_ik0"],
        "mask_select": (np.arange(P)[:, None] % R == np.arange(3)[None, :]).astype(np.float32),
        "head_select": np.stack([select, select / np.float32(SQRT_DH)], axis=1).astype(np.float32),
        "alibi": (-dist[:, None, :] * slopes[None, :, None]).astype(ml_dtypes.bfloat16),
        "countdown": np.tile(np.arange(NE, 0, -1, dtype=np.float32), (P, 1)),
        "w1_0": a["L0_ffn_W1"], "w2_0": a["L0_ffn_W2"], "b1_0": a["L0_ffn_b1"], "b2_0": a["L0_ffn_b2"],
        "wr_0": a["L0_ffn_W_router"], "br_0": a["L0_ffn_b_router"],
        "w1_1": T(a["L1_ffn_w1"]), "w2_1": T(a["L1_ffn_w2"]), "b1_1": a["L1_ffn_b1"], "b2_1": a["L1_ffn_b2"],
        "wr_1": T(a["L1_ffn_gate_w"]),
    }
    nc = bacc.Bacc("TRN2", target_bir_lowering=False, num_devices=1)
    arrays, aps = {}, {}
    for name, v in t.items():
        v = np.ascontiguousarray(v)
        arrays[f"in_{name}"] = v
        aps[name] = nc.dram_tensor(f"in_{name}", v.shape, mb.dt.from_np(v.dtype), kind="ExternalInput").ap()
    out = nc.dram_tensor("out", (NB, P, P), F32, kind="ExternalOutput").ap()
    build(nc, aps, out)
    r = run_bass_kernel_spmd(nc, [arrays], core_ids=[0])
    return r.results[0]["out"]
```

```python
import concourse.bass as bass
from concourse import mybir
from contextlib import ExitStack

F32 = mybir.dt.float32
BF16 = mybir.dt.bfloat16
I32 = mybir.dt.int32
U8 = mybir.dt.uint8
ALU = mybir.AluOpType
ACT = mybir.ActivationFunctionType
AX = mybir.AxisListType

NB = 16
P = 128
TC = 77
NH = 16
DH = P // NH
NG = 4
HG = NH // NG
R = P // NG
HID = 32
NE = 8
FF = 512
FC = FF // P
EPS = 1e-5
LR = 0.001
GRAD = LR * 2.0 / (P * P)
SQRT_DH = float(DH) ** 0.5
DENSITY = 0.3989422804014327

SQUARES = ["ident", "tk", "tv", "tq",
           "x0_q", "x0_k", "x0_v", "x0_o", "s1_q", "s1_o", "x1_q", "x1_k", "x1_v"]
HALVES = ["s1_k", "s1_v"]
COLS = ["x0_g1", "x0_b1", "x0_g2", "x0_b2", "x1_bq", "x1_bk"]
ROWS = ["x0_o", "s1_o", "x1_v", "s_b2"]


def wait(eng, sem, value):
    if isinstance(value, int) and value <= 0:
        return
    eng.wait_ge(sem, value)


def pass_waits(eng, m):
    eng.sem_inc(m["passed"], 1)


class Steps:

    def __init__(self, eng, sem, b, per):
        self.eng, self.sem, self.base, self.per, self.n = eng, sem, b * per, per, 0

    def done(self, ins):
        self.n += 1
        assert self.n <= self.per
        ins.then_inc(self.sem, 1)
        self.eng.wait_ge(self.sem, self.base + self.n)

    def end(self):
        assert self.n == self.per, (self.n, self.per)


def staggered(eng, stages, first=4):
    lags = [lag for lag, _ in stages]
    last = NB + min(min(lags), 0) // 2 * 2

    def peeled(k):
        for lag, stage in stages:
            if 0 <= k - lag < NB:
                stage(k - lag, (k - lag) % 2)
    for k in range(min(lags), first):
        peeled(k)
    with eng.Fori(0, (last - first) // 2) as i:
        for u in range(2):
            for lag, stage in stages:
                stage(i * 2 + (first + u - lag), (first + u - lag) % 2)
    for k in range(last, NB + max(lags)):
        peeled(k)


def build(nc, t, out):
    ctx = ExitStack()
    with ctx:
        def sb(name, shape, dt=F32):
            return ctx.enter_context(nc.sbuf_tensor(name, shape, dt))

        def sem(name):
            return ctx.enter_context(nc.semaphore(name))

        x = sb("x", [P, NB, P])
        c = sb("c", [TC, NB, P])
        sq = sb("sq", [P, len(SQUARES), P])
        half = sb("half", [P, len(HALVES), NH, DH])
        cols = sb("cols", [P, len(COLS)])
        rows = sb("rows", [1, len(ROWS), P])
        ones = sb("ones", [P, P])
        ones_bf = sb("ones_bf", [P, P], BF16)
        ident_bf = sb("ident_bf", [P, P], BF16)
        half_power = sb("half_power", [P, 2])
        headsel = sb("headsel", [P, 3, HG])
        alibi = sb("alibi", [P, NH, P], BF16)
        m = dict(x=x, c=c, sq=sq, half=half, cols=cols, rows=rows, ones=ones, ones_bf=ones_bf,
                 ident_bf=ident_bf, half_power=half_power, headsel=headsel, alibi=alibi)
        m["eye"] = sq[:, SQUARES.index("ident"), :]
        ctx_k = sb("ctx_k", [P, 2, NB, TC])
        ctx_v = sb("ctx_v", [TC, 2, NB, P])
        m["ctxT"] = sb("ctxT", [P, NB, TC])
        m["v_wide"] = sb("v_wide", [P, 2, NH, P])
        m.update(ctx_k=ctx_k, ctx_v=ctx_v)
        for q in (0, 1):
            m[f"kT_x{q}"], m[f"v_x{q}"] = ctx_k[:, q, :, :], ctx_v[:, q, :, :]
        m["w"] = lambda name: sq[:, SQUARES.index(name), :]
        m["row"] = lambda name: rows[0:1, ROWS.index(name), :]
        m["col"] = lambda name: cols[:, COLS.index(name):COLS.index(name) + 1]
        for q in (0, 1):
            m[f"w1_{q}"] = sb(f"w1_{q}", [P, NE, FF])
            m[f"w2_{q}"] = sb(f"w2_{q}", [P, NE, FC, P])
            m[f"b1_{q}"] = sb(f"b1_{q}", [P, NE, FC])
            m[f"b2_{q}"] = sb(f"b2_{q}", [NE, P])
            m[f"wr_{q}"] = sb(f"wr_{q}", [P, NE])
        m["br_0"] = sb("br_0", [1, NE])
        m["scan_w1T"] = sb("scan_w1T", [P, HID])
        m["scan_w2T"] = sb("scan_w2T", [HID + 1, P])
        m["scan_w2"] = sb("scan_w2", [P, HID])
        m["scan_b1c"] = sb("scan_b1c", [HID, 1])
        m["scan_b1r"] = sb("scan_b1r", [1, HID])
        m["mask_0"] = sb("mask_0", [P, NB, TC], BF16)
        m["mask_1"] = sb("mask_1", [P, NB, TC], BF16)
        m["mask_u8"] = sb("mask_u8", [P, NB, TC], U8)
        m["mask_i32"] = sb("mask_i32", [P, NB, TC], I32)
        m["mask_f"] = sb("mask_f", [P, NB, TC])
        m["mask_hi"] = sb("mask_hi", [P, NB, TC], BF16)
        m["mask_part"] = sb("mask_part", [P, NB, TC], BF16)
        m["mask_sel"] = sb("mask_sel", [P, 3])
        m["countdown"] = sb("countdown", [P, NE])

        loaded_scan = sem("loaded_scan")
        loaded_mask = sem("loaded_mask")
        loaded_context = sem("loaded_context")
        loaded_rest = sem("loaded_rest")
        stored = sem("stored")
        m.update(loaded_scan=loaded_scan, loaded_mask=loaded_mask, loaded_context=loaded_context, loaded_rest=loaded_rest,
                 stored=stored)
        m["passed"] = sem("passed")
        load_and_scan(nc, t, m)
        attention(nc, m, "x0", TC, mask="mask_0", mask_rows=1, exp_scale=1.0, sel=1)
        experts(nc, m, 0, None)
        attention(nc, m, "s1", P, mask=None, mask_rows=0, exp_scale=1.0 / SQRT_DH, sel=0)
        attention(nc, m, "x1", TC, mask="mask_1", mask_rows=3, exp_scale=1.0, sel=1)
        experts(nc, m, 1, out)


def load_and_scan(nc, t, m):
    x, c = m["x"], m["c"]
    eye, ones = m["eye"], m["ones"]
    ctx = ExitStack()
    with ctx:
        def sb(name, shape, dt=F32):
            return ctx.enter_context(nc.sbuf_tensor(name, shape, dt))

        def ps(name):
            return ctx.enter_context(nc.psum_tensor(name, [P, 512], F32))

        def sem(name):
            return ctx.enter_context(nc.semaphore(name))

        w1T, w2T, w2, b1c, b1r = (m[k] for k in ("scan_w1T", "scan_w2T", "scan_w2", "scan_b1c", "scan_b1r"))
        tkv = sb("tkv", [P, P])
        stats = sb("stats", [P, 2, 6])
        mv = sb("mv", [P, 2, 2])
        var = sb("var", [P, 2, 1])
        rstd = sb("rstd", [P, 2, 1])
        xn = sb("xn", [P, 2, P])
        xnT = sb("xnT", [P, 2, P])
        z = sb("z", [P, 2, P])
        zq = sb("zq", [P, 2, 2 * P])
        hT = sb("hT", [HID + 1, P])
        hqT = sb("hqT", [HID + 1, P])
        h = sb("h", [P, HID + 1])
        zero = sb("zero", [P, HID])
        a = sb("a", [P, HID])
        a2 = sb("a2", [P, HID])
        th = sb("th", [P, HID])
        dn = sb("dn", [P, 5, HID])
        slope = sb("slope", [P, HID])
        eT = sb("eT", [P, P])
        e = sb("e", [P, P])
        da = sb("da", [P, HID])

        p_pre, p_aT, p_a, p_eT, p_e, p_grad, p_out, p_ctx = (
            ps(f"p_{n}") for n in ("pre", "aT", "a", "eT", "e", "grad", "out", "ctx"))
        p_dh = p_a[:, 128:256]
        pc_turned, pc_k, pc_v = p_ctx[:, 0:TC], p_ctx[:, 2 * P:2 * P + 2 * TC], p_ctx[0:TC, 0:2 * P]
        g_w1T, g_w2T, g_w2 = p_grad[:, 0:HID], p_grad[0:HID + 1, 128:256], p_grad[:, 256:256 + HID]
        g_b1c, g_b1r = p_grad[0:HID, 300:301], p_grad[0:1, 320:320 + HID]

        set_pool, set_dve = sem("scan_set_pool"), sem("scan_set_dve")
        masks = sem("scan_masks")
        pre_dve, pre_pool = sem("pre_dve"), sem("pre_pool")
        normed, turned, turned_sb = sem("s_normed"), sem("s_turned"), sem("s_turned_sb")
        projected, projected_sb = sem("s_projected"), sem("s_projected_sb")
        acts_ready, a_ready, hT_ready, h_ready = (sem(n) for n in ("s_acts", "s_a", "s_hT", "s_h"))
        a_safe, th_ready, slope_dve = sem("s_a_safe"), sem("s_th"), sem("s_slope")
        th_mid = sem("s_th_mid")
        eT_ready, eT_sb, e_ready, e_sb = (sem(n) for n in ("s_eT", "s_eT_sb", "s_e", "s_e_sb"))
        dh_ready, da_ready, g2_ready, g1_ready = (sem(n) for n in ("s_dh", "s_da", "s_g2", "s_g1"))
        w1_new, w2_new = sem("s_w1_new"), sem("s_w2_new")
        aq_ready, hqT_ready, out_ready, added = (sem(n) for n in ("s_aq", "s_hqT", "s_out", "s_added"))

        c_stats, c_mv = sb("c_stats", [TC, 2, 6]), sb("c_mv", [TC, 2, 2])
        c_var, c_rstd = sb("c_var", [TC, 2, 1]), sb("c_rstd", [TC, 2, 1])
        cn = sb("cn", [TC, 2, P])
        cT = sb("cT", [P, 2, 2, TC])
        c_pre_dve, c_pre_pool = sem("c_pre_dve"), sem("c_pre_pool")
        c_copied, c_turned, c_turned_sb, c_projected, c_projected_sb = (
            sem(n) for n in ("c_copied", "c_turned", "c_turned_sb", "c_projected", "c_projected_sb"))

        SCAN_LOADS = 10
        with nc.Block() as block:
            @block.sync
            def _(sp):
                def load(dst, src, s):
                    sp.dma_start(dst, src).then_inc(s, 16)
                ls = m["loaded_scan"]
                load(x[:, :, :], t["x"].rearrange("b p d -> p b d"), ls)
                load(m["sq"][:, :, :], t["squares"].rearrange("n p d -> p n d"), ls)
                load(w1T[:, :], t["scan_w1T"], ls)
                load(w2T[0:HID, :], t["scan_w2T"], ls)
                load(w2T[HID:HID + 1, :], t["rows"][ROWS.index("s_b2"):ROWS.index("s_b2") + 1, :], ls)
                load(w2[:, :], t["scan_w2"], ls)
                load(b1c[:, :], t["scan_b1"].rearrange("(p a) -> p a", a=1), ls)
                load(b1r[:, :], t["scan_b1"].rearrange("(a p) -> a p", a=1), ls)
                load(m["mask_sel"][:, :], t["mask_select"], ls)
                load(m["headsel"][:, :, :], t["head_select"], ls)
                lc = m["loaded_context"]
                load(c[:, :, :], t["ctx"].rearrange("b p d -> p b d"), lc)
                load(m["ctxT"][:, :, :], t["ctxT"], lc)
                load(m["cols"][:, :], t["cols"], lc)
                load(m["rows"][:, :, :], t["rows"].rearrange("(a n) d -> a n d", a=1), lc)
                lm = m["loaded_mask"]
                for q in range(2):
                    load(m[("mask_u8", "mask_i32")[q]][:, :, :], t[f"mask_{q}"].rearrange("(a b) s -> a b s", a=1).to_broadcast([P, NB, TC]), lm)
                lr = m["loaded_rest"]
                rest = [(m["alibi"][:, :, :], t["alibi"]),
                        (m["countdown"][:, :], t["countdown"])]
                for j in range(len(HALVES)):
                    for r in range(2):
                        rest.append((m["half"][:, j, :, :].rearrange("p (k r) d -> p k r d", r=2)[:, :, r, :],
                                     t["halves"][j].rearrange("p (k d) -> p k d", d=DH)))
                for q in range(2):
                    rest += [(m[f"w1_{q}"][:, :, :], t[f"w1_{q}"].rearrange("e p f -> p e f")),
                             (m[f"w2_{q}"][:, :, :, :], t[f"w2_{q}"].rearrange("e (k p) d -> p e k d", p=P)),
                             (m[f"b1_{q}"][:, :, :], t[f"b1_{q}"].rearrange("e (k p) -> p e k", p=P)),
                             (m[f"b2_{q}"][:, :], t[f"b2_{q}"]),
                             (m[f"wr_{q}"][:, :], t[f"wr_{q}"])]
                rest.append((m["br_0"][:, :], t["br_0"].rearrange("(a n) -> a n", a=1)))
                for dst, src in rest:
                    with nc.allow_non_contiguous_dma(reason="one-time weight load"):
                        load(dst, src, lr)
                m["n_rest"] = len(rest)

            @block.gpsimd
            def _(pool):
                n = 0
                for tile, value in ((m["half_power"][:, :], -0.5), (ones[:, :], 1.0), (m["ones_bf"][:, :], 1.0),
                                    (hT[HID:HID + 1, :], 1.0), (hqT[HID:HID + 1, :], 1.0), (h[:, HID:HID + 1], 1.0)):
                    nc.gpsimd.memset(tile, value).then_inc(set_pool, 1)
                    n += 1
                    pool.wait_ge(set_pool, n)

                def rstd_of(b, p):
                    pool.wait_ge(pre_dve, b * 3 + 2)
                    pass_waits(pool, m)
                    nc.gpsimd.tensor_scalar(var[:, p, :], mv[:, p, 1:2], EPS, None, ALU.add).then_inc(pre_pool, 1)
                    pool.wait_ge(pre_pool, b * 2 + 1)
                    nc.gpsimd.tensor_tensor(rstd[:, p, :], var[:, p, :], m["half_power"][:, 0:1], ALU.pow).then_inc(pre_pool, 1)

                def context_pre(b, p):
                    pool.wait_ge(c_pre_dve, b * 3 + 2)
                    pass_waits(pool, m)
                    nc.gpsimd.tensor_scalar(c_var[:, p, :], c_mv[:, p, 1:2], EPS, None, ALU.add).then_inc(c_pre_pool, 1)
                    pool.wait_ge(c_pre_pool, b * 2 + 1)
                    nc.gpsimd.tensor_tensor(c_rstd[:, p, :], c_var[:, p, :], m["half_power"][0:TC, 0:1], ALU.pow).then_inc(c_pre_pool, 1)
                    if not (isinstance(b, int) and b < 2):
                        pool.wait_ge(c_projected, b - 1)
                    pass_waits(pool, m)
                    nc.gpsimd.tensor_copy(cT[:, p, 1, :], m["ctxT"][:, bass.ds(b, 1), :].rearrange("p a k -> p (a k)")).then_inc(c_copied, 1)

                nc.gpsimd.memset(m["v_wide"][:, :, :, :], 0.0).then_inc(set_pool, 1)
                pool.wait_ge(set_pool, n + 1)
                pool.wait_ge(m["loaded_context"], 64)
                for b in range(2):
                    rstd_of(b, b)
                    context_pre(b, b)
                pool.wait_ge(m["loaded_mask"], 32)
                nc.gpsimd.tensor_scalar(m["mask_f"][:, :, :], m["mask_u8"][:, :, :], -1.0, 3e38, ALU.add, ALU.mult).then_inc(masks, 1)
                pool.wait_ge(masks, 1)
                nc.gpsimd.tensor_scalar(m["mask_0"][:, :, :], m["mask_f"][:, :, :], 3e38, None, ALU.mult).then_inc(masks, 1)
                with pool.Fori(0, (NB - 2) // 2) as i:
                    for u in range(2):
                        rstd_of(i * 2 + (u + 2), u)
                        context_pre(i * 2 + (u + 2), u)

            def scan(eng, pre, main, out_, last=None):
                pre(0, 0)
                main(0, 0, False)
                pre(1, 1)
                with eng.Fori(0, (NB - 2) // 2) as i:
                    for u in (1, 0):
                        s = i * 2 + (2 - u)
                        main(s, u, True)
                        pre(s + 1, 1 - u)
                main(NB - 1, 1, True)
                out_(NB - 1, 1)

            @block.vector
            def _(dve):
                dve.wait_ge(m["loaded_scan"], 16 * SCAN_LOADS)
                nc.vector.tensor_tensor(tkv[:, :], m["w"]("tk"), m["w"]("tv"), ALU.subtract).then_inc(set_dve, 1)
                nc.vector.tensor_copy(m["ident_bf"][:, :], eye).then_inc(set_dve, 1)
                dve.wait_ge(m["loaded_context"], 64)

                def pre(b, p):
                    s = Steps(dve, pre_dve, b, 3)
                    s.done(nc.vector.bn_stats(stats[:, p, :], x[:, bass.ds(b, 1), :].rearrange("p a d -> p (a d)")))
                    pass_waits(dve, m)
                    s.done(nc.vector.bn_aggr(mv[:, p, :], stats[:, p, :]))
                    dve.wait_ge(pre_pool, b * 2 + 2)
                    if not (isinstance(b, int) and b < 2):
                        dve.wait_ge(turned, b - 1)
                    s.done(nc.vector.tensor_scalar(xn[:, p, :], x[:, bass.ds(b, 1), :].rearrange("p a d -> p (a d)"),
                                                   mv[:, p, 0:1], rstd[:, p, 0:1], ALU.subtract, ALU.mult))
                    s.end()
                    s = Steps(dve, c_pre_dve, b, 3)
                    cb = c[:, bass.ds(b, 1), :].rearrange("k a d -> k (a d)")
                    s.done(nc.vector.bn_stats(c_stats[:, p, :], cb))
                    pass_waits(dve, m)
                    s.done(nc.vector.bn_aggr(c_mv[:, p, :], c_stats[:, p, :]))
                    dve.wait_ge(c_pre_pool, b * 2 + 2)
                    if not (isinstance(b, int) and b < 2):
                        dve.wait_ge(c_turned, b - 1)
                    s.done(nc.vector.tensor_scalar(cn[:, p, :], cb, c_mv[:, p, 0:1], c_rstd[:, p, 0:1],
                                                   ALU.subtract, ALU.mult))
                    s.end()

                def main(b, p, has_out):
                    s = Steps(dve, slope_dve, b, 9)
                    dve.wait_ge(a_ready, b + 1)
                    s.done(nc.vector.tensor_scalar(dn[:, 0, :], p_a[:, 0:HID], 0.0, 1e-12, ALU.is_equal, ALU.mult))
                    nc.vector.tensor_tensor(a[:, :], p_a[:, 0:HID], dn[:, 0, :], ALU.add).then_inc(a_safe, 1)
                    dve.wait_ge(a_safe, b + 1)
                    s.done(nc.vector.reciprocal(dn[:, 1, :], a[:, :]))
                    dve.wait_ge(eT_ready, b + 1)
                    wait(dve, dh_ready, b)
                    nc.vector.tensor_copy(eT[:, :], p_eT[:, 0:P]).then_inc(eT_sb, 1)
                    dve.wait_ge(th_ready, b + 1)
                    s.done(nc.vector.tensor_scalar(dn[:, 2, :], th[:, :], 1.0, None, ALU.add))
                    s.done(nc.vector.reciprocal(dn[:, 3, :], dn[:, 2, :]))
                    s.done(nc.vector.tensor_scalar(dn[:, 4, :], th[:, :], -DENSITY, DENSITY, ALU.mult, ALU.add))
                    s.done(nc.vector.tensor_tensor(dn[:, 4, :], dn[:, 4, :], dn[:, 3, :], ALU.mult))
                    s.done(nc.vector.tensor_tensor(dn[:, 4, :], dn[:, 4, :], a[:, :], ALU.mult))
                    dve.wait_ge(h_ready, b + 1)
                    s.done(nc.vector.tensor_tensor(dn[:, 0, :], h[:, 0:HID], dn[:, 1, :], ALU.mult))
                    s.done(nc.vector.tensor_tensor(slope[:, :], dn[:, 0, :], dn[:, 4, :], ALU.add))
                    s.end()
                    dve.wait_ge(dh_ready, b + 1)
                    wait(dve, g1_ready, b)
                    nc.vector.tensor_tensor(da[:, :], p_dh[:, 0:HID], slope[:, :], ALU.mult).then_inc(da_ready, 1)
                    if has_out:
                        out_(b - 1, 1 - p)
                    dve.wait_ge(g1_ready, b + 1)
                    for w_, g_ in ((w1T[:, :], g_w1T), (b1c[:, :], g_b1c), (b1r[:, :], g_b1r)):
                        nc.vector.scalar_tensor_tensor(w_, g_, -GRAD, w_, ALU.mult, ALU.add).then_inc(w1_new, 1)
                    for w_, g_ in ((w2T[:, :], g_w2T), (w2[:, :], g_w2)):
                        nc.vector.scalar_tensor_tensor(w_, g_, -GRAD, w_, ALU.mult, ALU.add).then_inc(w2_new, 1)

                def out_(b, p):
                    dve.wait_ge(out_ready, b + 1)
                    xb = x[:, bass.ds(b, 1), :].rearrange("p a d -> p (a d)")
                    nc.vector.tensor_tensor(xb, p_out[:, 0:P], xb, ALU.add).then_inc(added, 1)

                scan(dve, pre, main, out_)

            @block.scalar
            def _(act):
                act.wait_ge(m["loaded_scan"], 16 * SCAN_LOADS)
                act.wait_ge(m["loaded_context"], 64)
                act.wait_ge(set_pool, 7)

                def pre(b, p):
                    act.wait_ge(turned, b + 1)
                    if not (isinstance(b, int) and b < 2):
                        act.wait_ge(out_ready, b - 1)
                    nc.scalar.activation(xnT[:, p, :], p_pre[:, 0:P], ACT.Copy).then_inc(turned_sb, 1)
                    act.wait_ge(projected, b + 1)
                    if not (isinstance(b, int) and b < 2):
                        act.wait_ge(g1_ready, b - 1)
                        act.wait_ge(aq_ready, b - 1)
                    nc.scalar.activation(z[:, p, :], p_pre[:, 128:256], ACT.Copy).then_inc(projected_sb, 1)
                    nc.scalar.activation(zq[:, p, :], p_pre[:, 256:512], ACT.Copy).then_inc(projected_sb, 1)

                def main(b, p, has_out):
                    act.wait_ge(acts_ready, b + 1)
                    wait(act, e_ready, b)
                    nc.scalar.activation(hT[0:HID, :], p_aT[0:HID, 0:P], ACT.Gelu, bias=b1c[:, 0:1]).then_inc(hT_ready, 1)
                    act.wait_ge(a_safe, b + 1)
                    nc.scalar.activation(a2[:, :], a[:, :], ACT.Square, scale=0.5).then_inc(th_mid, 1)
                    wait(act, g2_ready, b)
                    nc.scalar.activation(h[:, 0:HID], a[:, :], ACT.Gelu).then_inc(h_ready, 1)
                    context_turned(b, p)
                    act.wait_ge(th_mid, b + 1)
                    nc.scalar.activation(th[:, :], a2[:, :], ACT.Tanh).then_inc(th_ready, 1)
                    act.wait_ge(e_ready, b + 1)
                    nc.scalar.activation(e[:, :], p_e[:, 0:P], ACT.Copy).then_inc(e_sb, 1)
                    if has_out:
                        out_(b - 1, 1 - p)
                    context_projected(b, p)

                def context_turned(b, p):
                    act.wait_ge(c_turned, b + 1)
                    if not (isinstance(b, int) and b < 2):
                        act.wait_ge(c_projected, b - 1)
                    nc.scalar.activation(cT[:, p, 0, :], pc_turned, ACT.Identity, bias=m["col"]("x0_b2"), scale=m["col"]("x0_g2")).then_inc(c_turned_sb, 1)

                def context_projected(b, p):
                    act.wait_ge(c_projected, b + 1)
                    ck = m["ctx_k"]
                    for q in range(2):
                        to = ck[:, q, bass.ds(b, 1), :].rearrange("p a k -> p (a k)")
                        src = pc_k[:, q * TC:(q + 1) * TC]
                        if q:
                            nc.scalar.activation(to, src, ACT.Identity, bias=m["col"]("x1_bk")).then_inc(c_projected_sb, 1)
                        else:
                            nc.scalar.activation(to, src, ACT.Copy).then_inc(c_projected_sb, 1)
                    nc.scalar.activation(m["ctx_v"][:, :, bass.ds(b, 1), :].rearrange("k q a d -> k q (a d)"),
                                         pc_v.rearrange("k (q d) -> k q d", q=2), ACT.Copy).then_inc(c_projected_sb, 1)

                def out_(b, p):
                    act.wait_ge(aq_ready, b + 1)
                    wait(act, out_ready, b)
                    nc.scalar.activation(hqT[0:HID, :], p_aT[0:HID, 128:256], ACT.Gelu, bias=b1c[:, 0:1]).then_inc(hqT_ready, 1)

                scan(act, pre, main, out_)

            @block.tensor
            def _(pe):
                pe.wait_ge(m["loaded_scan"], 16 * SCAN_LOADS)
                pe.wait_ge(m["loaded_context"], 64)
                pe.wait_ge(set_pool, 7)
                pe.wait_ge(set_dve, 2)
                mm = nc.tensor.matmul

                def pre(b, p):
                    pe.wait_ge(pre_dve, b * 3 + 3)
                    wait(pe, projected_sb, 2 * b)
                    nc.tensor.transpose(p_pre[:, 0:P], xn[:, p, :], eye).then_inc(turned, 1)
                    pe.wait_ge(turned_sb, b + 1)
                    mm(p_pre[:, 128:256], xnT[:, p, :], m["w"]("tk"), start=True, stop=True)
                    mm(p_pre[:, 256:384], m["w"]("tk"), xnT[:, p, :], start=True, stop=True)
                    mm(p_pre[:, 384:512], m["w"]("tq"), xnT[:, p, :], start=True, stop=True).then_inc(projected, 1)

                def main(b, p, has_out):
                    pe.wait_ge(projected_sb, 2 * b + 2)
                    wait(pe, w1_new, 3 * b)
                    mm(p_aT[0:HID, 0:P], w1T[:, :], zq[:, p, 0:P], start=True, stop=True).then_inc(acts_ready, 1)
                    wait(pe, a_safe, b)
                    mm(p_a[:, 0:HID], zq[:, p, 0:P], w1T[:, :], start=True, stop=False)
                    mm(p_a[:, 0:HID], ones[0:1, :], b1r[:, :], start=False, stop=True).then_inc(a_ready, 1)
                    context_turn(b, p)
                    wait(pe, eT_sb, b)
                    mm(p_eT[:, 0:P], tkv[:, :], xnT[:, p, :], start=True, stop=False)
                    pe.wait_ge(hT_ready, b + 1)
                    wait(pe, w2_new, 2 * b)
                    mm(p_eT[:, 0:P], w2T[:, :], hT[:, :], start=False, stop=True).then_inc(eT_ready, 1)
                    wait(pe, e_sb, b)
                    mm(p_e[:, 0:P], xnT[:, p, :], tkv[:, :], start=True, stop=False)
                    mm(p_e[:, 0:P], hT[:, :], w2T[:, :], start=False, stop=True).then_inc(e_ready, 1)
                    pe.wait_ge(eT_sb, b + 1)
                    wait(pe, da_ready, b)
                    mm(p_dh[:, 0:HID], eT[:, :], w2[:, :], start=True, stop=True).then_inc(dh_ready, 1)
                    if has_out:
                        out_(b - 1, 1 - p)
                    context_project(b, p)
                    pe.wait_ge(e_sb, b + 1)
                    pe.wait_ge(h_ready, b + 1)
                    mm(g_w2T, h[:, :], e[:, :], start=True, stop=True)
                    mm(g_w2, e[:, :], h[:, 0:HID], start=True, stop=True).then_inc(g2_ready, 1)
                    pe.wait_ge(da_ready, b + 1)
                    mm(g_b1c, da[:, :], ones[:, 0:1], start=True, stop=True)
                    mm(g_b1r, ones[:, 0:1], da[:, :], start=True, stop=True)
                    mm(g_w1T, z[:, p, :], da[:, :], start=True, stop=True).then_inc(g1_ready, 1)

                def context_turn(b, p):
                    pe.wait_ge(c_pre_dve, b * 3 + 3)
                    wait(pe, c_projected_sb, 3 * b)
                    nc.tensor.transpose(pc_turned, cn[:, p, :], m["eye"][0:TC, 0:TC]).then_inc(c_turned, 1)

                def context_project(b, p):
                    pe.wait_ge(c_copied, b + 1)
                    pe.wait_ge(c_turned_sb, b + 1)
                    for q in range(2):
                        mm(pc_k[:, q * TC:(q + 1) * TC], m["w"](f"x{q}_k"), cT[:, p, q, :], start=True, stop=True)
                        last = mm(pc_v[:, q * P:(q + 1) * P], cT[:, p, q, :], m["w"](f"x{q}_v"), start=True, stop=q == 0)
                    mm(pc_v[:, P:2 * P], ones[0:1, 0:TC], m["row"]("x1_v"), start=False, stop=True).then_inc(c_projected, 1)

                def out_(b, p):
                    pe.wait_ge(w1_new, 3 * b + 3)
                    pe.wait_ge(hT_ready, b + 1)
                    mm(p_aT[0:HID, 128:256], w1T[:, :], zq[:, p, P:2 * P], start=True, stop=True).then_inc(aq_ready, 1)
                    wait(pe, added, b)
                    mm(p_out[:, 0:P], xnT[:, p, :], m["w"]("tq"), start=True, stop=False)
                    pe.wait_ge(hqT_ready, b + 1)
                    pe.wait_ge(w2_new, 2 * b + 2)
                    mm(p_out[:, 0:P], hqT[:, :], w2T[:, :], start=False, stop=True).then_inc(out_ready, 1)

                scan(pe, pre, main, out_)


def attention(nc, m, name, T, mask, mask_rows, exp_scale, sel):
    x = m["x"]
    eye, ones, ones_bf = m["eye"], m["ones"], m["ones_bf"]
    own = name == "s1"
    GW = HG * T
    ctx = ExitStack()
    with ctx:
        def sb(n, shape, dt=F32):
            return ctx.enter_context(nc.sbuf_tensor(f"{name}_{n}", shape, dt))

        def sem(n):
            return ctx.enter_context(nc.semaphore(f"{name}_{n}"))

        stats = sb("stats", [P, 2, 6])
        mv = sb("mv", [P, 2, 2])
        var = sb("var", [P, 2, 1])
        rstd = sb("rstd", [P, 2, 1])
        xn = sb("xn", [P, 2, P])
        xT = sb("xT", [P, P])
        qT = sb("qT", [P, 2, NG, P])
        kT = sb("kT", [P, 2, HG, T])
        top = sb("top", [P, NH])
        prob = sb("prob", [P, 2, NH, T])
        pT = sb("pT", [P, NG, HG, P])
        total = sb("total", [P, NH])
        inv = sb("inv", [P, NH])
        inv_wide = sb("inv_wide", [P, NH, DH])
        invT = sb("invT", [P, P])
        oT = sb("oT", [P, P])
        v = m["v_wide"]
        if mask:
            m_fix = sb("m_fix", [P, 2, TC], BF16)

        p_s = ctx.enter_context(nc.psum_tensor(f"{name}_p_s", [P, NG, 512], F32))
        p_pT = ctx.enter_context(nc.psum_tensor(f"{name}_p_pT", [P, 2, 512], F32))
        p_in = ctx.enter_context(nc.psum_tensor(f"{name}_p_in", [P, 512], F32))
        p_o = ctx.enter_context(nc.psum_tensor(f"{name}_p_o", [P, 512], F32))
        scores = p_s[:, :, 0:GW].rearrange("p g (h k) -> p g h k", k=T)
        pi_x, pi_inv = p_in[:, 0:P], p_in[:, 3 * P:4 * P]
        pi_q, pi_k, pi_v = p_in[:, 0:P], p_in[:, P:2 * P], p_in[0:T, 2 * P:3 * P]
        po_mix, po_out = p_o[:, 0:P], p_o[:, P:2 * P]

        set_up = sem("set_up")
        counted, in_pool, normed = sem("counted"), sem("in_pool"), sem("normed")
        copied, turned, turned_sb, projected = sem("copied"), sem("turned"), sem("turned_sb"), sem("projected")
        inv_turned, inv_sb = sem("inv_turned"), sem("inv_sb")
        q_sb, k_sb, v_sb = sem("q_sb"), sem("k_sb"), sem("v_sb")
        scored, top_done, shifted, exped = sem("scored"), sem("top_done"), sem("shifted"), sem("exped")
        summed = sem("summed")
        p_turned, pT_sb, mixed = sem("p_turned"), sem("pT_sb"), sem("mixed")
        o_done, projected_o, res_done = sem("o_done"), sem("projected_o"), sem("res_done")

        def at(tile, b):
            return tile[:, bass.ds(b, 1), :].rearrange("p a d -> p (a d)")

        def diagonal(tile, p):
            return tile[0:T, p, :, :].rearrange("k h (g d) -> k (h g) d", d=DH)[:, 0:NH * NH:NH + 1, :]

        with nc.Block() as block:
            @block.gpsimd
            def _(pool):
                def rstd_of(b, p):
                    pool.wait_ge(counted, (b + 1) * 2)
                    pass_waits(pool, m)
                    nc.gpsimd.tensor_scalar(var[:, p, :], mv[:, p, 1:2], EPS, None, ALU.add).then_inc(in_pool, 1)
                    pool.wait_ge(in_pool, b * 2 + 1)
                    nc.gpsimd.tensor_tensor(rstd[:, p, :], var[:, p, :], m["half_power"][:, 0:1], ALU.pow).then_inc(in_pool, 1)

                def copy_mask(b, p):
                    if mask:
                        wait(pool, scored, b - 1)
                        pass_waits(pool, m)
                        nc.gpsimd.tensor_copy(m_fix[:, p, :], at(m[mask], b)).then_inc(copied, 1)

                def copy_v(b, p):
                    if not own:
                        wait(pool, mixed, b - 1)
                        pass_waits(pool, m)
                        nc.gpsimd.tensor_copy(diagonal(v, p), at(m[f"v_{name}"], b).rearrange("k (h d) -> k h d", d=DH)).then_inc(v_sb, 1)

                nc.gpsimd.memset(pT[:, :, :, :], 0.0).then_inc(set_up, 1)
                pool.wait_ge(set_up, 1)
                pool.wait_ge(m["loaded_rest"], 16 * m["n_rest"])
                staggered(pool, [(-1, rstd_of), (0, copy_mask), (1, copy_v)])

            @block.vector
            def _(dve):
                def count(b, p):
                    s = Steps(dve, counted, b, 2)
                    s.done(nc.vector.bn_stats(stats[:, p, :], at(x, b)))
                    pass_waits(dve, m)
                    s.done(nc.vector.bn_aggr(mv[:, p, :], stats[:, p, :]))
                    s.end()

                def normalise(b, p):
                    dve.wait_ge(in_pool, b * 2 + 2)
                    wait(dve, turned, b - 1)
                    nc.vector.tensor_scalar(xn[:, p, :], at(x, b), mv[:, p, 0:1], rstd[:, p, 0:1],
                                            ALU.subtract, ALU.mult).then_inc(normed, 1)

                def masked_k(b, p):
                    if own:
                        dve.wait_ge(projected, b + 1)
                        src = pi_k[:, 0:T]
                    else:
                        src = at(m[f"kT_{name}"], b)
                    wait(dve, scored, b - 1)
                    nc.vector.tensor_tensor(kT[:, p, :, :], src.unsqueeze(1).to_broadcast([P, HG, T]),
                                            m["headsel"][:, sel, :].unsqueeze(2).to_broadcast([P, HG, T]), ALU.mult).then_inc(k_sb, 1)

                def copy_q(b, p):
                    dve.wait_ge(projected, b + 1)
                    wait(dve, scored, b - 1)
                    to = qT[:, p, :, :]
                    src = pi_q.unsqueeze(1).to_broadcast([P, NG, P])
                    groups = m["headsel"][:, 2, :].unsqueeze(2).to_broadcast([P, NG, P])
                    if name == "x1":
                        nc.vector.scalar_tensor_tensor(to, src, m["col"]("x1_bq"), groups, ALU.add, ALU.mult).then_inc(q_sb, 1)
                    else:
                        nc.vector.tensor_tensor(to, src, groups, ALU.mult).then_inc(q_sb, 1)

                def copy_v(b, p):
                    if own:
                        dve.wait_ge(projected, b + 1)
                        wait(dve, mixed, b - 1)
                        nc.vector.tensor_copy(diagonal(v, p), pi_v.rearrange("k (h d) -> k h d", d=DH)).then_inc(v_sb, 1)

                def find_top(b, p):
                    dve.wait_ge(scored, b + 1)
                    nc.vector.tensor_reduce(top[:, :].rearrange("p (g h) -> p g h", h=HG), scores, AX.X, ALU.max).then_inc(top_done, 1)

                def shift(b, p):
                    dve.wait_ge(top_done, b + 1)
                    wait(dve, p_turned, NG * (b - 1))
                    nc.vector.tensor_tensor(prob[:, p, :, :].rearrange("p (g h) k -> p g h k", h=HG), scores,
                                            top[:, :].rearrange("p (g h) -> p g h", h=HG).unsqueeze(3).to_broadcast([P, NG, HG, T]),
                                            ALU.subtract).then_inc(shifted, 1)

                def sum_up(b, p):
                    dve.wait_ge(exped, b + 1)
                    s = Steps(dve, summed, b, 3)
                    s.done(nc.vector.tensor_reduce(total[:, :], prob[:, p, :, :], AX.X, ALU.add))
                    s.done(nc.vector.reciprocal(inv[:, :], total[:, :]))
                    wait(dve, inv_turned, b)
                    s.done(nc.vector.tensor_copy(inv_wide[:, :, :], inv[:, :].unsqueeze(2).to_broadcast([P, NH, DH])))
                    s.end()

                def scale_out(b, p):
                    dve.wait_ge(mixed, b + 1)
                    dve.wait_ge(inv_sb, b + 1)
                    wait(dve, projected_o, b)
                    nc.vector.tensor_tensor(oT[:, :], po_mix, invT[:, :], ALU.mult).then_inc(o_done, 1)

                def residual(b, p):
                    xb = at(x, b)
                    dve.wait_ge(projected_o, b + 1)
                    nc.vector.tensor_tensor(xb, po_out, xb, ALU.add).then_inc(res_done, 1)

                staggered(dve, [(3, scale_out), (2, sum_up), (-1, count), (3, residual), (1, find_top), (1, shift),
                                (-1, normalise), (0, masked_k), (0, copy_q), (0, copy_v)])

            @block.scalar
            def _(act):
                def turn_in(b, p):
                    act.wait_ge(turned, b + 1)
                    wait(act, inv_turned, b - 1)
                    wait(act, projected, b)
                    if name == "x0":
                        nc.scalar.activation(xT[:, :], pi_x, ACT.Identity, bias=m["col"]("x0_b1"), scale=m["col"]("x0_g1")).then_inc(turned_sb, 1)
                    else:
                        nc.scalar.activation(xT[:, :], pi_x, ACT.Copy).then_inc(turned_sb, 1)

                def turn_inv(b, p):
                    act.wait_ge(inv_turned, b + 1)
                    wait(act, o_done, b)
                    nc.scalar.activation(invT[:, :], pi_inv, ACT.Copy).then_inc(inv_sb, 1)

                def exps(b, p):
                    act.wait_ge(shifted, b + 1)
                    pr = prob[:, p, :, :].rearrange("p h k -> p (h k)")
                    nc.scalar.activation(pr, pr, ACT.Exp, scale=exp_scale).then_inc(exped, 1)

                def copy_pT(groups):
                    def run(b, p):
                        for g in groups:
                            act.wait_ge(p_turned, NG * b + g + 1)
                            wait(act, mixed, b)
                            nc.scalar.activation(pT[0:T, g, :, :].rearrange("k h q -> k (h q)"), p_pT[0:T, g % 2, :], ACT.Copy).then_inc(pT_sb, 1)
                    return run

                act.wait_ge(set_up, 1)
                staggered(act, [(2, copy_pT((0, 1, 2))), (0, turn_in), (2, turn_inv), (2, copy_pT((3,))), (1, exps)])

            @block.tensor
            def _(pe):
                mm = nc.tensor.matmul

                def bank_read(n):
                    if isinstance(n, int):
                        n = min(n, NB)
                    for s in (q_sb, k_sb, v_sb) if own else (q_sb,):
                        wait(pe, s, n)

                def turn_in(b, p):
                    pe.wait_ge(normed, b + 1)
                    bank_read(b)
                    nc.tensor.transpose(pi_x, xn[:, p, :], eye).then_inc(turned, 1)

                def turn_inv(b, p):
                    pe.wait_ge(summed, 3 * b + 3)
                    bank_read(b + 2)
                    nc.tensor.transpose(pi_inv, inv_wide[:, :, :].rearrange("p h d -> p (h d)"), eye).then_inc(inv_turned, 1)

                def project(b, p):
                    pe.wait_ge(turned_sb, b + 1)
                    wait(pe, inv_sb, b - 1)
                    last = mm(pi_q, m["w"](name + "_q"), xT[:, :], start=True, stop=True)
                    if own:
                        wk, wv = (m["half"][:, j, :, :].rearrange("p h d -> p (h d)") for j in range(2))
                        mm(pi_k[:, 0:T], wk, xT[:, :], start=True, stop=True)
                        last = mm(pi_v, xT[:, :], wv, start=True, stop=True)
                    last.then_inc(projected, 1)

                def score(groups):
                    def run(b, p):
                        if groups[0] == 0:
                            pe.wait_ge(q_sb, b + 1)
                            pe.wait_ge(k_sb, b + 1)
                            wait(pe, shifted, b)
                            if mask:
                                pe.wait_ge(copied, b + 1)
                        for g in groups:
                            to = p_s[:, g, 0:GW]
                            if mask:
                                r = slice(R * g, R * g + mask_rows)
                                mm(to.rearrange("p (h k) -> p h k", k=T), ones_bf[r, :],
                                   m_fix[r, p, :].unsqueeze(1).to_broadcast([mask_rows, HG, T]), start=True, stop=False)
                            else:
                                mm(to, m["ident_bf"][:, :], m["alibi"][:, HG * g:HG * (g + 1), :].rearrange("p h k -> p (h k)"),
                                   start=True, stop=False)
                            last = mm(to, qT[:, p, g, :], kT[:, p, :, :].rearrange("p h k -> p (h k)"), start=False, stop=True)
                        if groups[-1] == NG - 1:
                            last.then_inc(scored, 1)
                    return run

                def turn_p(groups):
                    def run(b, p):
                        pe.wait_ge(exped, b + 1)
                        for g in groups:
                            wait(pe, pT_sb, NG * b + g - 1)
                            for h in range(HG):
                                last = nc.tensor.transpose(p_pT[0:T, g % 2, h * P:(h + 1) * P], prob[:, p, HG * g + h, :], eye)
                            last.then_inc(p_turned, 1)
                    return run

                def mix(g):
                    def run(b, p):
                        if g == 0:
                            wait(pe, res_done, b)
                            pe.wait_ge(v_sb, b + 1)
                        pe.wait_ge(pT_sb, NG * b + g + 1)
                        for h in range(HG * g, HG * (g + 1)):
                            last = mm(po_mix, v[:, p, h, :], pT[:, g, h % HG, :], start=h == 0, stop=h == NH - 1)
                        if g == NG - 1:
                            last.then_inc(mixed, 1)
                    return run

                def project_o(b, p):
                    pe.wait_ge(o_done, b + 1)
                    if name == "x1":
                        mm(po_out, oT[:, :], eye, start=True, stop=True).then_inc(projected_o, 1)
                    else:
                        mm(po_out, oT[:, :], m["w"](name + "_o"), start=True, stop=False)
                        mm(po_out, ones[0:1, :], m["row"](name + "_o"), start=False, stop=True).then_inc(projected_o, 1)

                staggered(pe, [(2, turn_p((0, 1))), (1, score((0, 1))), (3, project_o), (1, score((2, 3))), (2, mix(0)),
                               (2, turn_p((2,))), (0, turn_in), (2, turn_inv), (2, mix(1)), (2, turn_p((3,))), (2, mix(2)),
                               (0, project), (2, mix(3))])


def mask_parts(nc, pool, m, masks):
    g = nc.gpsimd
    s = Steps(pool, masks, 0, 11)
    f, hi, part, mask = (m[k][:, :, :] for k in ("mask_f", "mask_hi", "mask_part", "mask_1"))
    s.done(g.tensor_scalar(f, m["mask_i32"][:, :, :], -1.0, 10000.0, ALU.add, ALU.mult))
    s.done(g.tensor_copy(hi, f))
    s.done(g.tensor_scalar(mask, hi, m["mask_sel"][:, 0:1], None, ALU.mult))
    for r in (1, 2):
        s.done(g.tensor_tensor(f, f, hi, ALU.subtract))
        s.done(g.tensor_copy(hi, f))
        s.done(g.tensor_scalar(part, hi, m["mask_sel"][:, r:r + 1], None, ALU.mult))
        s.done(g.tensor_tensor(mask, mask, part, ALU.add))
    s.end()


def experts(nc, m, q, out):
    x, eye, ones = m["x"], m["eye"], m["ones"]
    GT = 4
    w1, w2, b1, b2, wr = (m[f"{k}_{q}"] for k in ("w1", "w2", "b1", "b2", "wr"))
    ctx = ExitStack()
    with ctx:
        def sb(n, shape, dt=F32):
            return ctx.enter_context(nc.sbuf_tensor(f"f{q}_{n}", shape, dt))

        def sem(n):
            return ctx.enter_context(nc.semaphore(f"f{q}_{n}"))

        def ps(n, shape, c):
            return c.enter_context(nc.psum_tensor(f"f{q}_{n}", shape, F32))

        def at(tile, b):
            return tile[:, bass.ds(b, 1), :].rearrange("p a d -> p (a d)")

        stats = sb("stats", [P, 2, 6])
        mv = sb("mv", [P, 2, 2])
        var = sb("var", [P, 2, 1])
        rstd = sb("rstd", [P, 2, 1])
        xn = sb("xn", [P, 2, P])
        xT = sb("xT", [P, 2, P])
        xTs = sb("xTs", [P, NB, P])
        lg = sb("lg", [P, NB, NE])
        best = sb("best", [P, 2, NB])
        where = sb("where", [P, 2, NB])
        gap = sb("gap", [P, NB])
        egap = sb("egap", [P, NB])
        den = sb("den", [P, NB])
        inv = sb("inv", [P, NB])
        one_hot = sb("one_hot", [P, 2, NB, NE])
        wts = sb("wts", [P, NB, NE])
        wT = sb("wT", [NE, NB, P])
        hT = sb("hT", [P, 2, FC, GT * P])

        counted, in_pool, in_dve = sem("counted"), sem("in_pool"), sem("in_dve")
        turned, turned_sb, routed, gap_ready = sem("turned"), sem("turned_sb"), sem("routed"), sem("gap_ready")
        router_dve, router_act = sem("router_dve"), sem("router_act")
        w_turned, w_sb, b2_ready, b2_added = sem("w_turned"), sem("w_sb"), sem("b2_ready"), sem("b2_added")
        masks = sem("masks")
        h_ready, h_sb, y_ready, combined = sem("h_ready"), sem("h_sb"), sem("y_ready"), sem("combined")

        with ExitStack() as pctx:
            p_t = ps("p_t", [P, 2, 512], pctx)
            p_l = ps("p_l", [P, 512], pctx)
            p_w = ps("p_w", [P, 4, 512], pctx)
            with nc.Block() as block:
                @block.gpsimd
                def _(pool):
                    def rstd_of(b, p):
                        pool.wait_ge(counted, (b + 1) * 2)
                        pass_waits(pool, m)
                        nc.gpsimd.tensor_scalar(var[:, p, :], mv[:, p, 1:2], EPS, None, ALU.add).then_inc(in_pool, 1)
                        pool.wait_ge(in_pool, b * 2 + 1)
                        nc.gpsimd.tensor_tensor(rstd[:, p, :], var[:, p, :], m["half_power"][:, 0:1], ALU.pow).then_inc(in_pool, 1)
                    staggered(pool, [(0, rstd_of)])

                @block.vector
                def _(dve):
                    def count(b, p):
                        s = Steps(dve, counted, b, 2)
                        s.done(nc.vector.bn_stats(stats[:, p, :], at(x, b)))
                        pass_waits(dve, m)
                        s.done(nc.vector.bn_aggr(mv[:, p, :], stats[:, p, :]))
                        s.end()

                    def normalise(b, p):
                        dve.wait_ge(in_pool, b * 2 + 2)
                        wait(dve, turned, b - 1)
                        nc.vector.tensor_scalar(xn[:, p, :], at(x, b), mv[:, p, 0:1], rstd[:, p, 0:1],
                                                ALU.subtract, ALU.mult).then_inc(in_dve, 1)

                    staggered(dve, [(0, count), (0, normalise)])
                    s = Steps(dve, router_dve, 0, 17)
                    dve.wait_ge(routed, NB)
                    logits = p_l[:, 0:NB * NE].rearrange("p (b e) -> p b e", e=NE)
                    s.done(nc.vector.tensor_copy(lg[:, :, :], logits))
                    for j in range(2):
                        hot = one_hot[:, j, :, :]
                        s.done(nc.vector.tensor_reduce(best[:, j, :], lg[:, :, :], AX.X, ALU.max))
                        s.done(nc.vector.tensor_tensor(hot, lg[:, :, :], best[:, j, :].unsqueeze(2).to_broadcast([P, NB, NE]), ALU.is_equal))
                        countdown = m["countdown"][:, :].unsqueeze(1).to_broadcast([P, NB, NE])
                        s.done(nc.vector.tensor_tensor(hot, hot, countdown, ALU.mult))
                        s.done(nc.vector.tensor_reduce(where[:, j, :], hot, AX.X, ALU.max))
                        s.done(nc.vector.tensor_tensor(hot, countdown, where[:, j, :].unsqueeze(2).to_broadcast([P, NB, NE]), ALU.is_equal))
                        if j == 0:
                            s.done(nc.vector.scalar_tensor_tensor(lg[:, :, :], hot, -3e38, lg[:, :, :], ALU.mult, ALU.add))
                    nc.vector.tensor_tensor(gap[:, :], best[:, 1, :], best[:, 0, :], ALU.subtract).then_inc(gap_ready, 1)
                    dve.wait_ge(router_act, 1)
                    s.done(nc.vector.tensor_scalar(den[:, :], egap[:, :], 1.0, None, ALU.add))
                    s.done(nc.vector.reciprocal(inv[:, :], den[:, :]))
                    s.done(nc.vector.tensor_tensor(one_hot[:, 1, :, :], one_hot[:, 1, :, :],
                                                   egap[:, :].unsqueeze(2).to_broadcast([P, NB, NE]), ALU.mult))
                    s.done(nc.vector.tensor_tensor(one_hot[:, 0, :, :], one_hot[:, 0, :, :], one_hot[:, 1, :, :], ALU.add))
                    s.done(nc.vector.tensor_tensor(wts[:, :, :], one_hot[:, 0, :, :],
                                                   inv[:, :].unsqueeze(2).to_broadcast([P, NB, NE]), ALU.mult))
                    s.end()
                    for g in range(4):
                        dve.wait_ge(w_turned, g + 1)
                        nc.vector.tensor_copy(wT[:, 4 * g:4 * g + 4, :].rearrange("e b t -> e (b t)"), p_w[0:NE, g, :]).then_inc(w_sb, 1)
                    for g in range(4):
                        dve.wait_ge(b2_ready, g + 1)
                        xg = x[:, 4 * g:4 * g + 4, :].rearrange("p b d -> p (b d)")
                        nc.vector.tensor_tensor(xg, p_w[:, g, :], xg, ALU.add).then_inc(b2_added, 1)

                @block.scalar
                def _(act):
                    def turn_in(b, p):
                        act.wait_ge(turned, b + 1)
                        wait(act, routed, b - 1)
                        nc.scalar.activation(xT[:, p, :], p_t[:, p, 0:P], ACT.Copy).then_inc(turned_sb, 1)
                        nc.scalar.activation(at(xTs, b), p_t[:, p, 0:P], ACT.Copy).then_inc(turned_sb, 1)
                    staggered(act, [(0, turn_in)])
                    act.wait_ge(gap_ready, 1)
                    nc.scalar.activation(egap[:, :], gap[:, :], ACT.Exp).then_inc(router_act, 1)

                @block.tensor
                def _(pe):
                    mm = nc.tensor.matmul

                    def turn_in(b, p):
                        pe.wait_ge(in_dve, b + 1)
                        wait(pe, turned_sb, 2 * (b - 1))
                        nc.tensor.transpose(p_t[:, p, 0:P], xn[:, p, :], eye).then_inc(turned, 1)

                    def route(b, p):
                        pe.wait_ge(turned_sb, 2 * (b + 1))
                        to = p_l[:, bass.ds(b * NE, NE)]
                        last = mm(to, xT[:, p, :], wr[:, :], start=True, stop=q == 1)
                        if q == 0:
                            last = mm(to, ones[0:1, :], m["br_0"][:, :], start=False, stop=True)
                        last.then_inc(routed, 1)

                    staggered(pe, [(0, turn_in), (1, route)])
                    pe.wait_ge(router_dve, 17)
                    for g in range(4):
                        for j in range(4):
                            last = nc.tensor.transpose(p_w[0:NE, g, P * j:P * j + P], wts[:, 4 * g + j, :], eye)
                        last.then_inc(w_turned, 1)
                    for g in range(4):
                        pe.wait_ge(w_sb, g + 1)
                        for j in range(4):
                            last = mm(p_w[:, g, P * j:P * j + P], wT[:, 4 * g + j, :], b2[:, :], start=True, stop=True)
                        last.then_inc(b2_ready, 1)

        with ExitStack() as pctx:
            p_h = ps("p_h", [P, FC, 512], pctx)
            p_y = ps("p_y", [P, 2, 512], pctx)
            with nc.Block() as block:
                def groups(eng, run):
                    run(0)
                    with eng.Fori(1, NB // GT) as g:
                        run(g)

                @block.tensor
                def _(pe):
                    mm = nc.tensor.matmul

                    def run(g):
                        def up(e):
                            n = g * NE + e
                            for k in range(FC):
                                wait(pe, h_sb, FC * (n - 1) + k + 1)
                                mm(p_h[:, k, :], w1[:, e, P * k:P * k + P],
                                   xTs[:, bass.ds(g * GT, GT), :].rearrange("p b t -> p (b t)"),
                                   start=True, stop=True).then_inc(h_ready, 1)

                        def down(e):
                            n = g * NE + e
                            wait(pe, combined, GT * (n - 1))
                            pe.wait_ge(h_sb, FC * n + FC)
                            for j in range(GT):
                                for k in range(FC):
                                    last = mm(p_y[:, e % 2, P * j:P * j + P], hT[:, e % 2, k, P * j:P * j + P],
                                              w2[:, e, k, :], start=k == 0, stop=k == FC - 1)
                            last.then_inc(y_ready, 1)
                        up(0)
                        for e in range(1, NE):
                            up(e)
                            down(e - 1)
                        down(NE - 1)
                    groups(pe, run)

                @block.scalar
                def _(act):
                    def run(g):
                        for e in range(NE):
                            n = g * NE + e
                            wait(act, y_ready, n - 1)
                            for k in range(FC):
                                act.wait_ge(h_ready, FC * n + k + 1)
                                nc.scalar.activation(hT[:, e % 2, k, :], p_h[:, k, :], ACT.Relu,
                                                     bias=b1[:, e, k:k + 1]).then_inc(h_sb, 1)
                    groups(act, run)

                @block.vector
                def _(dve):
                    def run(g):
                        for e in range(NE):
                            n = g * NE + e
                            dve.wait_ge(y_ready, n + 1)
                            wait(dve, combined, GT * n)
                            for j in range(GT):
                                xb = at(x, g * GT + j)
                                nc.vector.scalar_tensor_tensor(xb, p_y[:, e % 2, P * j:P * j + P],
                                                               wts[:, bass.ds(g * GT + j, 1), e:e + 1].rearrange("p a b -> p (a b)"),
                                                               xb, ALU.mult, ALU.add).then_inc(combined, 1)
                    groups(dve, run)

                @block.gpsimd
                def _(pool):
                    if q == 0:
                        mask_parts(nc, pool, m, masks)

                @block.sync
                def _(sp):
                    if out is not None:
                        for g in range(NB // GT):
                            sp.wait_ge(combined, GT * NE * (g + 1))
                            sp.dma_start(out[GT * g:GT * (g + 1)].rearrange("b p d -> p b d"),
                                         x[:, GT * g:GT * (g + 1), :]).then_inc(m["stored"], 16)
                        sp.wait_ge(m["stored"], 16 * (NB // GT))


def kernel(**inputs):
    import numpy as np
    import concourse.bacc as bacc
    from concourse import mybir as mb
    from concourse.bass_utils import run_bass_kernel_spmd
    import ml_dtypes

    a = {k: np.asarray(v) for k, v in inputs.items()}
    T = lambda w: np.ascontiguousarray(np.swapaxes(w, -1, -2))
    squares = {"ident": np.eye(P, dtype=np.float32),
               "tk": T(a["L0_attn_t_k"]), "tv": T(a["L0_attn_t_v"]), "tq": T(a["L0_attn_t_q"]),
               "x0_q": T(a["L0_xattn_Wq"]), "x0_k": T(a["L0_xattn_Wk"]), "x0_v": T(a["L0_xattn_Wv"]),
               "x0_o": T(a["L0_xattn_Wo"]), "s1_q": T(a["L1_attn_Wq"]), "s1_o": T(a["L1_attn_Wo"]),
               "x1_q": T(a["L1_xattn_Wq"]), "x1_k": T(a["L1_xattn_Wk"]), "x1_v": T(a["L1_xattn_Wv"])}
    head = np.arange(P) // DH
    select = (head[:, None] % HG == np.arange(HG)[None, :]).astype(np.float32)
    group = (head[:, None] // HG == np.arange(NG)[None, :]).astype(np.float32)
    slopes = 2.0 ** -(np.arange(NH) + 1.0)
    dist = np.abs(np.arange(P)[:, None] - np.arange(P)[None, :])
    t = {
        "x": a["x"], "ctx": a["ctx_1024"],
        "ctxT": np.ascontiguousarray(a["ctx_1024"].transpose(2, 0, 1)),
        "squares": np.stack([squares[k] for k in SQUARES]),
        "halves": np.stack([T(a["L1_attn_Wk"]), T(a["L1_attn_Wv"])]),
        "cols": np.stack([a[k] for k in ("L0_xattn_g1", "L0_xattn_b1", "L0_xattn_g2", "L0_xattn_b2",
                                         "L1_xattn_bq", "L1_xattn_bk")], axis=1),
        "rows": np.stack([a[k] for k in ("L0_xattn_bo", "L1_attn_bo", "L1_xattn_bv", "L0_attn_b2")]),
        "scan_w1T": T(a["L0_attn_W1"]), "scan_w2T": T(a["L0_attn_W2"]), "scan_w2": a["L0_attn_W2"],
        "scan_b1": a["L0_attn_b1"],
        "mask_0": a["mask_BxS2_bf1"].view(np.uint8), "mask_1": a["mask_BxS2_ik0"],
        "mask_select": (np.arange(P)[:, None] % R == np.arange(3)[None, :]).astype(np.float32),
        "head_select": np.stack([select, select / np.float32(SQRT_DH), group], axis=1).astype(np.float32),
        "alibi": (-dist[:, None, :] * slopes[None, :, None]).astype(ml_dtypes.bfloat16),
        "countdown": np.tile(np.arange(NE, 0, -1, dtype=np.float32), (P, 1)),
        "w1_0": a["L0_ffn_W1"], "w2_0": a["L0_ffn_W2"], "b1_0": a["L0_ffn_b1"], "b2_0": a["L0_ffn_b2"],
        "wr_0": a["L0_ffn_W_router"], "br_0": a["L0_ffn_b_router"],
        "w1_1": T(a["L1_ffn_w1"]), "w2_1": T(a["L1_ffn_w2"]), "b1_1": a["L1_ffn_b1"], "b2_1": a["L1_ffn_b2"],
        "wr_1": T(a["L1_ffn_gate_w"]),
    }
    nc = bacc.Bacc("TRN2", target_bir_lowering=False, num_devices=1)
    arrays, aps = {}, {}
    for name, v in t.items():
        v = np.ascontiguousarray(v)
        arrays[f"in_{name}"] = v
        aps[name] = nc.dram_tensor(f"in_{name}", v.shape, mb.dt.from_np(v.dtype), kind="ExternalInput").ap()
    out = nc.dram_tensor("out", (NB, P, P), F32, kind="ExternalOutput").ap()
    build(nc, aps, out)
    r = run_bass_kernel_spmd(nc, [arrays], core_ids=[0])
    return r.results[0]["out"]
```

```python
import concourse.bass as bass
from concourse import mybir
from contextlib import ExitStack, contextmanager

F32 = mybir.dt.float32
F32R = mybir.dt.float32r
BF16 = mybir.dt.bfloat16
I32 = mybir.dt.int32
U8 = mybir.dt.uint8
ALU = mybir.AluOpType
ACT = mybir.ActivationFunctionType
AX = mybir.AxisListType

NB = 16
P = 128
TC = 77
NH = 16
DH = P // NH
NG = 4
HG = NH // NG
KM, KR = P // 2, P // 8
KL = TC - KM
HID = 32
NE = 8
FF = 512
FC = FF // P
CONTEXT_LOADS = 5
SCAN_LOADS = 6
EPS = 1e-5
LR = 0.001
GRAD = LR * 2.0 / (P * P)
SQRT_DH = float(DH) ** 0.5
DENSITY = 0.3989422804014327

SQUARES = ["ident", "tk", "tv", "tq",
           "x0_q", "x0_k", "x0_v", "x0_o", "s1_q", "s1_o", "x1_q", "x1_k", "x1_v"]
HALVES = ["s1_k", "s1_v"]
COLS = ["x0_g1", "x0_b1", "x0_g2", "x0_b2", "x1_bq", "x1_bk"]
ROWS = ["x0_o", "s1_o", "x1_v", "s_b2"]


def wait(eng, sem, value):
    if isinstance(value, int) and value <= 0:
        return
    eng.wait_ge(sem, value)


def pass_waits(eng, m):
    eng.sem_inc(m["passed"], 1)


class Steps:

    def __init__(self, eng, sem, b, per):
        self.eng, self.sem, self.base, self.per, self.n = eng, sem, b * per, per, 0

    def done(self, ins):
        self.n += 1
        assert self.n <= self.per
        ins.then_inc(self.sem, 1)
        self.eng.wait_ge(self.sem, self.base + self.n)

    def end(self):
        assert self.n == self.per, (self.n, self.per)


def staggered(eng, stages, first=6):
    lags = [lag for lag, _ in stages]
    last = NB + min(min(lags), 0) // 2 * 2

    def peeled(k):
        for lag, stage in stages:
            if 0 <= k - lag < NB:
                stage(k - lag, (k - lag) % 2)
    for k in range(min(lags), first):
        peeled(k)
    with eng.Fori(0, (last - first) // 2) as i:
        for u in range(2):
            for lag, stage in stages:
                stage(i * 2 + (first + u - lag), (first + u - lag) % 2)
    for k in range(last, NB + max(lags)):
        peeled(k)


def build(nc, t, out):
    ctx = ExitStack()
    with ctx:
        def sb(name, shape, dt=F32):
            return ctx.enter_context(nc.sbuf_tensor(name, shape, dt))

        def sem(name):
            return ctx.enter_context(nc.semaphore(name))

        x = sb("x", [P, NB, P])
        sq = sb("sq", [P, len(SQUARES), P])
        half = sb("half", [P, len(HALVES), NH, DH])
        cols = sb("cols", [P, len(COLS)])
        ones = sb("ones", [P, P])
        ones_bf = sb("ones_bf", [P, P], BF16)
        ident_bf = sb("ident_bf", [P, P], BF16)
        half_power = sb("half_power", [P, 4])
        headsel = sb("headsel", [P, 3, HG])
        alibi = sb("alibi", [P, NH, P], BF16)
        m = dict(x=x, sq=sq, half=half, cols=cols, ones=ones, ones_bf=ones_bf,
                 ident_bf=ident_bf, half_power=half_power, headsel=headsel, alibi=alibi)
        m["eye"] = sq[:, SQUARES.index("ident"), :]
        ctx_k = sb("ctx_k", [P, 2, NB, TC])
        ctx_v = sb("ctx_v", [P, 2, NB, P])
        ctx_vr = sb("ctx_vr", [P, 2, NB, P])
        keep_v = sb("keep_v", [P, 2 * DH])
        keep_vr = sb("keep_vr", [P, 8 * DH])
        m["x1_bv"] = sb("x1_bv", [P, P])
        m["bo_x0"], m["bo_s1"] = sb("bo_x0", [P, P]), sb("bo_s1", [P, P])
        m.update(ctx_k=ctx_k, ctx_v=ctx_v, ctx_vr=ctx_vr, keep_v=keep_v, keep_vr=keep_vr)
        for q in (0, 1):
            m[f"kT_x{q}"], m[f"v_x{q}"], m[f"vr_x{q}"] = ctx_k[:, q, :, :], ctx_v[:, q, :, :], ctx_vr[:, q, :, :]
        m["w"] = lambda name: sq[:, SQUARES.index(name), :]
        m["col"] = lambda name: cols[:, COLS.index(name):COLS.index(name) + 1]
        for q in (0, 1):
            m[f"b1_{q}"] = sb(f"b1_{q}", [P, NE, FC])
            m[f"b2_{q}"] = sb(f"b2_{q}", [P, NE])
            m[f"wr_{q}"] = sb(f"wr_{q}", [P, NE])
        m["br_0"] = sb("br_0", [P, NE])
        m["scan_w1T"] = sb("scan_w1T", [P, HID])
        m["scan_w2T"] = sb("scan_w2T", [HID + 1, P])
        m["scan_w2"] = sb("scan_w2", [P, HID])
        m["scan_b1c"] = sb("scan_b1c", [HID, 1])
        m["scan_b1r"] = sb("scan_b1r", [1, HID])
        m["mask_0"] = sb("mask_0", [3, NB, TC], BF16)
        m["mask_1"] = sb("mask_1", [3, NB, TC], BF16)
        m["countdown"] = sb("countdown", [P, NE])

        loaded_scan = sem("loaded_scan")
        loaded_mask = sem("loaded_mask")
        masks_placed = sem("masks_placed")
        loaded_context = sem("loaded_context")
        loaded_rest = sem("loaded_rest")
        stored = sem("stored")
        m.update(masks_placed=masks_placed, loaded_scan=loaded_scan, loaded_mask=loaded_mask,
                 loaded_context=loaded_context, loaded_rest=loaded_rest, stored=stored)
        m["passed"] = sem("passed")
        load_and_scan(nc, t, m)
        with split_weights(nc, m, 0):
            attention(nc, m, "x0", TC, mask="mask_0", mask_rows=1, exp_scale=1.0, sel=1, experts_of=t, q=0)
            experts(nc, m, 0, None)
        attention(nc, m, "s1", P, mask=None, mask_rows=0, exp_scale=1.0 / SQRT_DH, sel=0)
        with split_weights(nc, m, 1):
            attention(nc, m, "x1", TC, mask="mask_1", mask_rows=3, exp_scale=1.0, sel=1, experts_of=t, q=1)
            experts(nc, m, 1, out)


@contextmanager
def split_weights(nc, m, q):
    with nc.sbuf_tensor(f"w_hi_{q}", [P, 2 * NE, FF], F32R) as hi, nc.sbuf_tensor(f"w_lo_{q}", [P, 2 * NE, FF], F32R) as lo:
        m.update(w_hi=hi, w_lo=lo)
        yield


def load_and_scan(nc, t, m):
    x = m["x"]
    eye, ones = m["eye"], m["ones"]
    GS = 4
    ctx = ExitStack()
    with ctx:
        def sb(name, shape, dt=F32):
            return ctx.enter_context(nc.sbuf_tensor(name, shape, dt))

        def ps(name, c):
            return c.enter_context(nc.psum_tensor(name, [P, 512], F32))

        sems = []

        def sem(name):
            sems.append(nc.alloc_semaphore(name=name))
            return sems[-1]

        def flat(tile, g):
            return tile[:, GS * g:GS * (g + 1), :].rearrange("p b d -> p (b d)")

        w1T, w2T, w2, b1c, b1r = (m[k] for k in ("scan_w1T", "scan_w2T", "scan_w2", "scan_b1c", "scan_b1r"))
        tkv = sb("tkv", [P, P])
        stats = sb("stats", [P, GS, 6])
        mv = sb("mv", [P, NB, 2])
        var = sb("var", [P, NB])
        rstd = sb("rstd", [P, NB])
        z = sb("z", [P, NB, P])
        zT = sb("zT", [P, NB, P])
        qT = sb("qT", [P, NB, P])
        e0T = sb("e0T", [P, NB, P])

        set_pool, set_dve = sem("scan_set_pool"), sem("scan_set_dve")
        masks = sem("scan_masks")
        loaded_x = [sem(f"loaded_x{g}") for g in range(NB // GS)]
        loaded_squares = sem("loaded_squares")
        last_zero = sem("last_zero")
        first_ordered = [sem("first_ordered_0"), sem("first_ordered_1")]
        last_ordered = [sem("last_ordered_0"), sem("last_ordered_1")]
        counted, centred, rstd_ready, normed = sem("s_counted"), sem("s_centred"), sem("s_rstd"), sem("s_normed")
        turned, xnT_sb = sem("s_turned"), sem("s_xnT_sb")
        zT_ready, zT_sb, qT_ready, qT_sb = sem("s_zT"), sem("s_zT_sb"), sem("s_qT"), sem("s_qT_sb")
        e0T_ready, e0T_sb, z_ready, z_sb = sem("s_e0T"), sem("s_e0T_sb"), sem("s_z"), sem("s_z_sb")
        q_ready, q_added = sem("s_q"), sem("s_q_added")
        c_counted, c_centred, c_rstd_ready, c_normed = (
            sem(n) for n in ("c_counted", "c_centred", "c_rstd_ready", "c_normed"))
        c_turned, cT_sb, k_ready, k_sb, v0_ready, v0_sb, v1_ready, v1_sb = (
            sem(n) for n in ("c_turned", "c_cT_sb", "c_k", "c_k_sb", "c_v0", "c_v0_sb", "c_v1", "c_v1_sb"))

        with ExitStack() as pctx:
            def csb(name, shape):
                return pctx.enter_context(nc.sbuf_tensor(name, shape, F32))

            c_stats, c_mv = csb("c_stats", [TC, GS, 6]), csb("c_mv", [TC, NB, 2])
            c_var, c_rstd = csb("c_var", [TC, NB]), csb("c_rstd", [TC, NB])
            xn, xnT = csb("xn", [P, NB, P]), csb("xnT", [P, NB, P])
            c = csb("c", [TC, NB, P])
            cnT = csb("cnT", [P, NB, TC])
            ctxT = csb("ctxT", [P, NB, TC])
            first = csb("first", [P, 3, GS, P])
            last = csb("last", [P, 3, GS, P])
            mk_u8 = pctx.enter_context(nc.sbuf_tensor("mk_u8", [NB, TC], U8))
            mk_i32 = pctx.enter_context(nc.sbuf_tensor("mk_i32", [NB, TC], I32))
            mk_f = csb("mk_f", [NB, TC])
            mk_0 = pctx.enter_context(nc.sbuf_tensor("mk_0", [NB, TC], BF16))
            mk_1 = pctx.enter_context(nc.sbuf_tensor("mk_1", [NB, 3, TC], BF16))
            groups = range(NB // GS)

            def normalise_all(dve, src, st, mv_, rstd_, out, s_counted, s_centred, s_rstd, s_normed, loaded):
                for g in groups:
                    if loaded is not None:
                        dve.wait_ge(loaded[g], 16)
                    wait(dve, s_centred, GS * g)
                    for j in range(GS):
                        nc.vector.bn_stats(st[:, j, :], src[:, GS * g + j, :]).then_inc(s_counted, 1)
                    dve.wait_ge(s_counted, GS * (g + 1))
                    for j in range(GS):
                        nc.vector.bn_aggr(mv_[:, GS * g + j, :], st[:, j, :]).then_inc(s_centred, 1)
                    if g:
                        apply_norm(dve, src, mv_, rstd_, out, s_rstd, s_normed, g - 1)
                apply_norm(dve, src, mv_, rstd_, out, s_rstd, s_normed, groups[-1])

            def apply_norm(dve, src, mv_, rstd_, out, s_rstd, s_normed, g):
                dve.wait_ge(s_rstd, 2 * (g + 1))
                for b in range(GS * g, GS * (g + 1)):
                    nc.vector.tensor_scalar(out[:, b, :], src[:, b, :], mv_[:, b, 0:1], rstd_[:, b:b + 1],
                                            ALU.subtract, ALU.mult).then_inc(s_normed, 1)

            def rstd_all(pool, rows, mv_, var_, rstd_, s_centred, s_rstd):
                for g in groups:
                    of = slice(GS * g, GS * (g + 1))
                    pool.wait_ge(s_centred, GS * (g + 1))
                    nc.gpsimd.tensor_scalar(var_[:, of], mv_[:, of, 1:2].rearrange("p b a -> p (b a)"), EPS, None, ALU.add).then_inc(s_rstd, 1)
                    pool.wait_ge(s_rstd, 2 * g + 1)
                    nc.gpsimd.tensor_tensor(rstd_[:, of], var_[:, of], m["half_power"][0:rows, 0:GS], ALU.pow).then_inc(s_rstd, 1)

            with ExitStack() as pc:
                p_x, p_zT, p_qT, p_e0T, p_z, p_q = (ps(f"p_{n}", pc) for n in ("x", "zT", "qT", "e0T", "z", "q"))
                with nc.Block() as block:
                    @block.sync
                    def _(sp):
                        def load(dst, src, s):
                            sp.dma_start(dst, src).then_inc(s, 16)
                        ls = m["loaded_scan"]
                        NS = 4
                        load(x[:, 0:GS, :], t["x"][0:GS].rearrange("b p d -> p b d"), loaded_x[0])
                        load(m["sq"][:, 0:NS, :], t["squares"][0:NS].rearrange("n p d -> p n d"), loaded_squares)
                        for g in groups[1:]:
                            load(x[:, GS * g:GS * (g + 1), :], t["x"][GS * g:GS * (g + 1)].rearrange("b p d -> p b d"), loaded_x[g])
                        lc = m["loaded_context"]
                        load(c[:, :, :], t["ctx"].rearrange("b p d -> p b d"), lc)
                        load(ctxT[:, :, :], t["ctxT"], lc)
                        load(m["sq"][:, NS:, :], t["squares"][NS:].rearrange("n p d -> p n d"), lc)
                        load(m["cols"][:, :], t["cols"], lc)
                        load(m["x1_bv"][:, :], t["rows"][ROWS.index("x1_v"):ROWS.index("x1_v") + 1, :].to_broadcast([P, P]), lc)
                        load(w1T[:, :], t["scan_w1T"], ls)
                        load(w2T[0:HID, :], t["scan_w2T"], ls)
                        load(w2T[HID:HID + 1, :], t["rows"][ROWS.index("s_b2"):ROWS.index("s_b2") + 1, :], ls)
                        load(w2[:, :], t["scan_w2"], ls)
                        load(b1c[:, :], t["scan_b1"].rearrange("(p a) -> p a", a=1), ls)
                        load(b1r[:, :], t["scan_b1"].rearrange("(a p) -> a p", a=1), ls)
                        lm = m["loaded_mask"]
                        load(mk_u8[:, :], t["mask_0"], lm)
                        load(mk_i32[:, :], t["mask_1"], lm)
                        lr = m["loaded_rest"]
                        rest = [(m[f"bo_{n}"][:, :], t["rows"][ROWS.index(n + "_o"):ROWS.index(n + "_o") + 1, :].to_broadcast([P, P]))
                                for n in ("x0", "s1")]
                        rest += [(m["keep_v"][:, :], t["keep_v"]), (m["keep_vr"][:, :], t["keep_vr"]), (m["headsel"][:, :, :], t["head_select"]),
                                (m["alibi"][:, :, :], t["alibi"]),
                                (m["countdown"][:, :], t["countdown"])]
                        for j in range(len(HALVES)):
                            for r in range(2):
                                rest.append((m["half"][:, j, :, :].rearrange("p (k r) d -> p k r d", r=2)[:, :, r, :],
                                             t["halves"][j].rearrange("p (k d) -> p k d", d=DH)))
                        for q in range(2):
                            rest += [(m[f"b1_{q}"][:, :, :], t[f"b1_{q}"].rearrange("e (k p) -> p e k", p=P)),
                                     (m[f"b2_{q}"][:, :], t[f"b2_{q}"]),
                                     (m[f"wr_{q}"][:, :], t[f"wr_{q}"])]
                        rest.append((m["br_0"][:, :], t["br_0"].rearrange("(a n) -> a n", a=1).to_broadcast([P, NE])))
                        for dst, src in rest:
                            with nc.allow_non_contiguous_dma(reason="one-time weight load"):
                                load(dst, src, lr)
                        m["n_rest"] = len(rest)

                    @block.gpsimd
                    def _(pool):
                        nc.gpsimd.memset(m["half_power"][:, :], -0.5).then_inc(set_pool, 1)
                        pool.wait_ge(set_pool, 1)
                        rstd_all(pool, P, mv, var, rstd, centred, rstd_ready)
                        for n, (tile, value) in enumerate(((ones[:, :], 1.0), (m["ones_bf"][:, :], 1.0))):
                            nc.gpsimd.memset(tile, value).then_inc(set_pool, 1)
                            pool.wait_ge(set_pool, n + 2)
                        nc.gpsimd.memset(last[:, :, :, :], 0.0).then_inc(last_zero, 1)
                        rstd_all(pool, TC, c_mv, c_var, c_rstd, c_centred, c_rstd_ready)
                        mask_rows(nc, pool, m, masks, mk_u8, mk_i32, mk_f, mk_0, mk_1)

                    @block.vector
                    def _(dve):
                        normalise_all(dve, x, stats, mv, rstd, xn, counted, centred, rstd_ready, normed, loaded_x)
                        dve.wait_ge(loaded_squares, 16)
                        nc.vector.tensor_tensor(tkv[:, :], m["w"]("tk"), m["w"]("tv"), ALU.subtract).then_inc(set_dve, 1)
                        nc.vector.tensor_copy(m["ident_bf"][:, :], eye).then_inc(set_dve, 1)
                        for g in groups:
                            dve.wait_ge(q_ready, g + 1)
                            nc.vector.tensor_tensor(flat(x, g), p_q[:, :], flat(x, g), ALU.add).then_inc(q_added, 1)
                            if g == 0:
                                dve.wait_ge(m["loaded_context"], 16 * CONTEXT_LOADS)
                                normalise_all(dve, c, c_stats, c_mv, c_rstd, c, c_counted, c_centred, c_rstd_ready, c_normed, None)

                    @block.scalar
                    def _(act):
                        def copy(s, done, to, bank):
                            act.wait_ge(s, g + 1)
                            nc.scalar.activation(to, bank, ACT.Copy).then_inc(done, 1)
                        for g in groups:
                            copy(turned, xnT_sb, flat(xnT, g), p_x[:, :])
                            copy(zT_ready, zT_sb, flat(zT, g), p_zT[:, :])
                            copy(qT_ready, qT_sb, flat(qT, g), p_qT[:, :])
                            copy(e0T_ready, e0T_sb, flat(e0T, g), p_e0T[:, :])
                            copy(z_ready, z_sb, flat(z, g), p_z[:, :])

                    @block.tensor
                    def _(pe):
                        mm = nc.tensor.matmul
                        pe.wait_ge(loaded_squares, 16)

                        def turn(g):
                            wait(pe, xnT_sb, g)
                            pe.wait_ge(normed, GS * (g + 1))
                            for j in range(GS):
                                last = nc.tensor.transpose(p_x[:, P * j:P * (j + 1)], xn[:, GS * g + j, :], eye)
                            last.then_inc(turned, 1)
                        turn(0)
                        for g in groups:
                            if g + 1 < len(groups):
                                turn(g + 1)
                            else:
                                pe.wait_ge(xnT_sb, g + 1)
                            wait(pe, zT_sb, g)
                            mm(p_zT[:, :], m["w"]("tk"), flat(xnT, g), start=True, stop=True).then_inc(zT_ready, 1)
                            wait(pe, qT_sb, g)
                            mm(p_qT[:, :], m["w"]("tq"), flat(xnT, g), start=True, stop=True).then_inc(qT_ready, 1)
                            wait(pe, e0T_sb, g)
                            if g == 0:
                                pe.wait_ge(set_dve, 2)
                            mm(p_e0T[:, :], tkv[:, :], flat(xnT, g), start=True, stop=True).then_inc(e0T_ready, 1)
                            pe.wait_ge(zT_sb, g + 1)
                            wait(pe, z_sb, g)
                            for j in range(GS):
                                last = nc.tensor.transpose(p_z[:, P * j:P * (j + 1)], zT[:, GS * g + j, :], eye)
                            last.then_inc(z_ready, 1)
                            pe.wait_ge(qT_sb, g + 1)
                            wait(pe, q_added, g)
                            for j in range(GS):
                                last = nc.tensor.transpose(p_q[:, P * j:P * (j + 1)], qT[:, GS * g + j, :], eye)
                            last.then_inc(q_ready, 1)

            with ExitStack() as pc:
                p_c = ps("p_c", pc)
                p_k = [ps(f"p_k{q}", pc) for q in range(2)]
                p_v = [ps(f"p_v{q}", pc) for q in range(2)]
                p_r = [ps(f"p_r{q}", pc) for q in range(2)]
                GC = GS * TC

                def slot(g, q):
                    return q * (1 + g % 2)

                def order_first(copy, q, src, g, *how):
                    copy(first[:, slot(g, q), :, :].rearrange("p b (r k) -> p b r k", k=KM),
                         src[:, GS * g:GS * (g + 1), 0:KM].unsqueeze(2).to_broadcast([P, GS, P // KM, KM]), *how).then_inc(first_ordered[q], 1)

                def order_last(copy, q, src, g, *how):
                    copy(last[:, slot(g, q), :, :].rearrange("p b (r k) -> p b r k", k=KR)[:, :, :, 0:KL],
                         src[:, GS * g:GS * (g + 1), KM:TC].unsqueeze(2).to_broadcast([P, GS, P // KR, KL]), *how).then_inc(last_ordered[q], 1)
                with nc.Block() as block:
                    @block.gpsimd
                    def _(pool):
                        pool.wait_ge(m["loaded_context"], 16 * CONTEXT_LOADS)
                        for g in groups:
                            wait(pool, v1_ready, g - 1)
                            order_first(nc.gpsimd.tensor_copy, 1, ctxT, g)

                    @block.sync
                    def _(sp):
                        sp.wait_ge(masks, MASK_STEPS)
                        sp.dma_start(m["mask_0"][0:1, :, :].rearrange("a b k -> a (b k)"), mk_0[:, :]).then_inc(m["masks_placed"], 16)
                        for r in range(3):
                            sp.dma_start(m["mask_1"][r:r + 1, :, :].rearrange("a b k -> a (b k)"), mk_1[:, r, :]).then_inc(m["masks_placed"], 16)

                    @block.tensor
                    def _(pe):
                        mm = nc.tensor.matmul
                        pe.wait_ge(m["loaded_context"], 16 * CONTEXT_LOADS)

                        def turn(g):
                            wait(pe, cT_sb, g)
                            pe.wait_ge(c_normed, GS * (g + 1))
                            for j in range(GS):
                                last = nc.tensor.transpose(p_c[:, TC * j:TC * (j + 1)], c[:, GS * g + j, :], m["eye"][0:TC, 0:TC])
                            last.then_inc(c_turned, 1)

                        def values(g, q):
                            pe.wait_ge(first_ordered[q], g + 1)
                            pe.wait_ge(last_ordered[q], g + 1)
                            for j in range(GS):
                                of = slice(P * j, P * (j + 1))
                                mm(p_v[q][:, of], first[:, slot(g, q), j, :], m["w"](f"x{q}_v"), start=True, stop=True)
                                ins = mm(p_r[q][:, of], last[:, slot(g, q), j, :], m["w"](f"x{q}_v"), start=True, stop=True)
                            return ins
                        turn(0)
                        for g in groups:
                            wait(pe, k_sb, 2 * g)
                            mm(p_k[1][:, 0:GC], m["w"]("x1_k"), flat(ctxT, g), start=True, stop=True).then_inc(k_ready, 1)
                            wait(pe, v1_sb, 2 * g)
                            values(g, 1).then_inc(v1_ready, 1)
                            pe.wait_ge(cT_sb, g + 1)
                            mm(p_k[0][:, 0:GC], m["w"]("x0_k"), flat(cnT, g), start=True, stop=True).then_inc(k_ready, 1)
                            if g + 1 < len(groups):
                                turn(g + 1)
                            wait(pe, v0_sb, 2 * g)
                            values(g, 0).then_inc(v0_ready, 1)

                    @block.scalar
                    def _(act):
                        ck = m["ctx_k"]

                        def copy_cT(g):
                            act.wait_ge(c_turned, g + 1)
                            nc.scalar.activation(flat(cnT, g), p_c[:, 0:GC], ACT.Identity,
                                                 bias=m["col"]("x0_b2"), scale=m["col"]("x0_g2")).then_inc(cT_sb, 1)

                        act.wait_ge(last_zero, 1)

                        def order_c(g):
                            act.wait_ge(cT_sb, g + 1)
                            wait(act, v0_ready, g)
                            order_first(nc.scalar.activation, 0, cnT, g, ACT.Copy)
                            order_last(nc.scalar.activation, 0, cnT, g, ACT.Copy)
                        copy_cT(0)
                        order_c(0)
                        for g in groups:
                            act.wait_ge(k_ready, 2 * g + 1)
                            nc.scalar.activation(flat(ck[:, 1, :, :], g), p_k[1][:, 0:GC], ACT.Identity, bias=m["col"]("x1_bk")).then_inc(k_sb, 1)
                            if g + 1 < len(groups):
                                copy_cT(g + 1)
                            act.wait_ge(k_ready, 2 * g + 2)
                            nc.scalar.activation(flat(ck[:, 0, :, :], g), p_k[0][:, 0:GC], ACT.Copy).then_inc(k_sb, 1)
                            if g + 1 < len(groups):
                                order_c(g + 1)

                    @block.vector
                    def _(dve):
                        dve.wait_ge(m["loaded_context"], 16 * CONTEXT_LOADS)
                        dve.wait_ge(last_zero, 1)
                        order_last(nc.vector.tensor_copy, 1, ctxT, 0)
                        for g in groups:
                            if g + 1 < len(groups):
                                wait(dve, v1_ready, g)
                                order_last(nc.vector.tensor_copy, 1, ctxT, g + 1)
                            dve.wait_ge(v1_ready, g + 1)
                            for to, bank in ((m["ctx_v"], p_v[1]), (m["ctx_vr"], p_r[1])):
                                nc.vector.tensor_tensor(to[:, 1, GS * g:GS * (g + 1), :], bank[:, :].rearrange("k (b d) -> k b d", d=P),
                                                        m["x1_bv"][:, :].unsqueeze(1).to_broadcast([P, GS, P]), ALU.add).then_inc(v1_sb, 1)
                            dve.wait_ge(v0_ready, g + 1)
                            for to, bank in ((m["ctx_v"], p_v[0]), (m["ctx_vr"], p_r[0])):
                                nc.vector.tensor_copy(flat(to[:, 0, :, :], g), bank[:, :]).then_inc(v0_sb, 1)

        scan(nc, m, dict(z=z, zT=zT, qT=qT, e0T=e0T), sems)
        nc.clear_and_free_semaphores(sems)
        nc.all_engine_barrier()


def scan(nc, m, pre, sems):
    x, eye, ones = m["x"], m["eye"], m["ones"]
    ctx = ExitStack()
    with ctx:
        def sb(name, shape, dt=F32):
            return ctx.enter_context(nc.sbuf_tensor(f"s_{name}", shape, dt))

        def sem(name):
            sems.append(nc.alloc_semaphore(name=f"t_{name}"))
            return sems[-1]

        w1T, w2T, w2, b1c, b1r = (m[k] for k in ("scan_w1T", "scan_w2T", "scan_w2", "scan_b1c", "scan_b1r"))
        zf, zTf = sb("zf", [P, 2, P]), sb("zTf", [P, 2, P])
        hT = sb("hT", [HID + 1, P])
        hqT = sb("hqT", [HID + 1, P])
        h = sb("h", [P, HID + 1])
        a = sb("a", [P, HID])
        a2 = sb("a2", [P, HID])
        th = sb("th", [P, HID])
        zero, safe, den = (sb(n, [P, HID]) for n in ("zero", "safe", "den"))
        num = sb("num", [P, 2, HID])
        slope = sb("slope", [P, HID])
        eT = sb("eT", [P, P])
        e = sb("e", [P, P])
        da = sb("da", [P, HID])
        p_aT, p_aqT, p_a, p_eT, p_e, p_g1, p_g2, p_out = (
            ctx.enter_context(nc.psum_tensor(f"p_{n}", [P, 512], F32)) for n in ("aT", "aqT", "a", "eT", "e", "g1", "g2", "out"))
        p_dh = p_a[:, 128:128 + HID]
        g_w1T = p_g1[:, 0:HID]
        g_b1c, g_b1r = p_aqT[0:HID, 200:201], p_aqT[0:1, 256:256 + HID]
        g_w2T, g_w2 = p_g2[0:HID + 1, 0:P], p_g2[:, 256:256 + HID]
        set_up, z_copied, zT_copied = sem("set_up"), sem("z_copied"), sem("zT_copied")
        a_ready, acts_ready, aq_ready = sem("a"), sem("acts"), sem("aq")
        hT_ready, hqT_ready, h_ready, a_sb, sq_ready, th_ready = (
            sem(n) for n in ("hT", "hqT", "h", "a_sb", "sq", "th"))
        num_done = sem("num_done")
        slope_dve, eT_ready, eT_sb, e_ready, e_sb = (sem(n) for n in ("slope", "eT", "eT_sb", "e", "e_sb"))
        dh_ready, da_ready, g1_ready, g2_ready = (sem(n) for n in ("dh", "da", "g1", "g2"))
        g1b_ready, g2b_ready, b1_new, w2T_new = sem("g1b"), sem("g2b"), sem("b1_new"), sem("w2T_new")
        w1_new, w2_new, out_ready, added = sem("w1_new"), sem("w2_new"), sem("out"), sem("added")

        def at(tile, b):
            return tile[:, bass.ds(b, 1), :].rearrange("p a d -> p (a d)")

        def steps(eng, main, tail):
            main(0, 0, False)
            with eng.Fori(0, (NB - 2) // 2) as i:
                for u in (1, 0):
                    main(i * 2 + (2 - u), u, True)
            main(NB - 1, 1, True)
            tail()

        with nc.Block() as block:
            @block.gpsimd
            def _(pool):
                for n, (tile, value) in enumerate(((hT[HID:HID + 1, :], 1.0), (hqT[HID:HID + 1, :], 1.0), (h[:, HID:HID + 1], 1.0))):
                    nc.gpsimd.memset(tile, value).then_inc(set_up, 1)
                    pool.wait_ge(set_up, n + 1)

                def copy_z(b, p):
                    if not (isinstance(b, int) and b < 2):
                        pool.wait_ge(g1_ready, b - 1)
                    pass_waits(pool, m)
                    nc.gpsimd.tensor_copy(zTf[:, p, :], at(pre["zT"], b)).then_inc(zT_copied, 1)
                    pool.wait_ge(zT_copied, b + 1)
                    pass_waits(pool, m)
                    nc.gpsimd.tensor_copy(zf[:, p, :], at(pre["z"], b)).then_inc(z_copied, 1)
                    pool.wait_ge(z_copied, b + 1)
                copy_z(0, 0)
                copy_z(1, 1)
                with pool.Fori(0, (NB - 2) // 2) as i:
                    for u in range(2):
                        copy_z(i * 2 + (u + 2), u)

            @block.vector
            def _(dve):
                def main(b, p, has_out):
                    n = 6 * b
                    dve.wait_ge(a_sb, b + 1)
                    nc.vector.tensor_scalar(zero[:, :], a[:, :], 0.0, 1e-30, ALU.is_equal, ALU.mult).then_inc(slope_dve, 1)
                    dve.wait_ge(slope_dve, n + 1)
                    nc.vector.tensor_tensor(safe[:, :], a[:, :], zero[:, :], ALU.add).then_inc(slope_dve, 1)
                    if has_out:
                        new_w2(b - 1)
                    dve.wait_ge(th_ready, b + 1)
                    dve.wait_ge(slope_dve, n + 2)
                    nc.vector.scalar_tensor_tensor(den[:, :], th[:, :], 1.0, safe[:, :], ALU.add, ALU.mult).then_inc(slope_dve, 1)
                    nc.vector.scalar_tensor_tensor(num[:, 1, :], th[:, :], -1.0, a2[:, :], ALU.add, ALU.mult).then_inc(num_done, 1)
                    dve.wait_ge(h_ready, b + 1)
                    nc.vector.scalar_tensor_tensor(num[:, 0, :], th[:, :], 1.0, h[:, 0:HID], ALU.add, ALU.mult).then_inc(num_done, 1)
                    dve.wait_ge(eT_ready, b + 1)
                    wait(dve, e_ready, b)
                    nc.vector.tensor_tensor(eT[:, :], p_eT[:, 0:P], at(pre["e0T"], b), ALU.add).then_inc(eT_sb, 1)
                    dve.wait_ge(slope_dve, n + 3)
                    nc.vector.reciprocal(den[:, :], den[:, :]).then_inc(slope_dve, 1)
                    dve.wait_ge(num_done, 2 * b + 2)
                    nc.vector.scalar_tensor_tensor(num[:, 0, :], num[:, 1, :], -4.0 * DENSITY, num[:, 0, :], ALU.mult, ALU.add).then_inc(slope_dve, 1)
                    dve.wait_ge(slope_dve, n + 5)
                    nc.vector.tensor_tensor(slope[:, :], num[:, 0, :], den[:, :], ALU.mult).then_inc(slope_dve, 1)
                    dve.wait_ge(slope_dve, n + 6)
                    dve.wait_ge(dh_ready, b + 1)
                    wait(dve, g1b_ready, b)
                    nc.vector.tensor_tensor(da[:, :], p_dh, slope[:, :], ALU.mult).then_inc(da_ready, 1)
                    if has_out:
                        add_out(b - 1)
                    dve.wait_ge(g1_ready, b + 1)
                    nc.vector.scalar_tensor_tensor(w1T[:, :], g_w1T, -GRAD, w1T[:, :], ALU.mult, ALU.add).then_inc(w1_new, 1)
                    dve.wait_ge(g1b_ready, b + 1)
                    for w_, g_ in ((b1r[:, :], g_b1r), (b1c[:, :], g_b1c)):
                        nc.vector.scalar_tensor_tensor(w_, g_, -GRAD, w_, ALU.mult, ALU.add).then_inc(b1_new, 1)
                    dve.wait_ge(g2_ready, b + 1)
                    nc.vector.scalar_tensor_tensor(w2T[:, :], g_w2T, -GRAD, w2T[:, :], ALU.mult, ALU.add).then_inc(w2T_new, 1)

                def new_w2(b):
                    dve.wait_ge(g2b_ready, b + 1)
                    nc.vector.scalar_tensor_tensor(w2[:, :], g_w2, -GRAD, w2[:, :], ALU.mult, ALU.add).then_inc(w2_new, 1)

                def add_out(b):
                    dve.wait_ge(out_ready, b + 1)
                    nc.vector.tensor_tensor(at(x, b), p_out[:, 0:P], at(x, b), ALU.add).then_inc(added, 1)

                steps(dve, main, lambda: add_out(NB - 1))

            @block.scalar
            def _(act):
                act.wait_ge(set_up, 3)
                act.wait_ge(m["loaded_scan"], 16 * SCAN_LOADS)

                def main(b, p, has_out):
                    act.wait_ge(acts_ready, b + 1)
                    wait(act, eT_ready, b)
                    if has_out:
                        act.wait_ge(b1_new, 2 * b)
                    nc.scalar.activation(hT[0:HID, :], p_aT[0:HID, 0:P], ACT.Gelu, bias=b1c[:, 0:1]).then_inc(hT_ready, 1)
                    act.wait_ge(a_ready, b + 1)
                    wait(act, da_ready, b)
                    nc.scalar.activation(a[:, :], p_a[:, 0:HID], ACT.Copy).then_inc(a_sb, 1)
                    nc.scalar.activation(a2[:, :], p_a[:, 0:HID], ACT.Square, scale=0.5).then_inc(sq_ready, 1)
                    act.wait_ge(sq_ready, b + 1)
                    nc.scalar.activation(th[:, :], a2[:, :], ACT.Tanh).then_inc(th_ready, 1)
                    wait(act, g2b_ready, b)
                    act.wait_ge(slope_dve, 6 * b + 2)
                    nc.scalar.activation(h[:, 0:HID], safe[:, :], ACT.Gelu).then_inc(h_ready, 1)
                    if has_out:
                        apply_act(b - 1)
                    act.wait_ge(e_ready, b + 1)
                    nc.scalar.activation(e[:, :], p_e[:, 0:P], ACT.Copy).then_inc(e_sb, 1)

                def apply_act(b):
                    act.wait_ge(aq_ready, b + 1)
                    wait(act, out_ready, b)
                    nc.scalar.activation(hqT[0:HID, :], p_aqT[0:HID, 0:P], ACT.Gelu, bias=b1c[:, 0:1]).then_inc(hqT_ready, 1)

                def tail():
                    act.wait_ge(b1_new, 2 * NB)
                    apply_act(NB - 1)
                steps(act, main, tail)

            @block.tensor
            def _(pe):
                mm = nc.tensor.matmul
                pe.wait_ge(set_up, 3)
                pe.wait_ge(m["loaded_scan"], 16 * SCAN_LOADS)

                def main(b, p, has_out):
                    if has_out:
                        pe.wait_ge(w1_new, b)
                    mm(p_aT[0:HID, 0:P], w1T[:, :], at(pre["zT"], b), start=True, stop=True).then_inc(acts_ready, 1)
                    pe.wait_ge(zT_copied, b + 1)
                    wait(pe, da_ready, b)
                    mm(p_a[:, 0:HID], zTf[:, p, :], w1T[:, :], start=True, stop=False)
                    if has_out:
                        pe.wait_ge(b1_new, 2 * b)
                    mm(p_a[:, 0:HID], ones[0:1, :], b1r[:, :], start=False, stop=True).then_inc(a_ready, 1)
                    if has_out:
                        grad_w2(b - 1)
                    pe.wait_ge(hT_ready, b + 1)
                    if has_out:
                        pe.wait_ge(w2T_new, b)
                    wait(pe, eT_sb, b)
                    mm(p_eT[:, 0:P], w2T[:, :], hT[:, :], start=True, stop=True).then_inc(eT_ready, 1)
                    if has_out:
                        hidden_q(b - 1)
                    pe.wait_ge(eT_sb, b + 1)
                    pe.wait_ge(sq_ready, b + 1)
                    if has_out:
                        pe.wait_ge(w2_new, b)
                    mm(p_dh, eT[:, :], w2[:, :], start=True, stop=True).then_inc(dh_ready, 1)
                    wait(pe, e_sb, b)
                    nc.tensor.transpose(p_e[:, 0:P], eT[:, :], eye).then_inc(e_ready, 1)
                    if has_out:
                        output(b - 1)
                    pe.wait_ge(da_ready, b + 1)
                    pe.wait_ge(z_copied, b + 1)
                    mm(g_w1T, zf[:, p, :], da[:, :], start=True, stop=True).then_inc(g1_ready, 1)
                    mm(g_b1c, da[:, :], ones[:, 0:1], start=True, stop=True)
                    mm(g_b1r, ones[:, 0:1], da[:, :], start=True, stop=True).then_inc(g1b_ready, 1)
                    pe.wait_ge(e_sb, b + 1)
                    pe.wait_ge(h_ready, b + 1)
                    mm(g_w2T, h[:, :], e[:, :], start=True, stop=True).then_inc(g2_ready, 1)

                def grad_w2(b):
                    wait(pe, w2T_new, b + 1)
                    mm(g_w2, e[:, :], h[:, 0:HID], start=True, stop=True).then_inc(g2b_ready, 1)

                def hidden_q(b):
                    wait(pe, hqT_ready, b)
                    mm(p_aqT[0:HID, 0:P], w1T[:, :], at(pre["qT"], b), start=True, stop=True).then_inc(aq_ready, 1)

                def output(b):
                    wait(pe, added, b)
                    pe.wait_ge(hqT_ready, b + 1)
                    mm(p_out[:, 0:P], hqT[:, :], w2T[:, :], start=True, stop=True).then_inc(out_ready, 1)

                def tail():
                    pe.wait_ge(w1_new, NB)
                    pe.wait_ge(b1_new, 2 * NB)
                    hidden_q(NB - 1)
                    pe.wait_ge(w2T_new, NB)
                    output(NB - 1)
                steps(pe, main, tail)


def attention(nc, m, name, T, mask, mask_rows, exp_scale, sel, experts_of=None, q=None):
    x = m["x"]
    eye, ones_bf = m["eye"], m["ones_bf"]
    own = name == "s1"
    L = 1 if own else 0
    GW = HG * T
    ctx = ExitStack()
    with ctx:
        def sb(n, shape, dt=F32):
            return ctx.enter_context(nc.sbuf_tensor(f"{name}_{n}", shape, dt))

        def sem(n):
            return ctx.enter_context(nc.semaphore(f"{name}_{n}"))

        stats = sb("stats", [P, 2, 6])
        mv = sb("mv", [P, 2, 2])
        var = sb("var", [P, 2, 1])
        rstd = sb("rstd", [P, 2, 1])
        xn = sb("xn", [P, 2, P])
        xT = sb("xT", [P, P])
        qT = sb("qT", [P, 2, NG, P])
        kT = sb("kT", [P, 2, HG, T])
        top = sb("top", [P, NH])
        prob = sb("prob", [P, 2, NH * T if own else (NH // 2 + NH // 8) * P])
        chunks = NH if own else NH // 2 + NH // 8
        sets = [range(c, min(c + 4, chunks)) for c in range(0, chunks, 4)]
        NS = len(sets)
        pT = sb("pT", [P, chunks, P])
        total = sb("total", [P, 2, NH])
        SUMS = 2 if own else 3
        inv = sb("inv", [P, NH])
        inv_wide = sb("inv_wide", [P, NH, DH])
        invT = sb("invT", [P, P])
        oT = sb("oT", [P, P])
        parts = [(0, T, 0, T)] if own else [(0, KM, 0, KM), (NH * KM, KR, KM, TC)]

        def prob_of(p, part):
            at_, width, k0, k1 = part
            return prob[:, p, at_:at_ + NH * width].rearrange("p (h k) -> p h k", k=width)[:, :, 0:k1 - k0]

        v = sb("v", [P, 2, chunks, P])
        if mask:
            m_fix = sb("m_fix", [3, 2, TC], BF16)

        p_s = ctx.enter_context(nc.psum_tensor(f"{name}_p_s", [P, NG, 512], F32))
        p_pT = ctx.enter_context(nc.psum_tensor(f"{name}_p_pT", [P, 2, 512], F32))
        p_in = ctx.enter_context(nc.psum_tensor(f"{name}_p_in", [P, 512], F32))
        p_o = ctx.enter_context(nc.psum_tensor(f"{name}_p_o", [P, 512], F32))
        scores = p_s[:, :, 0:GW].rearrange("p g (h k) -> p g h k", k=T)
        pi_x, pi_inv = p_in[:, 0:P], p_in[:, 3 * P:4 * P]
        pi_q, pi_k, pi_v = p_in[:, 0:P], p_in[:, P:2 * P], p_in[0:T, 2 * P:3 * P]
        po_mix, po_out = p_o[:, 0:P], p_o[:, P:2 * P]

        set_up = sem("set_up")
        biased = sem("biased")
        counted, in_pool, normed = sem("counted"), sem("in_pool"), sem("normed")
        mask_fixed, turned, turned_sb, projected = sem("mask_fixed"), sem("turned"), sem("turned_sb"), sem("projected")
        inv_turned, inv_sb = sem("inv_turned"), sem("inv_sb")
        q_sb, k_sb, v_sb = sem("q_sb"), sem("k_sb"), sem("v_sb")
        scored, top_done, shifted, exped = sem("scored"), sem("top_done"), sem("shifted"), sem("exped")
        totalled, summed = sem("totalled"), sem("summed")
        p_turned, pT_sb, mixed = sem("p_turned"), sem("pT_sb"), sem("mixed")
        o_done, projected_o, res_done = sem("o_done"), sem("projected_o"), sem("res_done")

        if name == "x1":
            q_bias = sb("q_bias", [P, NG])
            bias_ready = sem("bias_ready")
        if own:
            v_flat = sb("v_flat", [T, 2, P])
            v_flat_sb = sem("v_flat_sb")
        if experts_of:
            w_raw = sb("w_raw", [P, 2, FF])
            w_loaded = [sem(f"w_loaded_{u}") for u in range(2)]
            w_hi_ready, w_lo_ready = sem("w_hi_ready"), sem("w_lo_ready")

        def at(tile, b):
            return tile[:, bass.ds(b, 1), :].rearrange("p a d -> p (a d)")

        def blocks(p, first, n, rows_of):
            flat = v[:, p, first:first + n, :].rearrange("k c (g d) -> k (c g) d", d=rows_of)
            return flat[:, 0:n * P // rows_of:P // rows_of + 1, :]

        with nc.Block() as block:
            @block.sync
            def _(sp):
                if experts_of:
                    for b in range(2 * NE):
                        e, p = b // 2, b % 2
                        wait(sp, w_lo_ready, b - 1)
                        if p == 0:
                            sp.dma_start(w_raw[:, p, :], experts_of[f"w1_{q}"][e]).then_inc(w_loaded[p], 16)
                        else:
                            sp.dma_start(w_raw[:, p, :].rearrange("p (k d) -> p k d", d=P),
                                         experts_of[f"w2_{q}"][e].rearrange("(k p) d -> p k d", p=P)).then_inc(w_loaded[p], 16)

            @block.gpsimd
            def _(pool):
                def rstd_of(b, p):
                    pool.wait_ge(counted, (b + 1) * 2)
                    pass_waits(pool, m)
                    nc.gpsimd.tensor_scalar(var[:, p, :], mv[:, p, 1:2], EPS, None, ALU.add).then_inc(in_pool, 1)
                    pool.wait_ge(in_pool, b * 2 + 1)
                    nc.gpsimd.tensor_tensor(rstd[:, p, :], var[:, p, :], m["half_power"][:, 0:1], ALU.pow).then_inc(in_pool, 1)

                def copy_mask(b, p):
                    if mask:
                        wait(pool, scored, b - 1)
                        pass_waits(pool, m)
                        nc.gpsimd.tensor_copy(m_fix[0:mask_rows, p, :], at(m[mask], b)[0:mask_rows, :]).then_inc(mask_fixed, 1)

                def copy_v(b, p):
                    if own:
                        pool.wait_ge(v_flat_sb, b + 1)
                        wait(pool, mixed, b - 1)
                        pass_waits(pool, m)
                        nc.gpsimd.tensor_copy(blocks(p, 0, NH, DH), v_flat[:, p, :].rearrange("k (h d) -> k h d", d=DH)).then_inc(v_sb, 1)
                        return
                    wait(pool, mixed, b - 1)
                    for src, keep, first, n, width in ((m[f"v_{name}"], m["keep_v"], 0, NH // 2, 2 * DH),
                                                       (m[f"vr_{name}"], m["keep_vr"], NH // 2, NH // 8, 8 * DH)):
                        pass_waits(pool, m)
                        nc.gpsimd.tensor_tensor(blocks(p, first, n, width), at(src, b).rearrange("k (c f) -> k c f", f=width),
                                                keep[:, :].unsqueeze(1).to_broadcast([P, n, width]), ALU.mult).then_inc(v_sb, 1)

                pool.wait_ge(m["loaded_rest"], 16 * m["n_rest"])
                pool.wait_ge(m["masks_placed"], 16 * MASK_ROWS)

                def weights_lo(b, p):
                    if experts_of:
                        pool.wait_ge(w_hi_ready, b + 1)
                        pass_waits(pool, m)
                        nc.gpsimd.tensor_tensor(at(m["w_lo"], b), w_raw[:, p, :], at(m["w_hi"], b), ALU.subtract).then_inc(w_lo_ready, 1)

                def masked_k(b, p):
                    if not own:
                        wait(pool, scored, b - 1)
                        pass_waits(pool, m)
                        nc.gpsimd.tensor_tensor(kT[:, p, :, :], at(m[f"kT_{name}"], b).unsqueeze(1).to_broadcast([P, HG, T]),
                                                m["headsel"][:, sel, :].unsqueeze(2).to_broadcast([P, HG, T]), ALU.mult).then_inc(k_sb, 1)

                def set_zero(b, p):
                    if isinstance(b, int) and b == 0:
                        nc.gpsimd.memset(v[:, :, :, :], 0.0).then_inc(set_up, 1)
                        pool.wait_ge(set_up, 1)
                        if not own:
                            nc.gpsimd.memset(prob[:, :, NH * KM:], 0.0).then_inc(set_up, 1)
                            pool.wait_ge(set_up, 2)

                def add_bias(b, p):
                    if name != "x1":
                        pool.wait_ge(normed, b + 1)
                        pass_waits(pool, m)
                        nc.gpsimd.tensor_tensor(at(x, b), at(x, b), m[f"bo_{name}"][:, :], ALU.add).then_inc(biased, 1)

                staggered(pool, [(-1, rstd_of), (0, add_bias), (0, copy_mask), (0, masked_k), (0, set_zero),
                                 (L + 1, copy_v), (0, weights_lo)])

            @block.vector
            def _(dve):
                def count(b, p):
                    s = Steps(dve, counted, b, 2)
                    s.done(nc.vector.bn_stats(stats[:, p, :], at(x, b)))
                    pass_waits(dve, m)
                    s.done(nc.vector.bn_aggr(mv[:, p, :], stats[:, p, :]))
                    s.end()

                def normalise(b, p):
                    dve.wait_ge(in_pool, b * 2 + 2)
                    wait(dve, turned, b - 1)
                    nc.vector.tensor_scalar(xn[:, p, :], at(x, b), mv[:, p, 0:1], rstd[:, p, 0:1],
                                            ALU.subtract, ALU.mult).then_inc(normed, 1)

                def masked_k(b, p):
                    dve.wait_ge(projected, b + 1)
                    wait(dve, scored, b - 1)
                    nc.vector.tensor_tensor(kT[:, p, :, :], pi_k[:, 0:T].unsqueeze(1).to_broadcast([P, HG, T]),
                                            m["headsel"][:, sel, :].unsqueeze(2).to_broadcast([P, HG, T]), ALU.mult).then_inc(k_sb, 1)

                def copy_q(b, p):
                    dve.wait_ge(projected, b + 1)
                    wait(dve, scored, b - 1)
                    to = qT[:, p, :, :]
                    src = pi_q.unsqueeze(1).to_broadcast([P, NG, P])
                    groups = m["headsel"][:, 2, :].unsqueeze(2).to_broadcast([P, NG, P])
                    nc.vector.tensor_tensor(to, src, groups, ALU.mult).then_inc(q_sb, NG)

                def copy_v(b, p):
                    if own:
                        dve.wait_ge(projected, b + 1)
                        wait(dve, v_sb, b - 1)
                        nc.vector.tensor_copy(v_flat[:, p, :], pi_v).then_inc(v_flat_sb, 1)

                def find_top(b, p):
                    dve.wait_ge(scored, b + 1)
                    nc.vector.tensor_reduce(top[:, :].rearrange("p (g h) -> p g h", h=HG), scores, AX.X, ALU.max).then_inc(top_done, 1)

                def shift(b, p):
                    dve.wait_ge(top_done, b + 1)
                    wait(dve, p_turned, NS * (b - 1))
                    if not own and isinstance(b, int) and b == 0:
                        dve.wait_ge(set_up, 2)
                    for part in parts:
                        k0, k1 = part[2:]
                        ins = nc.vector.tensor_tensor(prob_of(p, part).rearrange("p (g h) k -> p g h k", h=HG), scores[:, :, :, k0:k1],
                                                      top[:, :].rearrange("p (g h) -> p g h", h=HG).unsqueeze(3).to_broadcast([P, NG, HG, k1 - k0]),
                                                      ALU.subtract)
                        ins.then_inc(shifted, 1)

                def sum_up(b, p):
                    dve.wait_ge(exped, len(parts) * (b + 1))
                    nc.vector.tensor_reduce(total[:, 0, :], prob_of(p, parts[0]), AX.X, ALU.add).then_inc(totalled, 1)
                    if not own:
                        nc.vector.tensor_reduce(total[:, 1, :], prob_of(p, parts[1]), AX.X, ALU.add).then_inc(totalled, 1)

                def invert(b, p):
                    dve.wait_ge(totalled, len(parts) * (b + 1))
                    s = Steps(dve, summed, b, SUMS)
                    if not own:
                        s.done(nc.vector.tensor_tensor(total[:, 0, :], total[:, 0, :], total[:, 1, :], ALU.add))
                    s.done(nc.vector.reciprocal(inv[:, :], total[:, 0, :]))
                    wait(dve, inv_turned, b)
                    s.done(nc.vector.tensor_copy(inv_wide[:, :, :], inv[:, :].unsqueeze(2).to_broadcast([P, NH, DH])))
                    s.end()

                def scale_out(b, p):
                    dve.wait_ge(mixed, b + 1)
                    dve.wait_ge(inv_sb, b + 1)
                    wait(dve, projected_o, b)
                    nc.vector.tensor_tensor(oT[:, :], po_mix, invT[:, :], ALU.mult).then_inc(o_done, 1)

                def residual(b, p):
                    xb = at(x, b)
                    dve.wait_ge(projected_o, b + 1)
                    if name != "x1":
                        dve.wait_ge(biased, b + 1)
                    nc.vector.tensor_tensor(xb, po_out, xb, ALU.add).then_inc(res_done, 1)

                if name == "x1":
                    nc.vector.tensor_scalar(q_bias[:, :], m["headsel"][:, 2, :], m["col"]("x1_bq"), None, ALU.mult).then_inc(bias_ready, 1)
                if own:
                    staggered(dve, [(4, scale_out), (-1, count), (1, masked_k), (1, copy_q), (1, copy_v), (3, sum_up),
                                    (4, residual), (3, invert), (2, find_top), (2, shift), (-1, normalise)])
                else:
                    staggered(dve, [(3, scale_out), (-1, count), (2, sum_up), (3, residual), (2, invert), (1, find_top),
                                    (1, shift), (-1, normalise)])

            @block.scalar
            def _(act):
                def turn_in(b, p):
                    act.wait_ge(turned, b + 1)
                    wait(act, inv_turned, b - 1 - L)
                    wait(act, projected, b)
                    if name == "x0":
                        nc.scalar.activation(xT[:, :], pi_x, ACT.Identity, bias=m["col"]("x0_b1"), scale=m["col"]("x0_g1")).then_inc(turned_sb, 1)
                    else:
                        nc.scalar.activation(xT[:, :], pi_x, ACT.Copy).then_inc(turned_sb, 1)

                def turn_inv(b, p):
                    act.wait_ge(inv_turned, b + 1)
                    wait(act, o_done, b)
                    nc.scalar.activation(invT[:, :], pi_inv, ACT.Copy).then_inc(inv_sb, 1)

                def copy_q(b, p):
                    act.wait_ge(projected, b + 1)
                    wait(act, scored, b - 1)
                    if name == "x1" and isinstance(b, int) and b == 0:
                        act.wait_ge(bias_ready, 1)
                    for g in range(NG):
                        group = m["headsel"][:, 2, g:g + 1]
                        if name == "x1":
                            nc.scalar.activation(qT[:, p, g, :], pi_q, ACT.Identity, bias=q_bias[:, g:g + 1], scale=group).then_inc(q_sb, 1)
                        else:
                            nc.scalar.activation(qT[:, p, g, :], pi_q, ACT.Copy, scale=group).then_inc(q_sb, 1)

                def weights_hi(b, p):
                    if experts_of:
                        act.wait_ge(w_loaded[p], (b - p) * 8 + 16)
                        nc.scalar.activation(at(m["w_hi"], b), w_raw[:, p, :], ACT.Copy).then_inc(w_hi_ready, 1)

                def exps(b, p):
                    for n, part in enumerate(parts):
                        act.wait_ge(shifted, len(parts) * b + n + 1)
                        nc.scalar.activation(prob_of(p, part), prob_of(p, part), ACT.Exp, scale=exp_scale).then_inc(exped, 1)

                def copy_pT(groups):
                    def run(b, p):
                        for g in groups:
                            act.wait_ge(p_turned, NS * b + g + 1)
                            wait(act, mixed, b)
                            of = slice(sets[g][0], sets[g][-1] + 1)
                            nc.scalar.activation(pT[:, of, :].rearrange("k c q -> k (c q)"), p_pT[:, g % 2, 0:P * len(sets[g])],
                                                 ACT.Copy).then_inc(pT_sb, 1)
                    return run

                if own:
                    staggered(act, [(3, copy_pT((0, 1))), (3, copy_pT((2,))), (0, turn_in), (3, turn_inv), (3, copy_pT((3,))), (2, exps)])
                else:
                    staggered(act, [(2, copy_pT((0, 1))), (0, weights_hi), (0, turn_in), (2, turn_inv), (2, copy_pT((2,))),
                                    (0, copy_q), (1, exps)])

            @block.tensor
            def _(pe):
                mm = nc.tensor.matmul

                def bank_read(n):
                    if isinstance(n, int):
                        n = min(n, NB)
                    wait(pe, q_sb, NG * n)
                    if own:
                        wait(pe, k_sb, n)
                        wait(pe, v_flat_sb, n)

                def turn_in(b, p):
                    pe.wait_ge(normed, b + 1)
                    bank_read(b)
                    nc.tensor.transpose(pi_x, xn[:, p, :], eye).then_inc(turned, 1)

                def turn_inv(b, p):
                    pe.wait_ge(summed, SUMS * (b + 1))
                    bank_read(b + 2 + L)
                    nc.tensor.transpose(pi_inv, inv_wide[:, :, :].rearrange("p h d -> p (h d)"), eye).then_inc(inv_turned, 1)

                def project(b, p):
                    pe.wait_ge(turned_sb, b + 1)
                    wait(pe, inv_sb, b - 1 - L)
                    last = mm(pi_q, m["w"](name + "_q"), xT[:, :], start=True, stop=True)
                    if own:
                        wk, wv = (m["half"][:, j, :, :].rearrange("p h d -> p (h d)") for j in range(2))
                        mm(pi_k[:, 0:T], wk, xT[:, :], start=True, stop=True)
                        last = mm(pi_v, xT[:, :], wv, start=True, stop=True)
                    last.then_inc(projected, 1)

                def score(groups):
                    def run(b, p):
                        if groups[0] == 0:
                            pe.wait_ge(q_sb, NG * (b + 1))
                            pe.wait_ge(k_sb, b + 1)
                            wait(pe, shifted, len(parts) * b)
                            if mask:
                                pe.wait_ge(mask_fixed, b + 1)
                        for g in groups:
                            to = p_s[:, g, 0:GW]
                            if mask:
                                r = slice(0, mask_rows)
                                mm(to.rearrange("p (h k) -> p h k", k=T), ones_bf[r, :],
                                   m_fix[r, p, :].unsqueeze(1).to_broadcast([mask_rows, HG, T]), start=True, stop=False)
                            else:
                                mm(to, m["ident_bf"][:, :], m["alibi"][:, HG * g:HG * (g + 1), :].rearrange("p h k -> p (h k)"),
                                   start=True, stop=False)
                            last = mm(to, qT[:, p, g, :], kT[:, p, :, :].rearrange("p h k -> p (h k)"), start=False, stop=True)
                        if groups[-1] == NG - 1:
                            last.then_inc(scored, 1)
                    return run

                def turn_p(groups):
                    def run(b, p):
                        pe.wait_ge(exped, len(parts) * (b + 1))
                        for g in groups:
                            wait(pe, pT_sb, NS * b + max(g - 1, 0))
                            for c in sets[g]:
                                last = nc.tensor.transpose(p_pT[:, g % 2, P * (c % 4):P * (c % 4 + 1)], prob[:, p, P * c:P * (c + 1)], eye)
                            last.then_inc(p_turned, 1)
                    return run

                def mix(g):
                    def run(b, p):
                        if g == 0:
                            wait(pe, res_done, b)
                            pe.wait_ge(v_sb, (1 if own else 2) * (b + 1))
                        pe.wait_ge(pT_sb, NS * b + g + 1)
                        for c in sets[g]:
                            last = mm(po_mix, v[:, p, c, :], pT[:, c, :], start=c == 0, stop=c == chunks - 1)
                        if g == NS - 1:
                            last.then_inc(mixed, 1)
                    return run

                def project_o(b, p):
                    pe.wait_ge(o_done, b + 1)
                    if name == "x1":
                        mm(po_out, oT[:, :], eye, start=True, stop=True).then_inc(projected_o, 1)
                    else:
                        mm(po_out, oT[:, :], m["w"](name + "_o"), start=True, stop=True).then_inc(projected_o, 1)

                if own:
                    staggered(pe, [(2, score((0, 1))), (3, turn_p((0, 1))), (4, project_o), (2, score((2, 3))), (3, mix(0)),
                                   (3, turn_p((2,))), (0, turn_in), (3, turn_inv), (3, mix(1)), (3, turn_p((3,))),
                                   (0, project), (3, mix(2)), (3, mix(3))])
                else:
                    staggered(pe, [(1, score((0, 1))), (2, turn_p((0, 1))), (3, project_o), (1, score((2, 3))), (0, turn_in),
                                   (2, turn_inv), (2, mix(0)), (2, turn_p((2,))), (0, project), (2, mix(1)), (2, mix(2))])


MASK_STEPS = 8
MASK_ROWS = 1 + 3


def mask_rows(nc, pool, m, masks, u8, i32, f, first, second):
    g = nc.gpsimd
    s = Steps(pool, masks, 0, MASK_STEPS)
    pool.wait_ge(m["loaded_mask"], 32)
    s.done(g.tensor_scalar(f[:, :], u8[:, :], -1.0, 3e38, ALU.add, ALU.mult))
    s.done(g.tensor_scalar(first[:, :], f[:, :], 3e38, None, ALU.mult))
    s.done(g.tensor_scalar(f[:, :], i32[:, :], -1.0, 10000.0, ALU.add, ALU.mult))
    for r in range(3):
        s.done(g.tensor_copy(second[:, r, :], f[:, :]))
        if r < 2:
            s.done(g.tensor_tensor(f[:, :], f[:, :], second[:, r, :], ALU.subtract))
    s.end()


def experts(nc, m, q, out):
    x, eye = m["x"], m["eye"]
    GT = 4
    groups = range(NB // GT)
    b1, b2, wr = (m[f"{k}_{q}"] for k in ("b1", "b2", "wr"))
    w_hi, w_lo = m["w_hi"], m["w_lo"]
    ctx = ExitStack()
    with ctx:
        def sb(n, shape, dt=F32):
            return ctx.enter_context(nc.sbuf_tensor(f"f{q}_{n}", shape, dt))

        def sem(n):
            return ctx.enter_context(nc.semaphore(f"f{q}_{n}"))

        def ps(n, shape, c):
            return c.enter_context(nc.psum_tensor(f"f{q}_{n}", shape, F32))

        def at(tile, b):
            return tile[:, bass.ds(b, 1), :].rearrange("p a d -> p (a d)")

        def flat(tile, g):
            return tile[:, GT * g:GT * (g + 1), :].rearrange("p b d -> p (b d)")

        stats = sb("stats", [P, GT, 6])
        mv = sb("mv", [P, NB, 2])
        var = sb("var", [P, NB])
        rstd = sb("rstd", [P, NB])
        xT_hi, xT_lo = sb("xT_hi", [P, NB, P], F32R), sb("xT_lo", [P, NB, P], F32R)
        lg = sb("lg", [P, NB, NE])
        best = sb("best", [P, 2, NB])
        where = sb("where", [P, 2, NB])
        gap = sb("gap", [P, NB])
        egap = sb("egap", [P, NB])
        den = sb("den", [P, NB])
        inv = sb("inv", [P, NB])
        one_hot = sb("one_hot", [P, 2, NB, NE])
        wts = sb("wts", [P, NB, NE])

        counted, centred, rstd_ready, normed = sem("counted"), sem("centred"), sem("rstd"), sem("normed")
        turned, xT_sb, hi_ready, lo_ready, routed, gap_ready = (
            sem(n) for n in ("turned", "xT_sb", "hi", "lo", "routed", "gap_ready"))
        logits_ready = sem("logits")
        router_dve, router_act = sem("router_dve"), sem("router_act")
        yT_ready, yT_sb = sem("yT_ready"), sem("yT_sb")
        h_ready, h_sb, h_hi_ready, h_lo_ready, y_ready, combined = (
            sem(n) for n in ("h_ready", "h_sb", "h_hi", "h_lo", "y_ready", "combined"))

        with ExitStack() as pctx:
            xn = pctx.enter_context(nc.sbuf_tensor(f"f{q}_xn", [P, 2, GT, P], F32))
            xT = pctx.enter_context(nc.sbuf_tensor(f"f{q}_xT", [P, 2, GT, P], F32))
            p_t = ps("p_t", [P, 2, 512], pctx)
            p_l = ps("p_l", [P, 512], pctx)
            with nc.Block() as block:
                @block.gpsimd
                def _(pool):
                    for g in groups:
                        of = slice(GT * g, GT * (g + 1))
                        pool.wait_ge(centred, GT * (g + 1))
                        nc.gpsimd.tensor_scalar(var[:, of], mv[:, of, 1:2].rearrange("p b a -> p (b a)"), EPS, None, ALU.add).then_inc(rstd_ready, 1)
                        pool.wait_ge(rstd_ready, 2 * g + 1)
                        nc.gpsimd.tensor_tensor(rstd[:, of], var[:, of], m["half_power"][:, 0:GT], ALU.pow).then_inc(rstd_ready, 1)

                @block.vector
                def _(dve):
                    def normalise(g):
                        dve.wait_ge(rstd_ready, 2 * (g + 1))
                        wait(dve, turned, g - 1)
                        for j in range(GT):
                            b = GT * g + j
                            nc.vector.tensor_scalar(xn[:, g % 2, j, :], x[:, b, :], mv[:, b, 0:1], rstd[:, b:b + 1],
                                                    ALU.subtract, ALU.mult).then_inc(normed, 1)

                    def low(g):
                        dve.wait_ge(xT_sb, g + 1)
                        dve.wait_ge(hi_ready, g + 1)
                        nc.vector.tensor_tensor(flat(xT_lo, g), xT[:, g % 2, :, :].rearrange("p b d -> p (b d)"),
                                                flat(xT_hi, g), ALU.subtract).then_inc(lo_ready, 1)

                    for g in groups:
                        wait(dve, centred, GT * g)
                        for j in range(GT):
                            nc.vector.bn_stats(stats[:, j, :], x[:, GT * g + j, :]).then_inc(counted, 1)
                        dve.wait_ge(counted, GT * (g + 1))
                        for j in range(GT):
                            nc.vector.bn_aggr(mv[:, GT * g + j, :], stats[:, j, :]).then_inc(centred, 1)
                        if g:
                            normalise(g - 1)
                        if g > 1:
                            low(g - 2)
                    normalise(groups[-1])
                    low(groups[-2])
                    low(groups[-1])
                    dve.wait_ge(routed, NB // GT)
                    logits = p_l[:, 0:NB * NE].rearrange("p (b e) -> p b e", e=NE)
                    if q == 0:
                        nc.vector.tensor_tensor(lg[:, :, :], logits, m["br_0"][:, :].unsqueeze(1).to_broadcast([P, NB, NE]), ALU.add).then_inc(logits_ready, 1)
                    else:
                        nc.vector.tensor_copy(lg[:, :, :], logits).then_inc(logits_ready, 1)
                    dve.wait_ge(logits_ready, 1)

                @block.scalar
                def _(act):
                    for g in groups:
                        act.wait_ge(turned, g + 1)
                        wait(act, routed, g - 1)
                        wait(act, lo_ready, g - 1)
                        nc.scalar.activation(xT[:, g % 2, :, :].rearrange("p b d -> p (b d)"), p_t[:, g % 2, :], ACT.Copy).then_inc(xT_sb, 1)
                        nc.scalar.activation(flat(xT_hi, g), p_t[:, g % 2, :], ACT.Copy).then_inc(hi_ready, 1)

                @block.tensor
                def _(pe):
                    mm = nc.tensor.matmul

                    def turn(g):
                        pe.wait_ge(normed, GT * (g + 1))
                        wait(pe, hi_ready, g - 1)
                        for j in range(GT):
                            last = nc.tensor.transpose(p_t[:, g % 2, P * j:P * (j + 1)], xn[:, g % 2, j, :], eye)
                        last.then_inc(turned, 1)
                    turn(0)
                    for g in groups:
                        if g + 1 < len(groups):
                            turn(g + 1)
                        pe.wait_ge(xT_sb, g + 1)
                        for j in range(GT):
                            b = GT * g + j
                            to = p_l[:, NE * b:NE * (b + 1)]
                            last = mm(to, xT[:, g % 2, j, :], wr[:, :], start=True, stop=True)
                        last.then_inc(routed, 1)

        with ExitStack() as pctx:
            h = pctx.enter_context(nc.sbuf_tensor(f"f{q}_h", [P, 2, GT * P], F32))
            h_hi = pctx.enter_context(nc.sbuf_tensor(f"f{q}_h_hi", [P, 2, FC, GT * P], F32R))
            h_lo = pctx.enter_context(nc.sbuf_tensor(f"f{q}_h_lo", [P, 2, FC, GT * P], F32R))
            yT = m["ctx_v"][:, 0, 0:2 * GT, :].rearrange("p (u b) d -> p u (b d)", u=2)
            p_h = ps("p_h", [P, FC, 512], pctx)
            p_yT = ps("p_yT", [P, 2, 512], pctx)
            p_y = ps("p_y", [P, 2, 512], pctx)
            with nc.Block() as block:
                def over_groups(eng, run):
                    run(0)
                    with eng.Fori(1, NB // GT) as g:
                        run(g)

                def lagging(g, e, lag, stage):
                    if e >= lag:
                        stage(g, e - lag)
                    elif not isinstance(g, int):
                        stage(g - 1, e - lag + NE)

                @block.tensor
                def _(pe):
                    mm = nc.tensor.matmul

                    def up(g, e):
                        n = g * NE + e
                        x_hi, x_lo = (t[:, bass.ds(g * GT, GT), :].rearrange("p b t -> p (b t)") for t in (xT_hi, xT_lo))
                        for k in range(FC):
                            of = slice(P * k, P * (k + 1))
                            wait(pe, h_hi_ready, FC * (n - 1) + k + 1)
                            mm(p_h[:, k, :], w_hi[:, 2 * e, of], x_hi, start=True, stop=False)
                            mm(p_h[:, k, :], w_hi[:, 2 * e, of], x_lo, start=False, stop=False)
                            mm(p_h[:, k, :], w_lo[:, 2 * e, of], x_hi, start=False, stop=True).then_inc(h_ready, 1)

                    def down(g, e):
                        n = g * NE + e
                        wait(pe, yT_sb, n - 1)
                        pe.wait_ge(h_hi_ready, FC * n + FC)
                        pe.wait_ge(h_lo_ready, FC * n + FC)
                        to = p_yT[:, e % 2, :]
                        for k in range(FC):
                            of = slice(P * k, P * (k + 1))
                            mm(to, w_hi[:, 2 * e + 1, of], h_hi[:, e % 2, k, :], start=k == 0, stop=False)
                            mm(to, w_hi[:, 2 * e + 1, of], h_lo[:, e % 2, k, :], start=False, stop=False)
                            last = mm(to, w_lo[:, 2 * e + 1, of], h_hi[:, e % 2, k, :], start=False, stop=k == FC - 1)
                        last.then_inc(yT_ready, 1)

                    def turn_back(g, e):
                        n = g * NE + e
                        pe.wait_ge(yT_sb, n + 1)
                        wait(pe, combined, GT * (n - 1))
                        for j in range(GT):
                            of = slice(P * j, P * (j + 1))
                            last = nc.tensor.transpose(p_y[:, e % 2, of], yT[:, e % 2, of], eye)
                        last.then_inc(y_ready, 1)

                    def run(g):
                        for e in range(NE):
                            up(g, e)
                            lagging(g, e, 1, down)
                            lagging(g, e, 2, turn_back)
                    over_groups(pe, run)
                    down(NB // GT - 1, NE - 1)
                    turn_back(NB // GT - 1, NE - 2)
                    turn_back(NB // GT - 1, NE - 1)

                @block.scalar
                def _(act):
                    def run(g):
                        for e in range(NE):
                            n = g * NE + e
                            for k in range(FC):
                                act.wait_ge(h_ready, FC * n + k + 1)
                                wait(act, h_lo_ready, FC * n + k - 1)
                                nc.scalar.activation(h[:, k % 2, :], p_h[:, k, :], ACT.Relu, bias=b1[:, e, k:k + 1]).then_inc(h_sb, 1)
                                if k == 0:
                                    wait(act, yT_ready, n - 1)
                                nc.scalar.activation(h_hi[:, e % 2, k, :], p_h[:, k, :], ACT.Relu,
                                                     bias=b1[:, e, k:k + 1]).then_inc(h_hi_ready, 1)
                                if isinstance(g, int) and (e, k) == (1, 2):
                                    act.wait_ge(gap_ready, 1)
                                    nc.scalar.activation(egap[:, :], gap[:, :], ACT.Exp).then_inc(router_act, 1)
                    over_groups(act, run)

                @block.vector
                def _(dve):
                    def low(g, e):
                        n = g * NE + e
                        wait(dve, yT_ready, n - 1)
                        for k in range(FC):
                            dve.wait_ge(h_sb, FC * n + k + 1)
                            dve.wait_ge(h_hi_ready, FC * n + k + 1)
                            nc.vector.tensor_tensor(h_lo[:, e % 2, k, :], h[:, k % 2, :], h_hi[:, e % 2, k, :], ALU.subtract).then_inc(h_lo_ready, 1)
                            if isinstance(g, int):
                                route(e, k)

                    s = Steps(dve, router_dve, 0, 16)

                    countdown = m["countdown"][:, :].unsqueeze(1).to_broadcast([P, NB, NE])

                    def wide(t):
                        return t.unsqueeze(2).to_broadcast([P, NB, NE])

                    def best_logit(j):
                        s.done(nc.vector.tensor_reduce(best[:, j, :], lg[:, :, :], AX.X, ALU.max))
                        s.done(nc.vector.tensor_tensor(one_hot[:, j, :, :], lg[:, :, :], wide(best[:, j, :]), ALU.is_equal))

                    def first_of_equal(j):
                        s.done(nc.vector.tensor_tensor(one_hot[:, j, :, :], one_hot[:, j, :, :], countdown, ALU.mult))
                        s.done(nc.vector.tensor_reduce(where[:, j, :], one_hot[:, j, :, :], AX.X, ALU.max))

                    def choose(j):
                        s.done(nc.vector.tensor_tensor(one_hot[:, j, :, :], countdown, wide(where[:, j, :]), ALU.is_equal))
                        if j == 0:
                            s.done(nc.vector.scalar_tensor_tensor(lg[:, :, :], one_hot[:, 0, :, :], -3e38, lg[:, :, :], ALU.mult, ALU.add))
                        else:
                            nc.vector.tensor_tensor(gap[:, :], best[:, 1, :], best[:, 0, :], ALU.subtract).then_inc(gap_ready, 1)

                    def weigh():
                        dve.wait_ge(router_act, 1)
                        s.done(nc.vector.tensor_scalar(den[:, :], egap[:, :], 1.0, None, ALU.add))
                        s.done(nc.vector.reciprocal(inv[:, :], den[:, :]))
                        s.done(nc.vector.tensor_tensor(one_hot[:, 1, :, :], one_hot[:, 1, :, :], wide(egap[:, :]), ALU.mult))

                    def combine_weights():
                        s.done(nc.vector.tensor_tensor(one_hot[:, 0, :, :], one_hot[:, 0, :, :], one_hot[:, 1, :, :], ALU.add))
                        s.done(nc.vector.tensor_tensor(wts[:, :, :], one_hot[:, 0, :, :], wide(inv[:, :]), ALU.mult))
                        s.end()

                    def route(e, k):
                        if e == 0:
                            (best_logit, first_of_equal, choose, best_logit)[k](k // 3)
                        elif (e, k) == (1, 0):
                            first_of_equal(1)
                        elif (e, k) == (1, 1):
                            choose(1)
                        elif (e, k) == (1, 3):
                            weigh()
                        elif (e, k) == (2, 0):
                            combine_weights()

                    def copy_yT(g, e):
                        n = g * NE + e
                        dve.wait_ge(yT_ready, n + 1)
                        wait(dve, y_ready, n - 1)
                        nc.vector.tensor_scalar(yT[:, e % 2, :], p_yT[:, e % 2, :], b2[:, e:e + 1], None, ALU.add).then_inc(yT_sb, 1)

                    def combine(g, e):
                        n = g * NE + e
                        dve.wait_ge(y_ready, n + 1)
                        wait(dve, combined, GT * n)
                        for j in range(GT):
                            xb = at(x, g * GT + j)
                            nc.vector.scalar_tensor_tensor(xb, p_y[:, e % 2, P * j:P * j + P],
                                                           wts[:, bass.ds(g * GT + j, 1), e:e + 1].rearrange("p a b -> p (a b)"),
                                                           xb, ALU.mult, ALU.add).then_inc(combined, 1)

                    def run(g):
                        for e in range(NE):
                            low(g, e)
                            lagging(g, e, 2, combine)
                            lagging(g, e, 1, copy_yT)
                    over_groups(dve, run)
                    combine(NB // GT - 1, NE - 2)
                    copy_yT(NB // GT - 1, NE - 1)
                    combine(NB // GT - 1, NE - 1)

                @block.sync
                def _(sp):
                    if out is not None:
                        for g in range(NB // GT):
                            sp.wait_ge(combined, GT * NE * (g + 1))
                            sp.dma_start(out[GT * g:GT * (g + 1)].rearrange("b p d -> p b d"),
                                         x[:, GT * g:GT * (g + 1), :]).then_inc(m["stored"], 16)
                        sp.wait_ge(m["stored"], 16 * (NB // GT))


def kernel(**inputs):
    import numpy as np
    import concourse.bacc as bacc
    from concourse import mybir as mb
    from concourse.bass_utils import run_bass_kernel_spmd
    import ml_dtypes

    a = {k: np.asarray(v) for k, v in inputs.items()}
    T = lambda w: np.ascontiguousarray(np.swapaxes(w, -1, -2))
    squares = {"ident": np.eye(P, dtype=np.float32),
               "tk": T(a["L0_attn_t_k"]), "tv": T(a["L0_attn_t_v"]), "tq": T(a["L0_attn_t_q"]),
               "x0_q": T(a["L0_xattn_Wq"]), "x0_k": T(a["L0_xattn_Wk"]), "x0_v": T(a["L0_xattn_Wv"]),
               "x0_o": T(a["L0_xattn_Wo"]), "s1_q": T(a["L1_attn_Wq"]), "s1_o": T(a["L1_attn_Wo"]),
               "x1_q": T(a["L1_xattn_Wq"]), "x1_k": T(a["L1_xattn_Wk"]), "x1_v": T(a["L1_xattn_Wv"])}
    head = np.arange(P) // DH
    select = (head[:, None] % HG == np.arange(HG)[None, :]).astype(np.float32)
    group = (head[:, None] // HG == np.arange(NG)[None, :]).astype(np.float32)
    row = np.arange(P)[:, None]
    slopes = 2.0 ** -(np.arange(NH) + 1.0)
    dist = np.abs(np.arange(P)[:, None] - np.arange(P)[None, :])
    t = {
        "x": a["x"], "ctx": a["ctx_1024"],
        "ctxT": np.ascontiguousarray(a["ctx_1024"].transpose(2, 0, 1)),
        "squares": np.stack([squares[k] for k in SQUARES]),
        "halves": np.stack([T(a["L1_attn_Wk"]), T(a["L1_attn_Wv"])]),
        "cols": np.stack([a[k] for k in ("L0_xattn_g1", "L0_xattn_b1", "L0_xattn_g2", "L0_xattn_b2",
                                         "L1_xattn_bq", "L1_xattn_bk")], axis=1),
        "rows": np.stack([a[k] for k in ("L0_xattn_bo", "L1_attn_bo", "L1_xattn_bv", "L0_attn_b2")]),
        "scan_w1T": T(a["L0_attn_W1"]), "scan_w2T": T(a["L0_attn_W2"]), "scan_w2": a["L0_attn_W2"],
        "scan_b1": a["L0_attn_b1"],
        "mask_0": a["mask_BxS2_bf1"].view(np.uint8), "mask_1": a["mask_BxS2_ik0"],
        "head_select": np.stack([select, select / np.float32(SQRT_DH), group], axis=1).astype(np.float32),
        "alibi": (-dist[:, None, :] * slopes[None, :, None]).astype(ml_dtypes.bfloat16),
        "keep_v": (row // KM == np.arange(2 * DH)[None, :] // DH).astype(np.float32),
        "keep_vr": (row // KR == np.arange(8 * DH)[None, :] // DH).astype(np.float32),
        "countdown": np.tile(np.arange(NE, 0, -1, dtype=np.float32), (P, 1)),
        "w1_0": a["L0_ffn_W1"], "w2_0": a["L0_ffn_W2"], "b1_0": a["L0_ffn_b1"], "b2_0": T(a["L0_ffn_b2"]),
        "wr_0": a["L0_ffn_W_router"], "br_0": a["L0_ffn_b_router"],
        "w1_1": T(a["L1_ffn_w1"]), "w2_1": T(a["L1_ffn_w2"]), "b1_1": a["L1_ffn_b1"], "b2_1": T(a["L1_ffn_b2"]),
        "wr_1": T(a["L1_ffn_gate_w"]),
    }
    nc = bacc.Bacc("TRN2", target_bir_lowering=False, num_devices=1)
    arrays, aps = {}, {}
    for name, v in t.items():
        v = np.ascontiguousarray(v)
        arrays[f"in_{name}"] = v
        aps[name] = nc.dram_tensor(f"in_{name}", v.shape, mb.dt.from_np(v.dtype), kind="ExternalInput").ap()
    out = nc.dram_tensor("out", (NB, P, P), F32, kind="ExternalOutput").ap()
    build(nc, aps, out)
    r = run_bass_kernel_spmd(nc, [arrays], core_ids=[0])
    return r.results[0]["out"]
```
